# Optimizing a Trainium2 kernel written in Bass

```python
import numpy as np
import jax
import jax.numpy as jnp

def _softmax(x, axis=-1):
    return jax.nn.softmax(x, axis=axis)

def _gelu(x):
    return jax.nn.gelu(x, approximate=True)

def _silu(x):
    return jax.nn.silu(x)

def _sigmoid(x):
    return jax.nn.sigmoid(x)

def _layernorm(x, axis=-1, eps=1e-05):
    m = jnp.mean(x, axis=axis, keepdims=True)
    v = jnp.var(x, axis=axis, keepdims=True)
    return (x - m) / jnp.sqrt(v + eps)

def _scatter_add(tgt, idx, src, axis=0):
    return tgt.at[idx].add(src)

def _segment_sum(src, seg, n):
    return jax.ops.segment_sum(src, seg, n)
kernel_name = 'mk_decoder_preln_d1_seqx_r8_9d40ed'

def setup_inputs(seed: int=0):
    np.random.seed(seed)
    _w = jnp.asarray

    def _rec_inputs():
        import jax
        import jax.numpy as jnp
        _rk = jax.random.key(seed)
        x = 7.22e-05 + 1 * jax.random.normal(jax.random.fold_in(_rk, 1), (4, 512, 128), jnp.float32)
        _lenS = 512 - jax.random.randint(jax.random.fold_in(_rk, 7), (4,), 0, max(1, 512 // 4) + 1, jnp.int32)
        _lenS2 = 77 - jax.random.randint(jax.random.fold_in(_rk, 8), (4,), 0, max(1, 77 // 4) + 1, jnp.int32)
        _ctx_1024P = jax.random.normal(jax.random.fold_in(_rk, 11), (4, 16, 128), jnp.float32)
        _ctx_1024c = jax.random.dirichlet(jax.random.fold_in(_rk, 511), 0.3 * jnp.ones((16,), jnp.float32), (4, 77))
        _ctx_1024t = jnp.einsum('bsk,bkd->bsd', _ctx_1024c, _ctx_1024P)
        _ctx_1024t = _ctx_1024t * jax.lax.rsqrt(jnp.mean(jnp.square(_ctx_1024t)) + 1e-12) * 0.953939
        ctx_1024 = 4.13588e-05 + 0.999923 * (_ctx_1024t + 0.3 * jax.random.normal(jax.random.fold_in(_rk, 611), (4, 77, 128), jnp.float32))
        return (x, ctx_1024)
    x, ctx_1024 = _rec_inputs()

    def _L0_attn_setup():
        import jax, jax.numpy as jnp
        import numpy as np
        H, DK, DV = (8, 64, 128)
        DECAY, THR, SBETA = (0.9, 0.5, 10.0)
        EPS = 1e-06

        def _rms(h, w):
            return h * jax.lax.rsqrt(jnp.mean(h * h, axis=-1, keepdims=True) + EPS) * w

        def _forward(x, w_norm_in, conv_w, conv_b, wq, wk, wv, w_out, w_spike, w_au, b_au, w_ad, b_ad, alpha_spike, w_beta, b_beta, beta_spike, w_hn, w_u1, b_u1, w_u2, b_u2, w_ffn, w_ff1, w_ff3, w_ff2):
            B, T, D = x.shape
            h = _rms(x, w_norm_in)
            CK = conv_w.shape[-1]
            hp = jnp.pad(h, ((0, 0), (CK - 1, 0), (0, 0)))
            conv = conv_b + sum((hp[:, j:j + T, :] * conv_w[:, j] for j in range(CK)))
            h = jax.nn.silu(conv)
            q = (h @ wq).reshape(B, T, H, DK)
            k = (h @ wk).reshape(B, T, H, DK)
            v = (h @ wv).reshape(B, T, H, DV)
            q = q / (jnp.linalg.norm(q, axis=-1, keepdims=True) + EPS)
            k = k / (jnp.linalg.norm(k, axis=-1, keepdims=True) + EPS)
            sd = (h @ w_spike).reshape(B, T, H, DK)
            ab = (jax.nn.silu(h @ w_au + b_au) @ w_ad + b_ad).reshape(B, T, H, DK)
            bb = h @ w_beta + b_beta

            def step(carry, inp):
                s, mem = carry
                qt, kt, vt, sdt, abt, bbt = inp
                mem = DECAY * mem + sdt
                sur = jax.nn.sigmoid(SBETA * (mem - THR))
                hard = (mem > THR).astype(x.dtype)
                spike = sur + jax.lax.stop_gradient(hard - sur)
                mem = mem - spike * THR
                alpha = jax.nn.sigmoid(abt + alpha_spike * spike)
                beta = jax.nn.sigmoid(bbt[..., None] + jnp.sum(spike * beta_spike, axis=-1, keepdims=True))
                active = jax.lax.stop_gradient((jnp.sum(hard, axis=-1, keepdims=True) > 0).astype(x.dtype))
                alpha = jnp.where(active > 0, alpha, jnp.ones_like(alpha))
                beta = beta * active
                s = s * alpha[..., None]
                u = jnp.einsum('bhd,bhdv->bhv', kt, s)
                s = s - beta[..., None] * jnp.einsum('bhd,bhv->bhdv', kt, u)
                s = s + beta[..., None] * jnp.einsum('bhd,bhv->bhdv', kt, vt)
                out = jnp.einsum('bhdv,bhd->bhv', s, qt)
                return ((s, mem), out)
            s0 = jnp.zeros((B, H, DK, DV), x.dtype)
            m0 = jnp.zeros((B, H, DK), x.dtype)
            tmaj = lambda a: jnp.moveaxis(a, 1, 0)
            (s, mem), outs = jax.lax.scan(step, (s0, m0), (tmaj(q), tmaj(k), tmaj(v), tmaj(sd), tmaj(ab), tmaj(bb)))
            y = jnp.moveaxis(outs, 0, 1)
            y = y * jax.lax.rsqrt(jnp.mean(y * y, axis=-1, keepdims=True) + EPS) * w_hn
            y = y.reshape(B, T, H * DV)
            gate = jax.nn.sigmoid(jax.nn.silu(x @ w_u1 + b_u1) @ w_u2 + b_u2)
            y = x + y @ w_out * gate
            h2 = _rms(y, w_ffn)
            y = y + jax.nn.silu(h2 @ w_ff1) * (h2 @ w_ff3) @ w_ff2
            return (y, s, mem)

        def _reference_tuple_inner(x, w_norm_in, conv_w, conv_b, wq, wk, wv, w_out, w_spike, w_au, b_au, w_ad, b_ad, alpha_spike, w_beta, b_beta, beta_spike, w_hn, w_u1, b_u1, w_u2, b_u2, w_ffn, w_ff1, w_ff3, w_ff2):
            return _forward(x, w_norm_in, conv_w, conv_b, wq, wk, wv, w_out, w_spike, w_au, b_au, w_ad, b_ad, alpha_spike, w_beta, b_beta, beta_spike, w_hn, w_u1, b_u1, w_u2, b_u2, w_ffn, w_ff1, w_ff3, w_ff2)
        key = jax.random.key(seed)
        B, T, D = (8, 256, 128)
        R, F, CK = (64, 512, 4)
        ks = jax.random.split(key, 16)
        n = lambda k, shp, s=0.02: jax.random.normal(k, shp, jnp.float32) * s
        return {'x': jax.random.normal(ks[0], (B, T, D), jnp.float32), 'w_norm_in': jnp.ones((D,), jnp.float32), 'conv_w': n(ks[1], (D, CK), 0.2), 'conv_b': jnp.zeros((D,), jnp.float32), 'wq': n(ks[2], (D, H * DK)), 'wk': n(ks[3], (D, H * DK)), 'wv': n(ks[4], (D, H * DV)), 'w_out': n(ks[5], (H * DV, D)), 'w_spike': n(ks[6], (D, H * DK), 0.1), 'w_au': n(ks[7], (D, R)), 'b_au': jnp.zeros((R,), jnp.float32), 'w_ad': n(ks[8], (R, H * DK)), 'b_ad': jnp.zeros((H * DK,), jnp.float32), 'alpha_spike': jnp.zeros((1, H, DK), jnp.float32), 'w_beta': n(ks[9], (D, H)), 'b_beta': jnp.zeros((H,), jnp.float32), 'beta_spike': jnp.zeros((1, H, DK), jnp.float32), 'w_hn': jnp.ones((H, DV), jnp.float32), 'w_u1': n(ks[10], (D, R)), 'b_u1': jnp.zeros((R,), jnp.float32), 'w_u2': n(ks[11], (R, D)), 'b_u2': jnp.zeros((D,), jnp.float32), 'w_ffn': jnp.ones((D,), jnp.float32), 'w_ff1': n(ks[12], (D, F)), 'w_ff3': n(ks[13], (D, F)), 'w_ff2': n(ks[14], (F, D))}
    _L0_attn_all = _L0_attn_setup()
    _L0_attn_in = {k: v for k, v in _L0_attn_all.items() if k in ('w_norm_in', 'conv_w', 'conv_b', 'wq', 'wk', 'wv', 'w_out', 'w_spike', 'w_au', 'b_au', 'w_ad', 'b_ad', 'alpha_spike', 'w_beta', 'b_beta', 'beta_spike', 'w_hn', 'w_u1', 'b_u1', 'w_u2', 'b_u2', 'w_ffn', 'w_ff1', 'w_ff3', 'w_ff2')}
    del _L0_attn_all

    def _L0_xattn_setup():
        import jax, jax.numpy as jnp
        import numpy as np
        N_HEAD, MODEL_DIM, KEY_DIM, VALUE_DIM = (16, 128, 64, 64)
        B, S = (4, 256)
        EPS = 1e-05
        TEMP = float(np.sqrt(KEY_DIM))
        key = jax.random.key(seed)
        ks = jax.random.split(key, 12)
        d = {'query': jax.random.normal(ks[0], (B, S, MODEL_DIM), jnp.float32), 'key': jax.random.normal(ks[1], (B, S, MODEL_DIM), jnp.float32), 'value': jax.random.normal(ks[2], (B, S, MODEL_DIM), jnp.float32), 'Wq': jax.random.normal(ks[3], (MODEL_DIM, N_HEAD * KEY_DIM), jnp.float32) * np.sqrt(2.0 / (MODEL_DIM + KEY_DIM)), 'bq': jnp.zeros((N_HEAD * KEY_DIM,), jnp.float32), 'Wk': jax.random.normal(ks[4], (MODEL_DIM, N_HEAD * KEY_DIM), jnp.float32) * np.sqrt(2.0 / (MODEL_DIM + KEY_DIM)), 'bk': jnp.zeros((N_HEAD * KEY_DIM,), jnp.float32), 'Wv': jax.random.normal(ks[5], (MODEL_DIM, N_HEAD * VALUE_DIM), jnp.float32) * np.sqrt(2.0 / (MODEL_DIM + VALUE_DIM)), 'bv': jnp.zeros((N_HEAD * VALUE_DIM,), jnp.float32), 'Wo': jax.random.normal(ks[6], (N_HEAD * VALUE_DIM, MODEL_DIM), jnp.float32) * np.sqrt(2.0 / (N_HEAD * VALUE_DIM + MODEL_DIM)), 'bo': jnp.zeros((MODEL_DIM,), jnp.float32), 'ln_gamma': jnp.ones((MODEL_DIM,), jnp.float32), 'ln_beta': jnp.zeros((MODEL_DIM,), jnp.float32)}
        return d
    _L0_xattn_all = _L0_xattn_setup()
    _L0_xattn_in = {k: v for k, v in _L0_xattn_all.items() if k in ('Wq', 'bq', 'Wk', 'bk', 'Wv', 'bv', 'Wo', 'bo', 'ln_gamma', 'ln_beta')}
    del _L0_xattn_all

    def _L0_ffn_setup():
        import jax, jax.numpy as jnp
        import numpy as np
        import math
        D_IN = 128
        FEATURES = (512, 512, 128)
        BATCH, SEQ = (8, 256)

        def _conn_dense(kernel_bool, x):
            w = jnp.where(kernel_bool, jnp.float32(1.0), jnp.float32(-1.0))
            return x @ w
        key = jax.random.key(seed)
        kx, kk0, kk1, kk2 = jax.random.split(key, 4)
        x = jax.random.normal(kx, (BATCH, SEQ, D_IN), dtype=jnp.float32)
        k0 = jax.random.randint(kk0, (2 * D_IN, FEATURES[0]), 0, 2).astype(jnp.bool_)
        k1 = jax.random.randint(kk1, (FEATURES[0], FEATURES[1]), 0, 2).astype(jnp.bool_)
        k2 = jax.random.randint(kk2, (FEATURES[1], FEATURES[2]), 0, 2).astype(jnp.bool_)
        s0 = jnp.asarray(1.0 / math.sqrt(2 * D_IN), dtype=jnp.float32)
        s1 = jnp.asarray(1.0 / math.sqrt(FEATURES[0]), dtype=jnp.float32)
        s2 = jnp.asarray(1.0 / math.sqrt(FEATURES[1]), dtype=jnp.float32)
        return {'x': x, 'k0': k0, 'k1': k1, 'k2': k2, 's0': s0, 's1': s1, 's2': s2}
    _L0_ffn_all = _L0_ffn_setup()
    _L0_ffn_in = {k: v for k, v in _L0_ffn_all.items() if k in ('k0', 'k1', 'k2', 's0', 's1', 's2')}
    del _L0_ffn_all
    return {'x': x, 'ctx_1024': ctx_1024, 'L0_attn_w_norm_in': _L0_attn_in['w_norm_in'], 'L0_attn_conv_w': _L0_attn_in['conv_w'], 'L0_attn_conv_b': _L0_attn_in['conv_b'], 'L0_attn_wq': _L0_attn_in['wq'], 'L0_attn_wk': _L0_attn_in['wk'], 'L0_attn_wv': _L0_attn_in['wv'], 'L0_attn_w_out': _L0_attn_in['w_out'], 'L0_attn_w_spike': _L0_attn_in['w_spike'], 'L0_attn_w_au': _L0_attn_in['w_au'], 'L0_attn_b_au': _L0_attn_in['b_au'], 'L0_attn_w_ad': _L0_attn_in['w_ad'], 'L0_attn_b_ad': _L0_attn_in['b_ad'], 'L0_attn_alpha_spike': _L0_attn_in['alpha_spike'], 'L0_attn_w_beta': _L0_attn_in['w_beta'], 'L0_attn_b_beta': _L0_attn_in['b_beta'], 'L0_attn_beta_spike': _L0_attn_in['beta_spike'], 'L0_attn_w_hn': _L0_attn_in['w_hn'], 'L0_attn_w_u1': _L0_attn_in['w_u1'], 'L0_attn_b_u1': _L0_attn_in['b_u1'], 'L0_attn_w_u2': _L0_attn_in['w_u2'], 'L0_attn_b_u2': _L0_attn_in['b_u2'], 'L0_attn_w_ffn': _L0_attn_in['w_ffn'], 'L0_attn_w_ff1': _L0_attn_in['w_ff1'], 'L0_attn_w_ff3': _L0_attn_in['w_ff3'], 'L0_attn_w_ff2': _L0_attn_in['w_ff2'], 'L0_xattn_Wq': _L0_xattn_in['Wq'], 'L0_xattn_bq': _L0_xattn_in['bq'], 'L0_xattn_Wk': _L0_xattn_in['Wk'], 'L0_xattn_bk': _L0_xattn_in['bk'], 'L0_xattn_Wv': _L0_xattn_in['Wv'], 'L0_xattn_bv': _L0_xattn_in['bv'], 'L0_xattn_Wo': _L0_xattn_in['Wo'], 'L0_xattn_bo': _L0_xattn_in['bo'], 'L0_xattn_ln_gamma': _L0_xattn_in['ln_gamma'], 'L0_xattn_ln_beta': _L0_xattn_in['ln_beta'], 'L0_ffn_k0': _L0_ffn_in['k0'], 'L0_ffn_k1': _L0_ffn_in['k1'], 'L0_ffn_k2': _L0_ffn_in['k2'], 'L0_ffn_s0': _L0_ffn_in['s0'], 'L0_ffn_s1': _L0_ffn_in['s1'], 'L0_ffn_s2': _L0_ffn_in['s2']}

def reference(x, ctx_1024, L0_attn_w_norm_in, L0_attn_conv_w, L0_attn_conv_b, L0_attn_wq, L0_attn_wk, L0_attn_wv, L0_attn_w_out, L0_attn_w_spike, L0_attn_w_au, L0_attn_b_au, L0_attn_w_ad, L0_attn_b_ad, L0_attn_alpha_spike, L0_attn_w_beta, L0_attn_b_beta, L0_attn_beta_spike, L0_attn_w_hn, L0_attn_w_u1, L0_attn_b_u1, L0_attn_w_u2, L0_attn_b_u2, L0_attn_w_ffn, L0_attn_w_ff1, L0_attn_w_ff3, L0_attn_w_ff2, L0_xattn_Wq, L0_xattn_bq, L0_xattn_Wk, L0_xattn_bk, L0_xattn_Wv, L0_xattn_bv, L0_xattn_Wo, L0_xattn_bo, L0_xattn_ln_gamma, L0_xattn_ln_beta, L0_ffn_k0, L0_ffn_k1, L0_ffn_k2, L0_ffn_s0, L0_ffn_s1, L0_ffn_s2):
    import jax
    import jax.numpy as jnp

    def _L0_attn_ref(x, w_norm_in, conv_w, conv_b, wq, wk, wv, w_out, w_spike, w_au, b_au, w_ad, b_ad, alpha_spike, w_beta, b_beta, beta_spike, w_hn, w_u1, b_u1, w_u2, b_u2, w_ffn, w_ff1, w_ff3, w_ff2):
        import jax, jax.numpy as jnp
        import numpy as np
        H, DK, DV = (8, 64, 128)
        DECAY, THR, SBETA = (0.9, 0.5, 10.0)
        EPS = 1e-06

        def _rms(h, w):
            return h * jax.lax.rsqrt(jnp.mean(h * h, axis=-1, keepdims=True) + EPS) * w

        def _forward(x, w_norm_in, conv_w, conv_b, wq, wk, wv, w_out, w_spike, w_au, b_au, w_ad, b_ad, alpha_spike, w_beta, b_beta, beta_spike, w_hn, w_u1, b_u1, w_u2, b_u2, w_ffn, w_ff1, w_ff3, w_ff2):
            B, T, D = x.shape
            h = _rms(x, w_norm_in)
            CK = conv_w.shape[-1]
            hp = jnp.pad(h, ((0, 0), (CK - 1, 0), (0, 0)))
            conv = conv_b + sum((hp[:, j:j + T, :] * conv_w[:, j] for j in range(CK)))
            h = jax.nn.silu(conv)
            q = (h @ wq).reshape(B, T, H, DK)
            k = (h @ wk).reshape(B, T, H, DK)
            v = (h @ wv).reshape(B, T, H, DV)
            q = q / (jnp.linalg.norm(q, axis=-1, keepdims=True) + EPS)
            k = k / (jnp.linalg.norm(k, axis=-1, keepdims=True) + EPS)
            sd = (h @ w_spike).reshape(B, T, H, DK)
            ab = (jax.nn.silu(h @ w_au + b_au) @ w_ad + b_ad).reshape(B, T, H, DK)
            bb = h @ w_beta + b_beta

            def step(carry, inp):
                s, mem = carry
                qt, kt, vt, sdt, abt, bbt = inp
                mem = DECAY * mem + sdt
                sur = jax.nn.sigmoid(SBETA * (mem - THR))
                hard = (mem > THR).astype(x.dtype)
                spike = sur + jax.lax.stop_gradient(hard - sur)
                mem = mem - spike * THR
                alpha = jax.nn.sigmoid(abt + alpha_spike * spike)
                beta = jax.nn.sigmoid(bbt[..., None] + jnp.sum(spike * beta_spike, axis=-1, keepdims=True))
                active = jax.lax.stop_gradient((jnp.sum(hard, axis=-1, keepdims=True) > 0).astype(x.dtype))
                alpha = jnp.where(active > 0, alpha, jnp.ones_like(alpha))
                beta = beta * active
                s = s * alpha[..., None]
                u = jnp.einsum('bhd,bhdv->bhv', kt, s)
                s = s - beta[..., None] * jnp.einsum('bhd,bhv->bhdv', kt, u)
                s = s + beta[..., None] * jnp.einsum('bhd,bhv->bhdv', kt, vt)
                out = jnp.einsum('bhdv,bhd->bhv', s, qt)
                return ((s, mem), out)
            s0 = jnp.zeros((B, H, DK, DV), x.dtype)
            m0 = jnp.zeros((B, H, DK), x.dtype)
            tmaj = lambda a: jnp.moveaxis(a, 1, 0)
            (s, mem), outs = jax.lax.scan(step, (s0, m0), (tmaj(q), tmaj(k), tmaj(v), tmaj(sd), tmaj(ab), tmaj(bb)))
            y = jnp.moveaxis(outs, 0, 1)
            y = y * jax.lax.rsqrt(jnp.mean(y * y, axis=-1, keepdims=True) + EPS) * w_hn
            y = y.reshape(B, T, H * DV)
            gate = jax.nn.sigmoid(jax.nn.silu(x @ w_u1 + b_u1) @ w_u2 + b_u2)
            y = x + y @ w_out * gate
            h2 = _rms(y, w_ffn)
            y = y + jax.nn.silu(h2 @ w_ff1) * (h2 @ w_ff3) @ w_ff2
            return (y, s, mem)

        def _reference_tuple_inner(x, w_norm_in, conv_w, conv_b, wq, wk, wv, w_out, w_spike, w_au, b_au, w_ad, b_ad, alpha_spike, w_beta, b_beta, beta_spike, w_hn, w_u1, b_u1, w_u2, b_u2, w_ffn, w_ff1, w_ff3, w_ff2):
            return _forward(x, w_norm_in, conv_w, conv_b, wq, wk, wv, w_out, w_spike, w_au, b_au, w_ad, b_ad, alpha_spike, w_beta, b_beta, beta_spike, w_hn, w_u1, b_u1, w_u2, b_u2, w_ffn, w_ff1, w_ff3, w_ff2)
        return _reference_tuple_inner(x, w_norm_in, conv_w, conv_b, wq, wk, wv, w_out, w_spike, w_au, b_au, w_ad, b_ad, alpha_spike, w_beta, b_beta, beta_spike, w_hn, w_u1, b_u1, w_u2, b_u2, w_ffn, w_ff1, w_ff3, w_ff2)[0]

    def _L0_xattn_ref(query, key, value, Wq, bq, Wk, bk, Wv, bv, Wo, bo, ln_gamma, ln_beta):
        import jax, jax.numpy as jnp
        import numpy as np
        N_HEAD, MODEL_DIM, KEY_DIM, VALUE_DIM = (16, 128, 64, 64)
        B, S = (4, 256)
        EPS = 1e-05
        TEMP = float(np.sqrt(KEY_DIM))
        b, sq, _ = query.shape
        residual = query
        q = (query @ Wq + bq).reshape(b, sq, N_HEAD, KEY_DIM)
        k = (key @ Wk + bk).reshape(b, key.shape[1], N_HEAD, KEY_DIM)
        v = (value @ Wv + bv).reshape(b, value.shape[1], N_HEAD, VALUE_DIM)
        scores = jnp.einsum('bqhd,bkhd->bhqk', q, k) / TEMP
        attn = jax.nn.softmax(scores, axis=-1)
        out = jnp.einsum('bhqk,bkhd->bqhd', attn, v).reshape(b, sq, N_HEAD * VALUE_DIM)
        out = out @ Wo + bo + residual
        mu = jnp.mean(out, axis=-1, keepdims=True)
        var = jnp.var(out, axis=-1, keepdims=True)
        return (out - mu) * jax.lax.rsqrt(var + EPS) * ln_gamma + ln_beta

    def _L0_ffn_ref(x, k0, k1, k2, s0, s1, s2):
        import jax, jax.numpy as jnp
        import numpy as np
        import math
        D_IN = 128
        FEATURES = (512, 512, 128)
        BATCH, SEQ = (8, 256)

        def _conn_dense(kernel_bool, x):
            w = jnp.where(kernel_bool, jnp.float32(1.0), jnp.float32(-1.0))
            return x @ w
        h = jnp.concatenate([x, -x], axis=-1)
        h = s0 * _conn_dense(k0, h)
        h = jax.nn.relu(h) * 2
        h = s1 * _conn_dense(k1, h)
        h = jax.nn.relu(h) * 2
        h = s2 * _conn_dense(k2, h)
        return h
    x = x + _L0_attn_ref(_layernorm(x, axis=-1), L0_attn_w_norm_in, L0_attn_conv_w, L0_attn_conv_b, L0_attn_wq, L0_attn_wk, L0_attn_wv, L0_attn_w_out, L0_attn_w_spike, L0_attn_w_au, L0_attn_b_au, L0_attn_w_ad, L0_attn_b_ad, L0_attn_alpha_spike, L0_attn_w_beta, L0_attn_b_beta, L0_attn_beta_spike, L0_attn_w_hn, L0_attn_w_u1, L0_attn_b_u1, L0_attn_w_u2, L0_attn_b_u2, L0_attn_w_ffn, L0_attn_w_ff1, L0_attn_w_ff3, L0_attn_w_ff2)
    x = x + _L0_xattn_ref(_layernorm(x, axis=-1), ctx_1024, ctx_1024, L0_xattn_Wq, L0_xattn_bq, L0_xattn_Wk, L0_xattn_bk, L0_xattn_Wv, L0_xattn_bv, L0_xattn_Wo, L0_xattn_bo, L0_xattn_ln_gamma, L0_xattn_ln_beta)
    x = x + _L0_ffn_ref(_layernorm(x, axis=-1), L0_ffn_k0, L0_ffn_k1, L0_ffn_k2, L0_ffn_s0, L0_ffn_s1, L0_ffn_s2)
    return x

_drawn_inputs = setup_inputs


def setup_inputs(seed=0):
    import zlib

    import numpy as np

    out = dict(_drawn_inputs(seed))
    spreads = {'L0_attn_w_norm_in': (1.0, 0.2),
     'L0_attn_conv_b': (0.0, 0.1),
     'L0_attn_b_au': (0.0, 0.8),
     'L0_attn_b_ad': (0.0, 0.8),
     'L0_attn_alpha_spike': (0.0, 0.8),
     'L0_attn_b_beta': (0.0, 0.8),
     'L0_attn_beta_spike': (0.0, 0.8),
     'L0_attn_w_hn': (1.0, 0.559),
     'L0_attn_b_u1': (0.0, 0.8),
     'L0_attn_b_u2': (0.0, 0.8),
     'L0_attn_w_ffn': (1.0, 0.6),
     'L0_xattn_bq': (0.0, 2.0),
     'L0_xattn_bk': (0.0, 2.0),
     'L0_xattn_bv': (0.0, 0.8),
     'L0_xattn_bo': (0.0, 1.767),
     'L0_xattn_ln_gamma': (1.0, 0.6),
     'L0_xattn_ln_beta': (0.0, 0.8)}
    factors = {'L0_attn_w_spike': 2.902,
     'L0_attn_w_au': 8.0,
     'L0_attn_w_ad': 8.0,
     'L0_attn_w_beta': 8.0,
     'L0_attn_w_u1': 8.0,
     'L0_attn_w_u2': 8.0,
     'L0_attn_w_ff1': 8.0,
     'L0_attn_w_ff3': 8.0,
     'L0_attn_w_ff2': 8.0,
     'L0_xattn_Wq': 2.905}
    for name, (base, spread) in spreads.items():
        noise = np.random.default_rng([zlib.crc32(name.encode()), seed]).standard_normal(out[name].shape)
        drawn = base * np.exp(spread * noise) if base else spread * noise
        out[name] = jnp.asarray(drawn.astype(out[name].dtype))
    for name, factor in factors.items():
        out[name] = (out[name] * factor).astype(out[name].dtype)
    return out
```

```python
from contextlib import ExitStack

import concourse.bass as bass
from concourse import mybir

P = 128
F32 = mybir.dt.float32
U32 = mybir.dt.uint32
U8 = mybir.dt.uint8
ACT = mybir.ActivationFunctionType
ALU = mybir.AluOpType
AX = mybir.AxisListType

VEC = {}
_at = 0
for _name, _n in (("conv_w", 4), ("conv_b", 1), ("w_norm", 1), ("b_ad", 4), ("alpha_spike", 4),
                  ("beta_spike", 4), ("b_au", 1), ("b_u1", 1), ("b_u2", 1), ("w_hn", 8), ("w_ffn", 1),
                  ("b_beta", 4), ("bq", 8), ("bk", 8), ("bv", 8), ("bo", 1), ("ln_gamma", 1),
                  ("ln_beta", 1), ("s0", 1), ("s1", 1), ("s2", 1)):
    VEC[_name] = (_at, _n)
    _at += _n
NVEC = _at


def decoder_kernel(nc, x, ctx_in, vec_in, wq, wk, w_spike, wv, w_out, w_au, w_ad, w_beta, w_u1, w_u2,
                   w_ff1, w_ff3, w_ff2, Wq, Wk, Wv, Wo, k0, k1, k2, out):
    B, T, D = x.shape
    TOK = B * T
    NT = TOK // P
    DK, DV = 64, 128
    HP = wq.shape[1] // P
    C = 64
    NC = T // C
    LEVELS = 6
    R = w_au.shape[1]
    FT = w_ff1.shape[1] // P
    XP = Wq.shape[1] // P
    XH = 2 * XP
    S = ctx_in.shape[1]
    CTX = B * S
    assert D == P and 2 * DK == P and DV == P and T == 512 and HP == 4 and XP == 8

    ctx = ExitStack()
    with ctx:
        def sb(name, shape, dt=F32):
            return ctx.enter_context(nc.sbuf_tensor(name, shape, dt))

        def sem(name):
            return ctx.enter_context(nc.semaphore(name))

        bank = [ctx.enter_context(nc.psum_tensor(f"bank{i}", [P, 512], F32)) for i in range(8)]

        qT = sb("qT", [P, HP, TOK])
        kT = sb("kT", [P, HP, TOK])
        gates = sb("gates", [P, 2, HP, TOK])
        aT, bT = gates[:, 0], gates[:, 1]
        zT = sb("zT", [P, TOK])
        hT = sb("hT", [P, TOK])
        xT = sb("xT", [P, TOK])
        wv_sb = sb("wv_sb", [P, HP, 2, DV])
        wout_sb = sb("wout_sb", [P, 2 * HP, D])
        wu1_sb = sb("wu1_sb", [P, R])
        wu2_sb = sb("wu2_sb", [R, D])
        ident = sb("ident", [P, P])
        bdones = sb("bdones", [P, P])
        mean_w = sb("mean_w", [P, P])
        mask = sb("mask", [P, LEVELS, P])
        vec = sb("vec", [P, NVEC])
        WORK = 10500
        work = sb("work", [P, WORK])
        used = [0]

        def region(shape, of=work, cursor=used):
            n = 1
            for s in shape:
                n *= s
            flat = of[:, cursor[0]:cursor[0] + n]
            cursor[0] += n
            assert cursor[0] <= of.shape[1], cursor
            names = "abcd"[:len(shape)]
            if len(shape) == 1:
                return flat
            sizes = {c: s for c, s in zip(names[1:], shape[1:])}
            return flat.rearrange(f"p ({' '.join(names)}) -> p {' '.join(names)}", **sizes)

        def v(name, i=0, rows=P):
            return vec[0:rows, VEC[name][0] + i:VEC[name][0] + i + 1]

        used[0] = 0
        wq_sb = region([HP, P])
        wk_sb = region([HP, P])
        wsp_sb = region([HP, P])
        wad_sb = region([HP, P])[0:R]
        wau_sb = region([R])
        wbeta_sb = region([2 * HP])
        wbeta_rep = region([HP, 2, DK])
        bspike_bd = region([HP, P])
        auT = region([TOK])[0:R]
        early_end = used[0]
        PAD = 3
        h0T = region([B, T + PAD])
        xn = bT.rearrange("p a t -> p (a t)")[:, 0:TOK].rearrange("p (n d) -> p n d", n=NT)
        zn = bT.rearrange("p a t -> p (a t)")[:, TOK:2 * TOK].rearrange("p (n d) -> p n d", n=NT)
        hn = bT.rearrange("p a t -> p (a t)")[:, 2 * TOK:3 * TOK].rearrange("p (n d) -> p n d", n=NT)
        sqn = bT.rearrange("p a t -> p (a t)")[:, 3 * TOK:4 * TOK].rearrange("p (n d) -> p n d", n=NT)
        conv = xn.rearrange("p n d -> p (n d)").rearrange("p (b t) -> p b t", b=B)
        sig = sqn.rearrange("p n d -> p (n d)").rearrange("p (b t) -> p b t", b=B)
        mom = sb("mom", [P, 6, NT])
        half = sb("half", [P, NT])

        w_loaded = sem("w_loaded")
        x_loaded = sem("x_loaded")
        consts = sem("consts")
        setup = sem("setup")
        vn = sem("vn")
        pn = sem("pn")
        an = sem("an")
        tr_mm = sem("tr_mm")
        tr_out = sem("tr_out")
        tr_out_v = sem("tr_out_v")
        conv_ok = sem("conv_ok")
        sig_ok = sem("sig_ok")
        h_ok = sem("h_ok")

        N_W = 13
        with nc.Block() as block:
            @block.sync
            def _(sp):
                sp.dma_start(xn, x.rearrange("b t d -> (b t) d").rearrange("(n p) d -> p n d", p=P))\
                    .then_inc(x_loaded, 16)
                sp.dma_start(vec[:, :], vec_in).then_inc(w_loaded, 16)
                for dst, src in ((wsp_sb, w_spike.rearrange("d (a n) -> d a n", a=HP)),
                                 (wq_sb, wq.rearrange("d (a n) -> d a n", a=HP)),
                                 (wk_sb, wk.rearrange("d (a n) -> d a n", a=HP)),
                                 (wau_sb, w_au), (wad_sb, w_ad.rearrange("d (a n) -> d a n", a=HP)),
                                 (wbeta_sb, w_beta),
                                 (wv_sb[:, :, :, :], wv.rearrange("d (a b n) -> d a b n", a=HP, b=2)),
                                 (wu1_sb[:, :], w_u1), (wu2_sb[:, :], w_u2)):
                    sp.dma_start(dst, src).then_inc(w_loaded, 16)
                sp.dma_start(wout_sb[:, :, :], w_out.rearrange("(h v) d -> v h d", v=DV)).then_inc(w_loaded, 16)

            @block.gpsimd
            def _(gp):
                gp.memset(half[:, :], -0.5).then_inc(consts, 1)
                gp.memset(h0T[:, :, 0:PAD], 0.0).then_inc(consts, 1)
                gp.memset(mean_w[:, :], 1.0 / D).then_inc(consts, 1)
                gp.memset(ident[:, :], 0.0).then_inc(consts, 1)
                gp.memset(bdones[:, :], 1.0).then_inc(consts, 1)
                gp.memset(mask[:, :, :], 0.0).then_inc(consts, 1)
                gp.wait_ge(consts, 6)
                gp.affine_select(out=ident[:, :], in_=ident[:, :], compare_op=ALU.not_equal, fill=1.0,
                                 base=0, pattern=[[-1, P]], channel_multiplier=1).then_inc(consts, 1)

                def keep_block(t, step, n, width, size, done):
                    gp.affine_select(out=t, in_=t, compare_op=ALU.is_ge, fill=0.0, base=0,
                                     pattern=[[-step, n], [0, width]], channel_multiplier=1).then_inc(consts, 1)
                    gp.wait_ge(consts, done + 1)
                    gp.affine_select(out=t, in_=t, compare_op=ALU.is_ge, fill=0.0, base=size - 1,
                                     pattern=[[step, n], [0, width]], channel_multiplier=-1).then_inc(consts, 1)

                keep_block(bdones[:, :].rearrange("p (a t) -> p a t", a=2), C, 2, C, C, 7)
                done = 9
                for l in range(LEVELS):
                    L = 1 << l
                    late = mask[:, l, :].rearrange("p (j s t) -> p j s t", s=2, t=L)[:, :, 1, :]
                    gp.memset(late, 1.0).then_inc(consts, 1)
                    gp.wait_ge(consts, done + 1)
                    keep_block(late, 2 * L, P // (2 * L), L, L, done + 1)
                    done += 3
                for i, (src, dst) in enumerate(((1, 2), (3, 4))):
                    gp.wait_ge(vn, (4, 8)[i])
                    gp.tensor_tensor(mom[:, dst, :], mom[:, src, :], half[:, :], ALU.pow).then_inc(pn, 1)

            N_CONST = 9 + 3 * LEVELS

            @block.vector
            def _(ve):
                ve.wait_ge(x_loaded, 16)
                ve.tensor_reduce(mom[:, 0, :], xn, AX.X, ALU.add).then_inc(vn, 1)
                ve.wait_ge(vn, 1)
                ve.tensor_scalar(mom[:, 5, :], mom[:, 0, :], 1.0 / D, None, ALU.mult).then_inc(vn, 1)
                ve.wait_ge(vn, 2)
                ve.tensor_tensor(zn, xn, mom[:, 5, :].unsqueeze(2).broadcast_to([P, NT, D]),
                                 ALU.subtract).then_inc(vn, 1)
                ve.wait_ge(an, 1)
                ve.tensor_reduce(mom[:, 0, :], sqn, AX.X, ALU.add).then_inc(setup, 1)
                ve.wait_ge(setup, 1)
                ve.tensor_scalar(mom[:, 1, :], mom[:, 0, :], 1.0 / D, 1e-5, ALU.mult, ALU.add).then_inc(vn, 1)
                ve.wait_ge(pn, 1)
                ve.tensor_tensor(zn, zn, mom[:, 2, :].unsqueeze(2).broadcast_to([P, NT, D]),
                                 ALU.mult).then_inc(vn, 1)
                ve.wait_ge(vn, 5)
                ve.tensor_tensor(sqn, zn, zn, ALU.mult).then_inc(vn, 1)
                ve.wait_ge(vn, 6)
                ve.tensor_reduce(mom[:, 0, :], sqn, AX.X, ALU.add).then_inc(vn, 1)
                ve.wait_ge(vn, 7)
                ve.tensor_scalar(mom[:, 3, :], mom[:, 0, :], 1.0 / D, 1e-6, ALU.mult, ALU.add).then_inc(vn, 1)
                ve.wait_ge(pn, 2)
                ve.tensor_tensor(hn, zn, mom[:, 4, :].unsqueeze(2).broadcast_to([P, NT, D]),
                                 ALU.mult).then_inc(vn, 1)
                for n in range(NT // 4):
                    for k, dst in enumerate((xT, zT)):
                        ve.wait_ge(tr_mm, (0, 4)[k] + n + 1)
                        ve.tensor_copy(dst[:, n * 512:(n + 1) * 512], bank[(4 * k + n) % 8][:, :]).then_inc(tr_out_v, 1)
                ve.wait_ge(tr_out, NT // 4)
                ve.wait_ge(w_loaded, 16 * 11)
                ve.tensor_scalar(conv, h0T[:, :, 0:T], v("conv_w", 0), v("conv_b"), ALU.mult, ALU.add)\
                    .then_inc(conv_ok, 1)
                for j in range(1, PAD + 1):
                    ve.wait_ge(conv_ok, j)
                    ve.scalar_tensor_tensor(conv, h0T[:, :, j:j + T], v("conv_w", j), conv, ALU.mult, ALU.add)\
                        .then_inc(conv_ok, 1)
                for b in range(B):
                    ve.wait_ge(sig_ok, b + 1)
                    ve.tensor_tensor(hT[:, b * T:(b + 1) * T], conv[:, b], sig[:, b], ALU.mult).then_inc(h_ok, 1)
                ve.tensor_copy(wbeta_rep, wbeta_sb.rearrange("p (a b) -> p a b", b=2).unsqueeze(3)
                               .broadcast_to([P, HP, 2, DK])).then_inc(setup, 1)
                for hp in range(HP):
                    ve.tensor_scalar(bspike_bd[:, hp, :], bdones[:, :], v("beta_spike", hp), None, ALU.mult)\
                        .then_inc(setup, 1)
                for h in range(2 * HP):
                    ve.tensor_scalar(wout_sb[:, h, :], wout_sb[:, h, :], v("w_hn", h), None, ALU.mult)\
                        .then_inc(setup, 1)

            @block.scalar
            def _(ac):
                ac.wait_ge(vn, 3)
                ac.activation(sqn, zn, ACT.Square).then_inc(an, 1)
                ac.wait_ge(w_loaded, 16 * 11)
                ac.wait_ge(consts, 2)
                for b in range(B):
                    ac.wait_ge(tr_mm, 8 + b + 1)
                    ac.activation(h0T[:, b, PAD:], bank[b][:, :], ACT.Copy, scale=v("w_norm")).then_inc(tr_out, 1)
                ac.wait_ge(conv_ok, PAD + 1)
                for b in range(B):
                    ac.activation(sig[:, b], conv[:, b], ACT.Sigmoid).then_inc(sig_ok, 1)

            @block.tensor
            def _(pe):
                pe.wait_ge(consts, N_CONST)
                pe.wait_ge(x_loaded, 16)
                for k, (src, ready) in enumerate(((xn, 3), (zn, 5), (hn, 9))):
                    pe.wait_ge(vn, ready)
                    for n in range(NT // 4):
                        if k == 2:
                            pe.wait_ge(tr_out_v, 2 * n + 1)
                        for j in range(4):
                            last = pe.transpose(bank[(4 * k + n) % 8][:, j * P:(j + 1) * P],
                                                src[:, 4 * n + j, :], ident[:, :])
                        last.then_inc(tr_mm, 1)

        used[0] = early_end
        sq_buf = region([2, 512])
        nrm = region([2, 512])
        au_sig = region([512])[0:R]
        NU = 1 + 3 * HP
        units = [("au", 0)] + [(what, hp) for what in ("sd", "q", "k") for hp in range(HP)]
        QK0 = 1 + HP
        NQK = 2 * HP

        proj_mm = sem("proj_mm")
        au_sg = sem("au_sg")
        au_ok = sem("au_ok")
        sd_ok = sem("sd_ok")
        sq_ok = sem("sq_ok")
        nrm_mm = sem("nrm_mm")
        nrm_sqrt = sem("nrm_sqrt")
        nrm_add = sem("nrm_add")
        nrm_inv = sem("nrm_inv")
        qk_ok = sem("qk_ok")

        with nc.Block() as block:
            @block.tensor
            def _(pe):
                with pe.Fori(0, B) as b:
                    tok = bass.ds(b * T, T)

                    def norm(j):
                        pe.wait_ge(sq_ok, b * NQK + j + 1)
                        pe.wait_ge(nrm_sqrt, b * NQK + j - 1) if j >= 2 else pe.wait_ge(nrm_sqrt, b * NQK)
                        pe.matmul(bank[4 + j % 2][:, :], bdones[:, :], sq_buf[:, j % 2, :],
                                  start=True, stop=True).then_inc(nrm_mm, 1)

                    for u, (what, hp) in enumerate(units):
                        if u < 4:
                            pe.wait_ge(qk_ok, b * NQK)
                        elif u == 4:
                            pe.wait_ge(au_ok, b + 1)
                        elif u < 4 + QK0:
                            pe.wait_ge(sd_ok, b * HP + u - 4)
                        else:
                            pe.wait_ge(qk_ok, b * NQK + u - 4 - QK0 + 1)
                        if what == "au":
                            pe.matmul(bank[0][0:R, :], wau_sb[:, :], hT[:, tok], start=True, stop=True)\
                                .then_inc(proj_mm, 1)
                        else:
                            w = {"sd": wsp_sb, "q": wq_sb, "k": wk_sb}[what]
                            pe.matmul(bank[u % 4][:, :], w[:, hp, :], hT[:, tok], start=True, stop=True)\
                                .then_inc(proj_mm, 1)
                        if u >= QK0 + 1:
                            norm(u - QK0 - 1)
                    norm(NQK - 1)

            @block.scalar
            def _(ac):
                with ac.Fori(0, B) as b:
                    tok = bass.ds(b * T, T)
                    ac.wait_ge(proj_mm, b * NU + 1)
                    ac.wait_ge(au_ok, b)
                    ac.activation(au_sig, bank[0][0:R, :], ACT.Sigmoid, bias=v("b_au", 0, R)).then_inc(au_sg, 1)
                    for hp in range(HP):
                        ac.wait_ge(proj_mm, b * NU + 2 + hp)
                        ac.mul(aT[:, hp, tok], bank[(1 + hp) % 4][:, :], 2.0).then_inc(sd_ok, 1)

                    def root(j):
                        ac.wait_ge(nrm_mm, b * NQK + j + 1)
                        ac.wait_ge(qk_ok, b * NQK + j - 1) if j >= 2 else ac.wait_ge(qk_ok, b * NQK)
                        ac.activation(nrm[:, j % 2, :], bank[4 + j % 2][:, :], ACT.Sqrt).then_inc(nrm_sqrt, 1)

                    for j in range(NQK):
                        ac.wait_ge(proj_mm, b * NU + QK0 + j + 1)
                        ac.wait_ge(nrm_mm, b * NQK + j - 1) if j >= 2 else ac.wait_ge(nrm_mm, b * NQK)
                        ac.activation(sq_buf[:, j % 2, :], bank[(QK0 + j) % 4][:, :], ACT.Square).then_inc(sq_ok, 1)
                        if j >= 1:
                            root(j - 1)
                    root(NQK - 1)

            @block.vector
            def _(ve):
                with ve.Fori(0, B) as b:
                    tok = bass.ds(b * T, T)
                    ve.wait_ge(au_sg, b + 1)
                    ve.scalar_tensor_tensor(auT[:, tok], bank[0][0:R, :], v("b_au", 0, R), au_sig,
                                            ALU.add, ALU.mult).then_inc(au_ok, 1)
                    for j in range(NQK):
                        dst = (qT if j < HP else kT)[:, j % HP, tok]
                        ve.wait_ge(nrm_sqrt, b * NQK + j + 1)
                        ve.tensor_scalar(nrm[:, j % 2, :], nrm[:, j % 2, :], 1e-6, None, ALU.add).then_inc(nrm_add, 1)
                        ve.wait_ge(nrm_add, b * NQK + j + 1)
                        ve.reciprocal(nrm[:, j % 2, :], nrm[:, j % 2, :]).then_inc(nrm_inv, 1)
                        ve.wait_ge(nrm_inv, b * NQK + j + 1)
                        ve.tensor_tensor(dst, bank[(QK0 + j) % 4][:, :], nrm[:, j % 2, :], ALU.mult)\
                            .then_inc(qk_ok, 1)

        neg_mem = mom[:, 0:2, :].rearrange("p a n -> p (a n)")[:, 0:HP * B]
        mem = aT.rearrange("p a (b t) -> p (a b) t", b=B)
        mem_z = sem("mem_z")
        charged = sem("charged")
        fired = sem("fired")
        STEPS = 32

        with nc.Block() as block:
            @block.vector
            def _(ve):
                ve.memset(neg_mem, 0.0).then_inc(mem_z, 1)
                ve.wait_ge(mem_z, 1)
                with ve.Fori(0, T // STEPS) as r:
                    for j in range(STEPS):
                        now = mem[:, :, bass.ds(r * STEPS + j, 1)].squeeze(2)
                        ve.wait_ge(fired, r * STEPS + j)
                        ve.scalar_tensor_tensor(now, neg_mem, -0.9, now, ALU.mult, ALU.add).then_inc(charged, 1)
                        ve.wait_ge(charged, r * STEPS + j + 1)
                        ve.scalar_tensor_tensor(neg_mem, now, 1.0, now, ALU.is_gt, ALU.subtract).then_inc(fired, 1)

        used[0] = early_end
        spk = region([2, 512])
        zal = region([2, 512])
        al0 = region([2, 512])
        be0 = region([2, 512])
        NG = HP
        spk_ok = sem("spk_ok")
        cnt_mm = sem("cnt_mm")
        beta_mm = sem("beta_mm")
        ab_mm = sem("ab_mm")
        zal_ok = sem("zal_ok")
        al0_ok = sem("al0_ok")
        be0_ok = sem("be0_ok")
        alpha_ok = sem("alpha_ok")
        beta_ok = sem("beta_ok")

        with nc.Block() as block:
            @block.tensor
            def _(pe):
                with pe.Fori(0, B) as b:
                    tok = bass.ds(b * T, T)
                    for g in range(NG):
                        n, s = b * NG + g, g % 2
                        pe.wait_ge(spk_ok, n + 1)
                        pe.wait_ge(beta_ok, n - 1) if g >= 2 else pe.wait_ge(beta_ok, b * NG)
                        pe.matmul(bank[4 * s + 1][:, :], bdones[:, :], spk[:, s, :], start=True, stop=True)\
                            .then_inc(cnt_mm, 1)
                        pe.matmul(bank[4 * s][:, :], wad_sb[:, g, :], auT[:, tok], start=True, stop=True)\
                            .then_inc(ab_mm, 1)
                        pe.matmul(bank[4 * s + 2][:, :], wbeta_rep[:, g].rearrange("p a b -> p (a b)"),
                                  hT[:, tok], start=True, stop=False)
                        pe.matmul(bank[4 * s + 2][:, :], bspike_bd[:, g, :], spk[:, s, :],
                                  start=False, stop=True).then_inc(beta_mm, 1)

            @block.vector
            def _(ve):
                with ve.Fori(0, B) as b:
                    tok = bass.ds(b * T, T)
                    for g in range(NG):
                        n, s = b * NG + g, g % 2
                        ve.wait_ge(beta_mm, n - 1) if g >= 2 else ve.wait_ge(beta_mm, b * NG)
                        ve.tensor_scalar(spk[:, s, :], aT[:, g, tok], 1.0, None, ALU.is_gt).then_inc(spk_ok, 1)
                        ve.wait_ge(spk_ok, n + 1)
                        ve.wait_ge(ab_mm, n + 1)
                        ve.wait_ge(al0_ok, n - 1) if g >= 2 else ve.wait_ge(al0_ok, b * NG)
                        ve.scalar_tensor_tensor(zal[:, s, :], spk[:, s, :], v("alpha_spike", g), bank[4 * s][:, :],
                                                ALU.mult, ALU.add).then_inc(zal_ok, 1)
                        ve.wait_ge(cnt_mm, n + 1)
                        ve.wait_ge(al0_ok, n + 1)
                        ve.scalar_tensor_tensor(aT[:, g, tok], bank[4 * s + 1][:, :], 0.0, al0[:, s, :],
                                                ALU.is_equal, ALU.max).then_inc(alpha_ok, 1)
                        ve.wait_ge(be0_ok, n + 1)
                        ve.scalar_tensor_tensor(bT[:, g, tok], bank[4 * s + 1][:, :], 0.0, be0[:, s, :],
                                                ALU.is_gt, ALU.mult).then_inc(beta_ok, 1)

            @block.scalar
            def _(ac):
                with ac.Fori(0, B) as b:
                    for g in range(NG):
                        n, s = b * NG + g, g % 2
                        ac.wait_ge(zal_ok, n + 1)
                        ac.wait_ge(beta_ok, n - 1) if g >= 2 else ac.wait_ge(beta_ok, b * NG)
                        ac.activation(al0[:, s, :], zal[:, s, :], ACT.Sigmoid, bias=v("b_ad", g)).then_inc(al0_ok, 1)
                        ac.wait_ge(beta_mm, n + 1)
                        ac.activation(be0[:, s, :], bank[4 * s + 2][:, :], ACT.Sigmoid, bias=v("b_beta", g))\
                            .then_inc(be0_ok, 1)

        used[0] = 0
        state = region([B, HP, DV])
        KS = region([HP, 2, C])
        KQ = region([2, HP, C])
        KPn = region([HP, 2, C])
        QPb = region([HP, 2, C])
        AQ = region([HP, 2, C])
        NE = 3
        E = region([NE, HP, P])
        XY = region([2, 2, 2, P])
        Z = region([2, 2, P])
        KSn = region([HP, P])
        res = region([HP, DV])
        U = region([HP, DV])
        On = res
        hc = region([C])
        tot = region([HP * 2 * (2 * C)])
        ms = region([4, HP])
        tot_at = [2 * HP * (2 * C - (2 * C >> l)) for l in range(LEVELS + 1)]
        T2 = [tot[:, tot_at[l]:tot_at[l] + (2 * HP * C >> l)].rearrange("p (a x j) -> p a x j", a=HP, x=2)
              for l in range(LEVELS + 1)]
        G = 2
        GP = HP // G
        psL, psZ, psXY, psR, psO = bank[0:2], bank[2:4], bank[4:6], bank[6], bank[7]

        zeroed = sem("zeroed")
        kq_ok = sem("kq_ok")
        ks_ok = sem("ks_ok")
        tot_ok = sem("tot_ok")
        lvl_mm = sem("lvl_mm")
        diag_mm = sem("diag_mm")
        e_ok = sem("e_ok")
        aq_ok = sem("aq_ok")
        x_init = sem("x_init")
        yt_mm = sem("yt_mm")
        xy_ok = sem("xy_ok")
        z_mm = sem("z_mm")
        z_ok = sem("z_ok")
        dxy_mm = sem("dxy_mm")
        hc_ok = sem("hc_ok")
        kpn_ok = sem("kpn_ok")
        qpb_ok = sem("qpb_ok")
        ksn_mm = sem("ksn_mm")
        ksn_ok = sem("ksn_ok")
        res_mm = sem("res_mm")
        res_ok = sem("res_ok")
        u_mm = sem("u_mm")
        u_ok = sem("u_ok")
        o_mm = sem("o_mm")
        o_sq = sem("o_sq")
        ms_ok = sem("ms_ok")
        rr_ok = sem("rr_ok")
        s_mm = sem("s_mm")
        s_ok = sem("s_ok")
        on_ok = sem("on_ok")
        yout_mm = sem("yout_mm")
        yout_ok = sem("yout_ok")
        NKQ = LEVELS + 1
        NKS = LEVELS + 2
        NINV = LEVELS - 1

        def halves(t):
            return [t[C * par:C * par + C, :, par, :] for par in range(2)]

        def rounds(eng, body):
            with eng.Fori(0, NC) as c:
                with eng.Fori(0, B) as b:
                    body(c * B + b, b, bass.ds(b * T + c * C, C))

        with nc.Block() as block:
            @block.gpsimd
            def _(gp):
                for t in (state, KS, KPn, QPb):
                    gp.memset(t, 0.0).then_inc(zeroed, 1)
                gp.memset(ms[:, 2, :], -0.5).then_inc(zeroed, 1)
                gp.memset(ms[:, 3, :], 1e-6).then_inc(zeroed, 1)
                gp.wait_ge(zeroed, 6)

                def body(it, b, tok):
                    gp.wait_ge(s_ok, it * HP)
                    gp.tensor_copy(T2[0], aT[:, :, tok].unsqueeze(2).broadcast_to([P, HP, 2, C])).then_inc(tot_ok, 1)
                    gp.wait_ge(ksn_mm, it)
                    gp.wait_ge(tot_ok, it * NKQ + 1)
                    for par, dst in enumerate(halves(KS)):
                        rows = slice(C * par, C * par + C)
                        gp.tensor_tensor(dst, kT[rows, :, tok], bT[rows, :, tok], ALU.mult).then_inc(ks_ok, 1)
                        gp.wait_ge(ks_ok, it * NKS + par + 1)
                    for l in range(LEVELS):
                        L = 1 << l
                        pair = T2[l].rearrange("p a x (j s) -> p (a x j) s", s=2)
                        gp.tensor_tensor(T2[l + 1].rearrange("p a x j -> p (a x j)"), pair[:, :, 0], pair[:, :, 1],
                                         ALU.mult).then_inc(tot_ok, 1)
                        gp.wait_ge(lvl_mm, it * LEVELS + l + 1)
                        if l == 0:
                            gp.wait_ge(diag_mm, it + 1)
                        first = KS.rearrange("p a x (j s t) -> p (a x j) s t", s=2, t=L)[:, :, 0, :]
                        gp.tensor_tensor(first, first, pair[:, :, 1].unsqueeze(2).broadcast_to([P, HP * C // L, L]),
                                         ALU.mult).then_inc(ks_ok, 1)
                        gp.wait_ge(tot_ok, it * NKQ + l + 2)
                        gp.wait_ge(ks_ok, it * NKS + l + 3)
                    gp.wait_ge(o_sq, it + 1)
                    gp.wait_ge(on_ok, it)
                    gp.tensor_tensor(ms[:, 0, :], ms[:, 0, :], ms[:, 3, :], ALU.add).then_inc(ms_ok, 1)
                    gp.wait_ge(ms_ok, it + 1)
                    gp.tensor_tensor(ms[:, 1, :], ms[:, 0, :], ms[:, 2, :], ALU.pow).then_inc(rr_ok, 1)

                rounds(gp, body)

            @block.vector
            def _(ve):
                ve.wait_ge(zeroed, 6)

                def invert(it, l, g):
                    ve.wait_ge(dxy_mm, it * G * NINV + G * (l - 1) + g + 1)
                    n = 2 if l < NINV else 1
                    ps = psXY[g][:, 0:n * GP * P].rearrange("p (x h t) -> p x h t", x=n, h=GP)
                    ve.tensor_tensor(XY[:, g, 0:n], XY[:, g, 0:n], ps, ALU.subtract).then_inc(xy_ok, 1)

                def body(it, b, tok):
                    ve.wait_ge(qpb_ok, it * 2)
                    ve.wait_ge(lvl_mm, it * LEVELS)
                    ve.tensor_tensor(KQ[:, 0], kT[:, :, tok], aT[:, :, tok], ALU.mult)
                    ve.tensor_tensor(KQ[:, 1], qT[:, :, tok], aT[:, :, tok], ALU.mult).then_inc(kq_ok, 1)
                    for l in range(LEVELS):
                        L = 1 << l
                        late = KQ.rearrange("p x a (j s t) -> p x a j s t", s=2, t=L)[:, :, :, :, 1, :]
                        by = T2[l][:, :, 0, :].rearrange("p a (j s) -> p a j s", s=2)[:, :, :, 0]
                        ve.wait_ge(lvl_mm, it * LEVELS + l + 1)
                        ve.wait_ge(tot_ok, it * NKQ + l + 1)
                        ve.wait_ge(kq_ok, it * NKQ + l + 1)
                        for x_ in range(2):
                            last = ve.tensor_tensor(late[:, x_], late[:, x_],
                                                    by.unsqueeze(3).broadcast_to([P, HP, C // (2 * L), L]), ALU.mult)
                        last.then_inc(kq_ok, 1)
                        ps = psLv[l % 2]
                        mk = mask[:, l, :].rearrange("p (x t) -> p x t", x=2).unsqueeze(1)
                        if l == 0:
                            ve.wait_ge(diag_mm, it + 1)
                            ve.wait_ge(o_mm, it)
                            ve.tensor_tensor(AQ, psZ[1][:, 0:HP * C].rearrange("p (a t) -> p a t", a=HP)
                                             .unsqueeze(2).broadcast_to([P, HP, 2, C]),
                                             ident[:, :].rearrange("p (x t) -> p x t", x=2).unsqueeze(1)
                                             .broadcast_to([P, HP, 2, C]), ALU.mult).then_inc(aq_ok, 1)
                        ve.wait_ge(aq_ok, it * NKQ + l + 1)
                        if l < NE:
                            ve.wait_ge(z_mm, it * G * NINV)
                        elif l == NE:
                            ve.wait_ge(yt_mm, (it + 1) * G)
                        else:
                            ve.wait_ge(z_mm, it * G * NINV + G * (l - NE))
                        ve.tensor_tensor(E[:, l % NE].rearrange("p a (x t) -> p a x t", x=2),
                                         ps[:, :, 0, :].unsqueeze(2).broadcast_to([P, HP, 2, C]),
                                         mk.broadcast_to([P, HP, 2, C]), ALU.mult).then_inc(e_ok, 1)
                        ve.copy_predicated(AQ, mk.broadcast_to([P, HP, 2, C]).bitcast(U32),
                                           ps[:, :, 1, :].unsqueeze(2).broadcast_to([P, HP, 2, C])).then_inc(aq_ok, 1)
                        if l == 0:
                            ve.wait_ge(e_ok, it * LEVELS + 1)
                            ve.wait_ge(u_mm, it)
                            for g in range(G):
                                last = ve.tensor_tensor(XY[:, g, 0], ident[:, :].unsqueeze(1).broadcast_to([P, GP, P]),
                                                        E[:, 0, g * GP:(g + 1) * GP, :], ALU.subtract)
                            last.then_inc(x_init, 1)
                        if l == 1:
                            for g in range(G):
                                ve.wait_ge(yt_mm, it * G + g + 1)
                                ve.tensor_tensor(XY[:, g, 1], ident[:, :].unsqueeze(1).broadcast_to([P, GP, P]),
                                                 psXY[g][:, GP * P:].rearrange("p (h t) -> p h t", h=GP),
                                                 ALU.subtract).then_inc(xy_ok, 1)
                        if l >= 2:
                            for g in range(G):
                                invert(it, l - 1, g)
                    for g in range(G):
                        invert(it, NINV, g)
                    for hp in range(HP):
                        ve.wait_ge(s_mm, it + 1)
                        s_b = state[:, bass.ds(b, 1), hp, :].squeeze(1)
                        ve.scalar_tensor_tensor(s_b, s_b, T2[LEVELS][:, hp, 0, :], psR[:, hp * DV:(hp + 1) * DV],
                                                ALU.mult, ALU.add).then_inc(s_ok, 1)
                    ve.wait_ge(rr_ok, it + 1)
                    ve.wait_ge(yout_mm, it)
                    ve.tensor_tensor(On, psO[:, :].rearrange("p (a n) -> p a n", a=HP),
                                     ms[:, 1, :].unsqueeze(2).broadcast_to([P, HP, DV]), ALU.mult).then_inc(on_ok, 1)

                psLv = [t[:, :].rearrange("p (a x t) -> p a x t", a=HP, x=2) for t in psL]
                rounds(ve, body)

            @block.tensor
            def _(pe):
                pe.wait_ge(zeroed, 6)

                def level(it, l):
                    pe.wait_ge(kq_ok, it * NKQ + l + 1)
                    pe.wait_ge(ks_ok, it * NKS + l + 2)
                    pe.wait_ge(aq_ok, it * NKQ + l) if l >= 2 else pe.wait_ge(aq_ok, it * NKQ)
                    for hp in range(HP):
                        last = pe.matmul(psL[l % 2][:, hp * P:(hp + 1) * P],
                                         KS[:, hp].rearrange("p x t -> p (x t)"), KQ[:, :, hp, :],
                                         start=True, stop=True)
                    last.then_inc(lvl_mm, 1)

                def transpose_e(it):
                    pe.wait_ge(e_ok, it * LEVELS + 1)
                    pe.wait_ge(xy_ok, it * G * LEVELS)
                    for g in range(G):
                        for h in range(GP):
                            last = pe.matmul(psXY[g][:, (GP + h) * P:(GP + h + 1) * P], E[:, 0, g * GP + h, :],
                                             ident[:, :], start=True, stop=True)
                        last.then_inc(yt_mm, 1)

                def double(it, l):
                    for g in range(G):
                        pe.wait_ge(e_ok, it * LEVELS + l + 1)
                        pe.wait_ge(x_init, it + 1)
                        pe.wait_ge(xy_ok, it * G * LEVELS + G * (l - 1) + g + 1)
                        if l == 1:
                            pe.wait_ge(ksn_ok, it)
                            pe.wait_ge(aq_ok, it * NKQ + 1)
                        for h in range(GP):
                            last = pe.matmul(psZ[g][:, h * P:(h + 1) * P], E[:, l % NE, g * GP + h, :],
                                             XY[:, g, 1, h, :], start=True, stop=True)
                        last.then_inc(z_mm, 1)
                    for g in range(G):
                        pe.wait_ge(z_ok, it * G * NINV + G * (l - 1) + g + 1)
                        for h in range(GP):
                            last = pe.matmul(psXY[g][:, h * P:(h + 1) * P], Z[:, g, h, :],
                                             XY[:, g, 0, h, :], start=True, stop=True)
                            if l < NINV:
                                last = pe.matmul(psXY[g][:, (GP + h) * P:(GP + h + 1) * P], XY[:, g, 0, h, :],
                                                 Z[:, g, h, :], start=True, stop=True)
                        last.then_inc(dxy_mm, 1)

                def body(it, b, tok):
                    level(it, 0)
                    pe.wait_ge(yout_ok, it * 2)
                    for hp in range(HP):
                        last = pe.matmul(psZ[1][:, hp * C:(hp + 1) * C], KS[:, hp].rearrange("p x t -> p (x t)"),
                                         qT[:, hp, tok], start=True, stop=True)
                    last.then_inc(diag_mm, 1)
                    level(it, 1)
                    transpose_e(it)
                    for l in range(2, LEVELS):
                        level(it, l)
                        double(it, l - 1)
                    pe.wait_ge(hc_ok, it + 1)
                    pe.wait_ge(s_ok, it * HP)
                    for par in range(2):
                        pe.matmul(psR[C * par:C * par + C, :], hc, wv_sb[:, :, par, :], start=True, stop=False,
                                  skip_group_check=True)
                    pe.wait_ge(kpn_ok, it * 2 + 2)
                    for hp in range(HP):
                        last = pe.matmul(psR[:, hp * DV:(hp + 1) * DV], KPn[:, hp].rearrange("p x t -> p (x t)"),
                                         state[:, bass.ds(b, 1), hp, :].squeeze(1), start=False, stop=True,
                                         skip_group_check=True)
                    last.then_inc(res_mm, 1)
                    double(it, NINV)
                    pe.wait_ge(ks_ok, (it + 1) * NKS)
                    pe.wait_ge(z_ok, (it + 1) * G * NINV)
                    for hp in range(HP):
                        last = pe.transpose(psZ[0][:, hp * P:(hp + 1) * P], KS[:, hp].rearrange("p x t -> p (x t)"),
                                            ident[:, :])
                    last.then_inc(ksn_mm, 1)
                    pe.wait_ge(res_ok, it + 1)
                    pe.wait_ge(xy_ok, (it + 1) * G * LEVELS)
                    for hp in range(HP):
                        last = pe.matmul(psR[:, hp * DV:(hp + 1) * DV], XY[:, hp // GP, 0, hp % GP, :], res[:, hp, :],
                                         start=True, stop=True)
                    last.then_inc(u_mm, 1)
                    pe.wait_ge(qpb_ok, it * 2 + 2)
                    pe.wait_ge(on_ok, it)
                    pe.wait_ge(aq_ok, (it + 1) * NKQ)
                    pe.wait_ge(u_ok, it + 1)
                    for hp in range(HP):
                        pe.matmul(psO[:, hp * DV:(hp + 1) * DV], QPb[:, hp].rearrange("p x t -> p (x t)"),
                                  state[:, bass.ds(b, 1), hp, :].squeeze(1), start=True, stop=False)
                        last = pe.matmul(psO[:, hp * DV:(hp + 1) * DV], AQ[:, hp].rearrange("p x t -> p (x t)"),
                                         U[:, hp, :], start=False, stop=True)
                    last.then_inc(o_mm, 1)
                    pe.wait_ge(ksn_ok, it + 1)
                    for hp in range(HP):
                        last = pe.matmul(psR[:, hp * DV:(hp + 1) * DV], KSn[:, hp, :], U[:, hp, :],
                                         start=True, stop=True)
                    last.then_inc(s_mm, 1)
                    pe.wait_ge(on_ok, it + 1)
                    for hp in range(HP):
                        last = pe.transpose(psZ[1][:, hp * P:(hp + 1) * P], On[:, hp, :], ident[:, :])
                    last.then_inc(yout_mm, 1)

                rounds(pe, body)

            @block.scalar
            def _(ac):
                ac.wait_ge(zeroed, 6)

                def copy_z(it, l):
                    for g in range(G):
                        ac.wait_ge(z_mm, it * G * NINV + G * (l - 1) + g + 1)
                        ac.wait_ge(dxy_mm, it * G * NINV + G * (l - 2) + g + 1) if l >= 2 else \
                            ac.wait_ge(dxy_mm, it * G * NINV)
                        ac.copy(Z[:, g], psZ[g][:, 0:GP * P].rearrange("p (h t) -> p h t", h=GP)).then_inc(z_ok, 1)

                def body(it, b, tok):
                    ac.wait_ge(res_mm, it)
                    ac.copy(hc, hT[:, tok]).then_inc(hc_ok, 1)
                    for l in range(1, NINV):
                        copy_z(it, l)
                    ac.wait_ge(kq_ok, (it + 1) * NKQ)
                    ac.wait_ge(o_mm, it)
                    for par in range(2):
                        rows = slice(C * par, C * par + C)
                        ac.mul(KPn[rows, :, par, :], KQ[rows, 0], -1.0).then_inc(kpn_ok, 1)
                    for par in range(2):
                        rows = slice(C * par, C * par + C)
                        ac.copy(QPb[rows, :, par, :], KQ[rows, 1]).then_inc(qpb_ok, 1)
                    ac.wait_ge(res_mm, it + 1)
                    ac.wait_ge(u_mm, it)
                    ac.copy(res, psR[:, :].rearrange("p (a n) -> p a n", a=HP)).then_inc(res_ok, 1)
                    copy_z(it, NINV)
                    ac.wait_ge(ksn_mm, it + 1)
                    ac.wait_ge(s_mm, it)
                    ac.copy(KSn, psZ[0][:, :].rearrange("p (a n) -> p a n", a=HP)).then_inc(ksn_ok, 1)
                    ac.wait_ge(u_mm, it + 1)
                    ac.copy(U, psR[:, :].rearrange("p (a n) -> p a n", a=HP)).then_inc(u_ok, 1)
                    ac.wait_ge(o_mm, it + 1)
                    ac.wait_ge(rr_ok, it)
                    for hp in range(HP):
                        last = ac.activation(res[:, hp, :], psO[:, hp * DV:(hp + 1) * DV], ACT.Square,
                                             scale=DV ** -0.5, accum_out=ms[:, 0, hp:hp + 1])
                    last.then_inc(o_sq, 1)
                    ac.wait_ge(yout_mm, it + 1)
                    for par, dst in enumerate((qT, kT)):
                        ac.copy(dst[:, :, tok], psZ[1][:, :].rearrange("p (a x t) -> p a x t", a=HP, x=2)[:, :, par, :])\
                            .then_inc(yout_ok, 1)

                rounds(ac, body)

        late = gates[:, :, :, :].rearrange("p g a t -> p (g a t)")
        late_at, used[0] = [0], 0

        def late_region(shape):
            return region(shape, late, late_at)

        wff1_sb = late_region([FT * P])
        wff3_sb = late_region([FT * P])
        wff2_sb = late_region([FT, D])
        Wq_sb = late_region([XP, P])
        Wk_sb = late_region([XP, P])
        Wv_sb = late_region([XP * P])
        Wo_sb = late_region([XP, D])
        N0 = k0.shape[1]
        F2 = N0 // P
        w0_sb = late_region([2, N0])
        w1_sb = late_region([F2, k1.shape[1]])
        w2_sb = late_region([F2, D])
        k0_sb = late_region([2 * N0 // 4]).bitcast(U8).rearrange("p (a n) -> p a n", a=2)
        k1_sb = late_region([F2 * k1.shape[1] // 4]).bitcast(U8).rearrange("p (a n) -> p a n", a=F2)
        k2_sb = late_region([F2 * D // 4]).bitcast(U8).rearrange("p (a n) -> p a n", a=F2)
        Q2 = late_region([XP, T])
        XO = Q2
        ctx_sb = region([B, D])[0:S]
        ctxT = region([B, S])
        cb = region([S])
        KB = region([XP, 2, S])
        VB = region([XH * DK])[0:S]
        PR = region([XH, S])
        PT = region([XH, P])[0:S]
        FH = hT[:, :].rearrange("p (f t) -> p f t", f=FT)
        smx = region([3, XH])
        m = [region([T]) for _ in range(7)]
        H1 = Q2[:, 0:F2]
        H2 = Q2[:, F2:2 * F2]
        s0x2 = region([1])
        s1x2 = region([1])
        epsr, epsl = 1e-6, 1e-5
        NP3 = [(0, 3), (3, 3), (6, 2)]
        NTB = T // P

        tw = sem("tail_w")
        ctx_ld = sem("ctx_ld")
        signs = sem("signs")
        ctx_mm, ctx_ok = sem("ctx_mm"), sem("ctx_ok")
        kb_zero = sem("kb_zero")
        row_done = sem("row_done")
        stored = sem("stored")
        at_mm, u1_mm, u1_sig, u1_ok = sem("at_mm"), sem("u1_mm"), sem("u1_sig"), sem("u1_ok")
        u2_mm, gate_ok, gated, y1_ok = sem("u2_mm"), sem("gate_ok"), sem("gated"), sem("y1_ok")
        n_sq, n_mm, n_rt, n_inv = sem("n_sq"), sem("n_mm"), sem("n_rt"), sem("n_inv")
        n_cen, n_out, mean_mm = sem("n_cen"), sem("n_out"), sem("mean_mm")
        ff_mm, ff_sig, ff_mul, ff_ok = sem("ff_mm"), sem("ff_sig"), sem("ff_mul"), sem("ff_ok")
        ff2_mm, y2_ok, x1_ok = sem("ff2_mm"), sem("y2_ok"), sem("x1_ok")
        q2_mm, q2_ok = sem("q2_mm"), sem("q2_ok")
        cb_ok, kb_mm, kb_ok, vb_mm, vb_ok = sem("cb_ok"), sem("kb_mm"), sem("kb_ok"), sem("vb_mm"), sem("vb_ok")
        sc_mm, mx_ok, sub_ok, exp_ok = sem("sc_mm"), sem("mx_ok"), sem("sub_ok"), sem("exp_ok")
        sum_ok, inv_ok, pr_ok = sem("sum_ok"), sem("inv_ok"), sem("pr_ok")
        pt_mm, pt_a, pt_v, pv_mm, xo_ok = sem("pt_mm"), sem("pt_a"), sem("pt_v"), sem("pv_mm"), sem("xo_ok")
        wo_mm, wo_ok, ln_sc, x2_ok = sem("wo_mm"), sem("wo_ok"), sem("ln_sc"), sem("x2_ok")
        h1_mm, h1_ok, h2_mm, h2_ok = sem("h1_mm"), sem("h1_ok"), sem("h2_mm"), sem("h2_ok")
        h3_mm, y_ok, yt2_mm = sem("h3_mm"), sem("y_ok"), sem("yt2_mm")
        NORMS = 4
        CEN = 3

        TW_FF, TW_Q, TW_K, TW_V, TW_O, TW_SIGN = 16 * 3, 16 * 4, 16 * 5, 16 * 6, 16 * 7, 16 * 10

        with nc.Block() as block:
            @block.sync
            def _(sp):
                sp.dma_start(ctx_sb, ctx_in.rearrange("b s d -> s b d")).then_inc(ctx_ld, 16)
                for dst, src in ((wff1_sb, w_ff1), (wff3_sb, w_ff3),
                                 (wff2_sb, w_ff2.rearrange("(a p) d -> p a d", p=P)),
                                 (Wq_sb, Wq.rearrange("d (a n) -> d a n", a=XP)),
                                 (Wk_sb, Wk.rearrange("d (a n) -> d a n", a=XP)), (Wv_sb, Wv),
                                 (Wo_sb, Wo.rearrange("(a p) d -> p a d", p=P)),
                                 (k0_sb, k0.rearrange("(a p) n -> p a n", p=P)),
                                 (k1_sb, k1.rearrange("(a p) n -> p a n", p=P)),
                                 (k2_sb, k2.rearrange("(a p) n -> p a n", p=P))):
                    sp.dma_start(dst, src).then_inc(tw, 16)
                out_v = out.rearrange("b t d -> (b t) d").rearrange("(b n p) d -> b p n d", p=P, n=NTB)
                with sp.Fori(0, B) as b:
                    sp.wait_ge(row_done, b + 1)
                    sp.dma_start(out_v[bass.ds(b, 1)].squeeze(0), m[6].rearrange("p (n d) -> p n d", n=NTB))\
                        .then_inc(stored, 16)
                sp.wait_ge(stored, 16 * B)

            @block.gpsimd
            def _(gp):
                gp.memset(KB, 0.0).then_inc(kb_zero, 1)
                gp.wait_ge(tw, TW_SIGN)
                gp.tensor_scalar(w0_sb, k0_sb, 2.0, -1.0, ALU.mult, ALU.add).then_inc(signs, 1)
                gp.tensor_scalar(w1_sb, k1_sb, 2.0, -1.0, ALU.mult, ALU.add).then_inc(signs, 1)
                gp.tensor_scalar(w2_sb, k2_sb, 2.0, -1.0, ALU.mult, ALU.add).then_inc(signs, 1)
                gp.wait_ge(signs, 3)
                gp.tensor_tensor(w0_sb[:, 0], w0_sb[:, 0], w0_sb[:, 1], ALU.subtract).then_inc(signs, 1)
                gp.tensor_scalar(s0x2, v("s0"), 2.0, None, ALU.mult).then_inc(signs, 1)
                gp.tensor_scalar(s1x2, v("s1"), 2.0, None, ALU.mult).then_inc(signs, 1)
                with gp.Fori(0, B) as b:
                    for n in range(NTB):
                        i = b * NTB + n
                        gp.wait_ge(inv_ok, i + 1)
                        gp.tensor_tensor(PR, PR, smx[:, 2, :].unsqueeze(2).broadcast_to([P, XH, S]), ALU.mult)\
                            .then_inc(pr_ok, 1)

            @block.tensor
            def _(pe):
                pe.wait_ge(ctx_ld, 16)
                for j in range(B):
                    last = pe.transpose(bank[0][:, j * S:(j + 1) * S], ctx_sb[:, j, :], ident[0:S, 0:S])
                last.then_inc(ctx_mm, 1)
                pe.wait_ge(ctx_ok, 1)

                def mean_square(b, k):
                    pe.wait_ge(n_sq, b * NORMS + k + 1)
                    pe.matmul(bank[3][:, :], mean_w[:, :], m[1], start=True, stop=True).then_inc(n_mm, 1)

                def mean(src, centred):
                    pe.matmul(bank[2][:, :], mean_w[:, :], src, start=True, stop=True).then_inc(centred, 1)

                with pe.Fori(0, B) as b:
                    tok = bass.ds(b * T, T)
                    pe.wait_ge(row_done, b)
                    pe.matmul(bank[1][0:R, :], wu1_sb[:, :], zT[:, tok], start=True, stop=True).then_inc(u1_mm, 1)
                    for h in range(2 * HP):
                        last = pe.matmul(bank[0][:, :], wout_sb[:, h, :], (qT, kT)[h % 2][:, h // 2, tok],
                                         start=h == 0, stop=h == 2 * HP - 1)
                    last.then_inc(at_mm, 1)
                    pe.wait_ge(u1_ok, b + 1)
                    pe.matmul(bank[1][:, :], wu2_sb[:, :], m[1][0:R], start=True, stop=True).then_inc(u2_mm, 1)
                    mean_square(b, 0)
                    pe.wait_ge(tw, TW_FF)
                    pe.wait_ge(n_out, b * NORMS + 1)
                    for f in range(FT):
                        if f >= 2:
                            pe.wait_ge(ff_ok, b * FT + f - 1)
                        for j, w in enumerate((wff1_sb, wff3_sb)):
                            last = pe.matmul(bank[4 + 2 * (f % 2) + j][:, :], w[:, f * P:(f + 1) * P], m[4],
                                             start=True, stop=True)
                        last.then_inc(ff_mm, 1)
                    for f in range(FT):
                        pe.wait_ge(ff_ok, b * FT + f + 1)
                        last = pe.matmul(bank[0][:, :], wff2_sb[:, f, :], FH[:, f, :], start=f == 0, stop=f == FT - 1)
                    last.then_inc(ff2_mm, 1)
                    pe.wait_ge(x1_ok, b + 1)
                    mean(m[4], mean_mm)
                    mean_square(b, 1)
                    pe.wait_ge(tw, TW_V)
                    for a in range(XP):
                        last = pe.matmul(bank[a // 4][:, (a % 4) * S:(a % 4 + 1) * S], Wk_sb[:, a, :],
                                         ctxT[:, bass.ds(b, 1), :].squeeze(1), start=True, stop=True)
                    last.then_inc(kb_mm, 1)
                    pe.wait_ge(n_out, b * NORMS + 2)
                    for a in range(XP):
                        if a >= 4:
                            pe.wait_ge(q2_ok, b * XP + a - 3)
                        pe.matmul(bank[4 + a % 4][:, :], Wq_sb[:, a, :], m[3], start=True, stop=True).then_inc(q2_mm, 1)
                    pe.wait_ge(cb_ok, b + 1)
                    for j in range(2):
                        last = pe.matmul(bank[2 + j][0:S, :], cb, Wv_sb[:, j * 512:(j + 1) * 512],
                                         start=True, stop=True)
                    last.then_inc(vb_mm, 1)
                    pe.wait_ge(kb_ok, b * 4 + 4)
                    pe.wait_ge(vb_ok, b * 2 + 2)
                    pe.wait_ge(q2_ok, (b + 1) * XP)

                    def scores(n):
                        pe.wait_ge(sub_ok, b * 3 * NTB + 3 * n)
                        for j, (a0, na) in enumerate(NP3):
                            for a in range(na):
                                last = pe.matmul(bank[4 + j][:, a * 2 * S:(a + 1) * 2 * S],
                                                 Q2[:, a0 + a, n * P:(n + 1) * P],
                                                 KB[:, a0 + a].rearrange("p x s -> p (x s)"), start=True, stop=True)
                            last.then_inc(sc_mm, 1)

                    scores(0)
                    for n in range(NTB):
                        i = b * NTB + n
                        pe.wait_ge(pr_ok, i + 1)
                        for q in range(4):
                            if q == 0:
                                pe.wait_ge(pt_v, i * 2)
                                pe.wait_ge(pt_a, i * 2)
                            elif q == 3:
                                pe.wait_ge(pt_a, i * 2 + 1)
                            for h in range(4):
                                last = pe.transpose(bank[q % 3][0:S, h * P:(h + 1) * P], PR[:, 4 * q + h, :], ident[:, :])
                            last.then_inc(pt_mm, 1)
                        if n + 1 < NTB:
                            scores(n + 1)
                        pe.wait_ge(pt_a, i * 2 + 2)
                        pe.wait_ge(pt_v, i * 2 + 2)
                        pe.wait_ge(xo_ok, i * 2)
                        for h in range(XH):
                            a, par = h // 2, h % 2
                            last = pe.matmul((bank[3], bank[7])[a // 4][DK * par:DK * par + DK, (a % 4) * P:(a % 4 + 1) * P],
                                             VB[:, h * DK:(h + 1) * DK], PT[:, h, :], start=True, stop=True)
                        last.then_inc(pv_mm, 1)
                    pe.wait_ge(xo_ok, (b + 1) * 2 * NTB)
                    for a in range(XP):
                        last = pe.matmul(bank[0][:, :], Wo_sb[:, a, :], XO[:, a, :], start=a == 0, stop=a == XP - 1)
                    last.then_inc(wo_mm, 1)
                    pe.wait_ge(wo_ok, b + 1)
                    mean(m[5], mean_mm)
                    mean_square(b, 2)
                    pe.wait_ge(x2_ok, b + 1)
                    mean(m[4], mean_mm)
                    mean_square(b, 3)
                    pe.wait_ge(signs, 6)
                    pe.wait_ge(n_out, b * NORMS + 4)
                    for f in range(F2):
                        pe.matmul(bank[4 + f][:, :], w0_sb[:, 0, f * P:(f + 1) * P], m[3], start=True, stop=True)\
                            .then_inc(h1_mm, 1)
                    pe.wait_ge(h1_ok, (b + 1) * F2)
                    for f in range(F2):
                        for a in range(F2):
                            last = pe.matmul(bank[f][:, :], w1_sb[:, a, f * P:(f + 1) * P], H1[:, a, :],
                                             start=a == 0, stop=a == F2 - 1)
                        last.then_inc(h2_mm, 1)
                    for a in range(F2):
                        pe.wait_ge(h2_ok, b * F2 + a + 1)
                        last = pe.matmul(bank[4][:, :], w2_sb[:, a, :], H2[:, a, :], start=a == 0, stop=a == F2 - 1)
                    last.then_inc(h3_mm, 1)
                    pe.wait_ge(y_ok, b + 1)
                    for n in range(NTB):
                        last = pe.transpose(bank[5][:, n * P:(n + 1) * P], m[5][:, n * P:(n + 1) * P], ident[:, :])
                    last.then_inc(yt2_mm, 1)

            @block.scalar
            def _(ac):
                ac.wait_ge(ctx_mm, 1)
                ac.copy(ctxT, bank[0][:, 0:B * S].rearrange("p (b s) -> p b s", b=B)).then_inc(ctx_ok, 1)
                ac.wait_ge(kb_zero, 1)
                ac.wait_ge(ctx_ok, 1)
                ac.wait_ge(signs, 6)

                def root(b, k, eps):
                    ac.wait_ge(n_mm, b * NORMS + k + 1)
                    ac.activation(m[2], bank[3][:, :], ACT.Sqrt, bias=eps).then_inc(n_rt, 1)

                def square(b, k, src):
                    ac.activation(m[1], src, ACT.Square).then_inc(n_sq, 1)

                with ac.Fori(0, B) as b:
                    ac.wait_ge(row_done, b)
                    ac.wait_ge(u1_mm, b + 1)
                    ac.activation(m[0][0:R], bank[1][0:R, :], ACT.Sigmoid, bias=v("b_u1", 0, R)).then_inc(u1_sig, 1)
                    ac.wait_ge(u2_mm, b + 1)
                    ac.activation(m[2], bank[1][:, :], ACT.Sigmoid, bias=v("b_u2")).then_inc(gate_ok, 1)
                    ac.wait_ge(y1_ok, b + 1)
                    square(b, 0, m[3])
                    root(b, 0, epsr)
                    for f in range(FT):
                        if f == 1:
                            ac.wait_ge(stored, b * 16)
                        ac.wait_ge(ff_mm, b * FT + f + 1)
                        if f >= 2:
                            ac.wait_ge(ff_ok, b * FT + f - 1)
                        ac.activation(m[5 + f % 2], bank[4 + 2 * (f % 2)][:, :], ACT.Sigmoid).then_inc(ff_sig, 1)
                    ac.wait_ge(n_cen, b * CEN + 1)
                    square(b, 1, m[0])
                    root(b, 1, epsl)
                    ac.wait_ge(kb_mm, b + 1)
                    for j in range(2):
                        for par in range(2):
                            rows = slice(DK * par, DK * par + DK)
                            for a in range(4):
                                last = ac.activation(KB[rows, 4 * j + a, par, :],
                                                     bank[j][rows, a * S:(a + 1) * S], ACT.Identity,
                                                     bias=vec[rows, VEC["bk"][0] + 4 * j + a:VEC["bk"][0] + 4 * j + a + 1])
                            last.then_inc(kb_ok, 1)
                    ac.copy(cb, ctxT[:, bass.ds(b, 1), :].squeeze(1)).then_inc(cb_ok, 1)
                    for a in range(XP):
                        ac.wait_ge(q2_mm, b * XP + a + 1)
                        ac.activation(Q2[:, a, :], bank[4 + a % 4][:, :], ACT.Identity, bias=v("bq", a)).then_inc(q2_ok, 1)
                    ac.wait_ge(vb_mm, b + 1)
                    for j in range(2):
                        ac.copy(VB[:, j * 512:(j + 1) * 512], bank[2 + j][0:S, :]).then_inc(vb_ok, 1)
                    for n in range(NTB):
                        i = b * NTB + n
                        ac.wait_ge(sub_ok, i * 3 + 3)
                        ac.activation(PR, PR, ACT.Exp, scale=DK ** -0.5).then_inc(exp_ok, 1)
                        ac.wait_ge(pv_mm, i)
                        for q in (0, 2):
                            ac.wait_ge(pt_mm, i * 4 + q + 1)
                            ac.copy(PT[:, 4 * q:4 * q + 4, :], bank[q % 3][0:S, :].rearrange("p (h t) -> p h t", h=4))\
                                .then_inc(pt_a, 1)
                        ac.wait_ge(pv_mm, i + 1)
                        for j in range(2):
                            for a in range(4):
                                last = ac.activation(XO[:, 4 * j + a, n * P:(n + 1) * P],
                                                     (bank[3], bank[7])[j][:, a * P:(a + 1) * P], ACT.Identity,
                                                     bias=v("bv", 4 * j + a))
                            last.then_inc(xo_ok, 1)
                    ac.wait_ge(n_cen, b * CEN + 2)
                    square(b, 2, m[0])
                    root(b, 2, epsl)
                    ac.wait_ge(n_cen, b * CEN + 3)
                    square(b, 3, m[0])
                    root(b, 3, epsl)
                    for f in range(F2):
                        ac.wait_ge(h1_mm, b * F2 + f + 1)
                        ac.activation(H1[:, f, :], bank[4 + f][:, :], ACT.Relu, scale=s0x2).then_inc(h1_ok, 1)
                    for f in range(F2):
                        ac.wait_ge(h2_mm, b * F2 + f + 1)
                        ac.activation(H2[:, f, :], bank[f][:, :], ACT.Relu, scale=s1x2).then_inc(h2_ok, 1)
                    ac.wait_ge(yt2_mm, b + 1)
                    ac.copy(m[6], bank[5][:, :]).then_inc(row_done, 1)

            @block.vector
            def _(ve):
                def invert(b, k):
                    ve.wait_ge(n_rt, b * NORMS + k + 1)
                    ve.reciprocal(m[2], m[2]).then_inc(n_inv, 1)
                    ve.wait_ge(n_inv, b * NORMS + k + 1)

                def centre(b, k, src):
                    ve.wait_ge(mean_mm, b * CEN + k + 1)
                    ve.tensor_tensor(m[0], src, bank[2][:, :], ALU.subtract).then_inc(n_cen, 1)

                with ve.Fori(0, B) as b:
                    tok = bass.ds(b * T, T)
                    ve.wait_ge(u1_sig, b + 1)
                    ve.scalar_tensor_tensor(m[1][0:R], bank[1][0:R, :], v("b_u1", 0, R), m[0][0:R],
                                            ALU.add, ALU.mult).then_inc(u1_ok, 1)
                    ve.wait_ge(gate_ok, b + 1)
                    ve.wait_ge(at_mm, b + 1)
                    ve.tensor_tensor(m[2], m[2], bank[0][:, :], ALU.mult).then_inc(gated, 1)
                    ve.wait_ge(gated, b + 1)
                    ve.tensor_tensor(m[3], m[2], zT[:, tok], ALU.add).then_inc(y1_ok, 1)
                    invert(b, 0)
                    ve.scalar_tensor_tensor(m[4], m[3], v("w_ffn"), m[2], ALU.mult, ALU.mult).then_inc(n_out, 1)
                    for f in range(FT):
                        g = m[5 + f % 2]
                        ve.wait_ge(ff_sig, b * FT + f + 1)
                        ve.tensor_tensor(g, g, bank[4 + 2 * (f % 2)][:, :], ALU.mult).then_inc(ff_mul, 1)
                        ve.wait_ge(ff_mul, b * FT + f + 1)
                        ve.tensor_tensor(FH[:, f, :], g, bank[5 + 2 * (f % 2)][:, :], ALU.mult).then_inc(ff_ok, 1)
                    ve.wait_ge(ff2_mm, b + 1)
                    ve.tensor_tensor(m[3], m[3], bank[0][:, :], ALU.add).then_inc(y2_ok, 1)
                    ve.wait_ge(y2_ok, b + 1)
                    ve.tensor_tensor(m[4], m[3], xT[:, tok], ALU.add).then_inc(x1_ok, 1)
                    ve.wait_ge(x1_ok, b + 1)
                    centre(b, 0, m[4])
                    invert(b, 1)
                    ve.tensor_tensor(m[3], m[0], m[2], ALU.mult).then_inc(n_out, 1)
                    for n in range(NTB):
                        i = b * NTB + n
                        ve.wait_ge(pt_mm, i * 4)
                        for j, (a0, na) in enumerate(NP3):
                            heads = slice(2 * a0, 2 * (a0 + na))
                            ps = bank[4 + j][:, 0:2 * na * S].rearrange("p (h s) -> p h s", s=S)
                            ve.wait_ge(sc_mm, i * 3 + j + 1)
                            ve.tensor_reduce(smx[:, 0, heads], ps, AX.X, ALU.max).then_inc(mx_ok, 1)
                            ve.wait_ge(mx_ok, i * 3 + j + 1)
                            ve.tensor_tensor(PR[:, heads, :], ps,
                                             smx[:, 0, heads].unsqueeze(2).broadcast_to([P, 2 * na, S]),
                                             ALU.subtract).then_inc(sub_ok, 1)
                        ve.wait_ge(exp_ok, i + 1)
                        ve.tensor_reduce(smx[:, 1, :], PR, AX.X, ALU.add).then_inc(sum_ok, 1)
                        ve.wait_ge(sum_ok, i + 1)
                        ve.reciprocal(smx[:, 2, :], smx[:, 1, :]).then_inc(inv_ok, 1)
                        ve.wait_ge(pv_mm, i)
                        for q in (1, 3):
                            ve.wait_ge(pt_mm, i * 4 + q + 1)
                            ve.tensor_copy(PT[:, 4 * q:4 * q + 4, :],
                                           bank[q % 3][0:S, :].rearrange("p (h t) -> p h t", h=4)).then_inc(pt_v, 1)
                    ve.wait_ge(wo_mm, b + 1)
                    ve.scalar_tensor_tensor(m[5], bank[0][:, :], v("bo"), m[3], ALU.add, ALU.add).then_inc(wo_ok, 1)
                    ve.wait_ge(wo_ok, b + 1)
                    centre(b, 1, m[5])
                    invert(b, 2)
                    ve.tensor_tensor(m[3], m[0], m[2], ALU.mult).then_inc(n_out, 1)
                    ve.wait_ge(n_out, b * NORMS + 3)
                    ve.tensor_scalar(m[3], m[3], v("ln_gamma"), v("ln_beta"), ALU.mult, ALU.add).then_inc(ln_sc, 1)
                    ve.wait_ge(ln_sc, b + 1)
                    ve.tensor_tensor(m[4], m[4], m[3], ALU.add).then_inc(x2_ok, 1)
                    ve.wait_ge(x2_ok, b + 1)
                    centre(b, 2, m[4])
                    invert(b, 3)
                    ve.tensor_tensor(m[3], m[0], m[2], ALU.mult).then_inc(n_out, 1)
                    ve.wait_ge(h3_mm, b + 1)
                    ve.scalar_tensor_tensor(m[5], bank[4][:, :], v("s2"), m[4], ALU.mult, ALU.add).then_inc(y_ok, 1)


_OUT = "out_dram"


def pack_vectors(a, np):
    rows = {
        "conv_w": a["L0_attn_conv_w"], "conv_b": a["L0_attn_conv_b"][:, None],
        "w_norm": a["L0_attn_w_norm_in"][:, None], "b_ad": a["L0_attn_b_ad"].reshape(-1, P).T,
        "alpha_spike": a["L0_attn_alpha_spike"].reshape(-1, P).T,
        "beta_spike": a["L0_attn_beta_spike"].reshape(-1, P).T,
        "b_au": a["L0_attn_b_au"][:, None], "b_u1": a["L0_attn_b_u1"][:, None],
        "b_u2": a["L0_attn_b_u2"][:, None], "w_hn": a["L0_attn_w_hn"].T,
        "w_ffn": a["L0_attn_w_ffn"][:, None],
        "b_beta": np.repeat(a["L0_attn_b_beta"], 64).reshape(-1, P).T,
        "bq": a["L0_xattn_bq"].reshape(-1, P).T, "bk": a["L0_xattn_bk"].reshape(-1, P).T,
        "bv": a["L0_xattn_bv"].reshape(-1, P).T, "bo": a["L0_xattn_bo"][:, None],
        "ln_gamma": a["L0_xattn_ln_gamma"][:, None], "ln_beta": a["L0_xattn_ln_beta"][:, None],
        "s0": np.repeat(a["L0_ffn_s0"].reshape(1, 1), P, 0), "s1": np.repeat(a["L0_ffn_s1"].reshape(1, 1), P, 0),
        "s2": np.repeat(a["L0_ffn_s2"].reshape(1, 1), P, 0),
    }
    packed = np.zeros((P, NVEC), np.float32)
    for name, (at, n) in VEC.items():
        r = rows[name]
        packed[:r.shape[0], at:at + n] = r
    return packed


def kernel(**inputs):
    import numpy as np
    import concourse.bacc as bacc
    from concourse.bass_utils import run_bass_kernel_spmd

    a = {n: np.ascontiguousarray(t) for n, t in inputs.items()}
    arrays = {"x": a["x"], "ctx": a["ctx_1024"], "vec": pack_vectors(a, np)}
    for n in ("wq", "wk", "w_spike", "wv", "w_out", "w_au", "w_ad", "w_beta", "w_u1", "w_u2",
              "w_ff1", "w_ff3", "w_ff2"):
        arrays[n] = a["L0_attn_" + n]
    for n in ("Wq", "Wk", "Wv", "Wo"):
        arrays["x_" + n] = a["L0_xattn_" + n]
    for n in ("k0", "k1", "k2"):
        arrays[n] = a["L0_ffn_" + n]
    nc = bacc.Bacc("TRN2", target_bir_lowering=False, num_devices=1)
    arrays = {f"in_{n}_dram": t for n, t in arrays.items()}
    args = [nc.dram_tensor(n, t.shape, mybir.dt.from_np(t.dtype), kind="ExternalInput").ap()
            for n, t in arrays.items()]
    args.append(nc.dram_tensor(_OUT, a["x"].shape, F32, kind="ExternalOutput").ap())
    decoder_kernel(nc, *args)
    return run_bass_kernel_spmd(nc, [arrays], core_ids=[0]).results[0][_OUT]
```

```python
from contextlib import ExitStack

import concourse.bass as bass
from concourse import mybir

P = 128
F32 = mybir.dt.float32
U32 = mybir.dt.uint32
U8 = mybir.dt.uint8
ACT = mybir.ActivationFunctionType
ALU = mybir.AluOpType
AX = mybir.AxisListType

VEC = {}
_at = 0
for _name, _n in (("conv_w", 4), ("conv_b", 1), ("w_norm", 1), ("b_ad", 4), ("alpha_spike", 4),
                  ("beta_spike", 4), ("b_au", 1), ("b_u1", 1), ("b_u2", 1), ("w_hn", 8), ("w_ffn", 1),
                  ("b_beta", 4), ("bq", 8), ("bk", 8), ("bv", 8), ("bo", 1), ("ln_gamma", 1),
                  ("ln_beta", 1), ("s0", 1), ("s1", 1), ("s2", 1)):
    VEC[_name] = (_at, _n)
    _at += _n
NVEC = _at


def decoder_kernel(nc, x, ctx_in, vec_in, wq, wk, w_spike, wv, w_out, w_au, w_ad, w_beta, w_u1, w_u2,
                   w_ff1, w_ff3, w_ff2, Wq, Wk, Wv, Wo, k0, k1, k2, out):
    B, T, D = x.shape
    TOK = B * T
    NT = TOK // P
    DK, DV = 64, 128
    HP = wq.shape[1] // P
    C = 64
    NC = T // C
    LEVELS = 6
    R = w_au.shape[1]
    FT = w_ff1.shape[1] // P
    XP = Wq.shape[1] // P
    XH = 2 * XP
    S = ctx_in.shape[1]
    CTX = B * S
    assert D == P and 2 * DK == P and DV == P and T == 512 and HP == 4 and XP == 8

    ctx = ExitStack()
    with ctx:
        def sb(name, shape, dt=F32):
            return ctx.enter_context(nc.sbuf_tensor(name, shape, dt))

        def sem(name):
            return ctx.enter_context(nc.semaphore(name))

        bank = [ctx.enter_context(nc.psum_tensor(f"bank{i}", [P, 512], F32)) for i in range(8)]

        qT = sb("qT", [P, HP, TOK])
        kT = sb("kT", [P, HP, TOK])
        gates = sb("gates", [P, 2, HP, TOK])
        aT, bT = gates[:, 0], gates[:, 1]
        zT = sb("zT", [P, TOK])
        hT = sb("hT", [P, TOK])
        wv_sb = sb("wv_sb", [P, HP, 2, DV])
        wu1_sb = sb("wu1_sb", [P, R])
        wu2_sb = sb("wu2_sb", [R, D])
        ident = sb("ident", [P, P])
        bdones = sb("bdones", [P, P])
        mean_w = sb("mean_w", [P, P])
        mask = sb("mask", [P, LEVELS, P])
        vec = sb("vec", [P, NVEC])
        WORK = 13000
        work = sb("work", [P, WORK])
        used = [0]

        def region(shape, of=work, cursor=used):
            n = 1
            for s in shape:
                n *= s
            flat = of[:, cursor[0]:cursor[0] + n]
            cursor[0] += n
            assert cursor[0] <= of.shape[1], cursor
            names = "abcd"[:len(shape)]
            if len(shape) == 1:
                return flat
            sizes = {c: s for c, s in zip(names[1:], shape[1:])}
            return flat.rearrange(f"p ({' '.join(names)}) -> p {' '.join(names)}", **sizes)

        def v(name, i=0, rows=P):
            return vec[0:rows, VEC[name][0] + i:VEC[name][0] + i + 1]

        primed = [sem("sd_ok"), sem("au_ok"), sem("sq_ok"), sem("ss_mm"), sem("bc_ok"), sem("qk_ok"),
                  sem("nrm_inv"), sem("beta_ok"), sem("beta_mm"), sem("al0_ok"), sem("row_done"),
                  sem("sub_ok"), sem("pt_v"), sem("pt_a"), sem("xo_ok"), sem("stored"), sem("pv_mm"),
                  sem("pt_mm")]
        (sd_ok, au_ok, sq_ok, ss_mm, bc_ok, qk_ok, nrm_inv, beta_ok, beta_mm, al0_ok, row_done,
         sub_ok, pt_v, pt_a, xo_ok, stored, pv_mm, pt_mm) = primed

        def at(n):
            return n + 1

        used[0] = 0
        wq_sb = region([HP, P])
        wk_sb = region([HP, P])
        wsp_sb = region([HP, P])
        wad_sb = region([HP, P])[0:R]
        wau_sb = region([R])
        wbeta_sb = region([2 * HP])
        wbeta_rep = region([HP, 2, DK])
        bspike_bd = region([HP, P])
        auT = region([TOK])[0:R]
        early_end = used[0]
        PAD = 3
        h0T = region([B, T + PAD])
        xn = bT.rearrange("p a t -> p (a t)")[:, 0:TOK].rearrange("p (n d) -> p n d", n=NT)
        zn = bT.rearrange("p a t -> p (a t)")[:, TOK:2 * TOK].rearrange("p (n d) -> p n d", n=NT)
        hn = bT.rearrange("p a t -> p (a t)")[:, 2 * TOK:3 * TOK].rearrange("p (n d) -> p n d", n=NT)
        sqn = bT.rearrange("p a t -> p (a t)")[:, 3 * TOK:4 * TOK].rearrange("p (n d) -> p n d", n=NT)
        conv = xn.rearrange("p n d -> p (n d)").rearrange("p (b t) -> p b t", b=B)
        sig = sqn.rearrange("p n d -> p (n d)").rearrange("p (b t) -> p b t", b=B)
        mom = sb("mom", [P, 6, NT])
        half = sb("half", [P, NT])

        w_loaded = sem("w_loaded")
        x_loaded = sem("x_loaded")
        consts = sem("consts")
        setup = sem("setup")
        vn = sem("vn")
        pn = sem("pn")
        an = sem("an")
        tr_mm = sem("tr_mm")
        tr_out = sem("tr_out")
        conv_ok = sem("conv_ok")
        sig_ok = sem("sig_ok")
        h_ok = sem("h_ok")

        with nc.Block() as block:
            @block.sync
            def _(sp):
                sp.dma_start(xn, x.rearrange("b t d -> (b t) d").rearrange("(n p) d -> p n d", p=P))\
                    .then_inc(x_loaded, 16)
                sp.dma_start(vec[:, :], vec_in).then_inc(w_loaded, 16)
                for dst, src in ((wsp_sb, w_spike.rearrange("d (a n) -> d a n", a=HP)),
                                 (wq_sb, wq.rearrange("d (a n) -> d a n", a=HP)),
                                 (wk_sb, wk.rearrange("d (a n) -> d a n", a=HP)),
                                 (wau_sb, w_au), (wad_sb, w_ad.rearrange("d (a n) -> d a n", a=HP)),
                                 (wbeta_sb, w_beta),
                                 (wv_sb[:, :, :, :], wv.rearrange("d (a b n) -> d a b n", a=HP, b=2)),
                                 (wu1_sb[:, :], w_u1), (wu2_sb[:, :], w_u2)):
                    sp.dma_start(dst, src).then_inc(w_loaded, 16)

            @block.gpsimd
            def _(gp):
                for s in primed:
                    gp.sem_inc(s, 1)
                gp.memset(half[:, :], -0.5).then_inc(consts, 1)
                gp.memset(h0T[:, :, 0:PAD], 0.0).then_inc(consts, 1)
                gp.memset(mean_w[:, :], 1.0 / D).then_inc(consts, 1)
                gp.memset(ident[:, :], 0.0).then_inc(consts, 1)
                gp.memset(bdones[:, :], 1.0).then_inc(consts, 1)
                gp.memset(mask[:, :, :], 0.0).then_inc(consts, 1)
                gp.wait_ge(consts, 6)
                gp.affine_select(out=ident[:, :], in_=ident[:, :], compare_op=ALU.not_equal, fill=1.0,
                                 base=0, pattern=[[-1, P]], channel_multiplier=1).then_inc(consts, 1)

                def keep_block(t, step, n, width, size, done):
                    gp.affine_select(out=t, in_=t, compare_op=ALU.is_ge, fill=0.0, base=0,
                                     pattern=[[-step, n], [0, width]], channel_multiplier=1).then_inc(consts, 1)
                    gp.wait_ge(consts, done + 1)
                    gp.affine_select(out=t, in_=t, compare_op=ALU.is_ge, fill=0.0, base=size - 1,
                                     pattern=[[step, n], [0, width]], channel_multiplier=-1).then_inc(consts, 1)

                keep_block(bdones[:, :].rearrange("p (a t) -> p a t", a=2), C, 2, C, C, 7)
                done = 9
                for l in range(LEVELS):
                    L = 1 << l
                    late = mask[:, l, :].rearrange("p (j s t) -> p j s t", s=2, t=L)[:, :, 1, :]
                    gp.memset(late, 1.0).then_inc(consts, 1)
                    gp.wait_ge(consts, done + 1)
                    keep_block(late, 2 * L, P // (2 * L), L, L, done + 1)
                    done += 3
                for i, (src, dst) in enumerate(((1, 2), (3, 4))):
                    gp.wait_ge(vn, (4, 8)[i])
                    gp.tensor_tensor(mom[:, dst, :], mom[:, src, :], half[:, :], ALU.pow).then_inc(pn, 1)

            N_CONST = 9 + 3 * LEVELS

            @block.vector
            def _(ve):
                ve.wait_ge(x_loaded, 16)
                ve.tensor_reduce(mom[:, 0, :], xn, AX.X, ALU.add).then_inc(vn, 1)
                ve.wait_ge(vn, 1)
                ve.tensor_scalar(mom[:, 5, :], mom[:, 0, :], 1.0 / D, None, ALU.mult).then_inc(vn, 1)
                ve.wait_ge(vn, 2)
                ve.tensor_tensor(zn, xn, mom[:, 5, :].unsqueeze(2).broadcast_to([P, NT, D]),
                                 ALU.subtract).then_inc(vn, 1)
                ve.wait_ge(an, 1)
                ve.tensor_reduce(mom[:, 0, :], sqn, AX.X, ALU.add).then_inc(setup, 1)
                ve.wait_ge(setup, 1)
                ve.tensor_scalar(mom[:, 1, :], mom[:, 0, :], 1.0 / D, 1e-5, ALU.mult, ALU.add).then_inc(vn, 1)
                ve.wait_ge(pn, 1)
                ve.tensor_tensor(zn, zn, mom[:, 2, :].unsqueeze(2).broadcast_to([P, NT, D]),
                                 ALU.mult).then_inc(vn, 1)
                ve.wait_ge(vn, 5)
                ve.tensor_tensor(sqn, zn, zn, ALU.mult).then_inc(vn, 1)
                ve.wait_ge(vn, 6)
                ve.tensor_reduce(mom[:, 0, :], sqn, AX.X, ALU.add).then_inc(vn, 1)
                ve.wait_ge(vn, 7)
                ve.tensor_scalar(mom[:, 3, :], mom[:, 0, :], 1.0 / D, 1e-6, ALU.mult, ALU.add).then_inc(vn, 1)
                ve.wait_ge(pn, 2)
                ve.tensor_tensor(hn, zn, mom[:, 4, :].unsqueeze(2).broadcast_to([P, NT, D]),
                                 ALU.mult).then_inc(vn, 1)
                for n in range(NT // 4):
                    ve.wait_ge(tr_mm, n + 1)
                    ve.tensor_copy(zT[:, n * 512:(n + 1) * 512], bank[n][:, :])
                ve.wait_ge(tr_out, NT // 4)
                ve.wait_ge(w_loaded, 16 * 10)
                ve.tensor_scalar(conv, h0T[:, :, 0:T], v("conv_w", 0), v("conv_b"), ALU.mult, ALU.add)\
                    .then_inc(conv_ok, 1)
                for j in range(1, PAD + 1):
                    ve.wait_ge(conv_ok, j)
                    ve.scalar_tensor_tensor(conv, h0T[:, :, j:j + T], v("conv_w", j), conv, ALU.mult, ALU.add)\
                        .then_inc(conv_ok, 1)
                for b in range(B):
                    ve.wait_ge(sig_ok, b + 1)
                    ve.tensor_tensor(hT[:, b * T:(b + 1) * T], conv[:, b], sig[:, b], ALU.mult).then_inc(h_ok, 1)
                ve.tensor_copy(wbeta_rep, wbeta_sb.rearrange("p (a b) -> p a b", b=2).unsqueeze(3)
                               .broadcast_to([P, HP, 2, DK])).then_inc(setup, 1)
                for hp in range(HP):
                    ve.tensor_scalar(bspike_bd[:, hp, :], bdones[:, :], v("beta_spike", hp), None, ALU.mult)\
                        .then_inc(setup, 1)

            @block.scalar
            def _(ac):
                ac.wait_ge(vn, 3)
                ac.activation(sqn, zn, ACT.Square).then_inc(an, 1)
                ac.wait_ge(w_loaded, 16 * 10)
                ac.wait_ge(consts, 2)
                for b in range(B):
                    ac.wait_ge(tr_mm, NT // 4 + b + 1)
                    ac.activation(h0T[:, b, PAD:], bank[4 + b][:, :], ACT.Copy, scale=v("w_norm")).then_inc(tr_out, 1)
                ac.wait_ge(conv_ok, PAD + 1)
                for b in range(B):
                    ac.activation(sig[:, b], conv[:, b], ACT.Sigmoid).then_inc(sig_ok, 1)

            @block.tensor
            def _(pe):
                pe.wait_ge(consts, N_CONST)
                pe.wait_ge(x_loaded, 16)
                for k, (src, ready) in enumerate(((zn, 5), (hn, 9))):
                    pe.wait_ge(vn, ready)
                    for n in range(NT // 4):
                        for j in range(4):
                            last = pe.transpose(bank[4 * k + n][:, j * P:(j + 1) * P],
                                                src[:, 4 * n + j, :], ident[:, :])
                        last.then_inc(tr_mm, 1)

        sd_mm = sem("sd_mm")

        with nc.Block() as block:
            @block.tensor
            def _(pe):
                with pe.Fori(0, B) as b:
                    for hp in range(HP):
                        pe.wait_ge(sd_ok, at(b * HP + hp))
                        pe.matmul(bank[hp][:, :], wsp_sb[:, hp, :], hT[:, bass.ds(b * T, T)],
                                  start=True, stop=True).then_inc(sd_mm, 1)

            @block.scalar
            def _(ac):
                with ac.Fori(0, B) as b:
                    for hp in range(HP):
                        ac.wait_ge(sd_mm, b * HP + hp + 1)
                        ac.mul(aT[:, hp, bass.ds(b * T, T)], bank[hp][:, :], 2.0).then_inc(sd_ok, 1)

        used[0] = early_end
        NQK = 2 * HP
        sq_buf = region([2, T])
        inv_bc = region([2, T])
        nrm = region([T])[0:2 * NQK]
        nrm_e = region([T])[0:2 * NQK]
        au_sig = region([T])[0:R]
        pick = region([NQK, 2 * NQK])
        spread = region([NQK, P])[0:2 * NQK]
        neg_mem = mom[:, 0:2, :].rearrange("p a n -> p (a n)")[:, 0:HP * B]
        mem = aT.rearrange("p a (b t) -> p (a b) t", b=B)
        STEPS = 64

        mconst = sem("mconst")
        au_mm, au_sg = sem("au_mm"), sem("au_sg")
        qk_mm, raw_ok = sem("qk_mm"), sem("raw_ok")
        nrm_ok, nrm_add = sem("nrm_ok"), sem("nrm_add")
        bc_mm = sem("bc_mm")
        charged = sem("charged")
        fired = sem("fired")

        def qk_dst(j, tok):
            return (qT if j < HP else kT)[:, j % HP, tok]

        with nc.Block() as block:
            @block.vector
            def _(ve):
                ve.memset(neg_mem, 0.0).then_inc(fired, 1)
                with ve.Fori(0, B) as b:
                    with ve.Fori(0, T // B // STEPS) as r:
                        done = (b * (T // B // STEPS) + r) * STEPS
                        for j in range(STEPS):
                            now = mem[:, :, bass.ds(done + j, 1)].squeeze(2)
                            ve.wait_ge(fired, done + j + 1)
                            ve.scalar_tensor_tensor(now, neg_mem, -0.9, now, ALU.mult, ALU.add).then_inc(charged, 1)
                            ve.wait_ge(charged, done + j + 1)
                            ve.scalar_tensor_tensor(neg_mem, now, 1.0, now, ALU.is_gt, ALU.subtract)\
                                .then_inc(fired, 1)
                    ve.wait_ge(au_sg, b + 1)
                    ve.scalar_tensor_tensor(auT[:, bass.ds(b * T, T)], bank[7][0:R, :], v("b_au", 0, R), au_sig,
                                            ALU.add, ALU.mult).then_inc(au_ok, 1)
                    ve.wait_ge(nrm_ok, b + 1)
                    ve.tensor_scalar(nrm_e, nrm, 1e-6, None, ALU.add).then_inc(nrm_add, 1)
                    ve.wait_ge(nrm_add, b + 1)
                    ve.reciprocal(nrm_e, nrm_e).then_inc(nrm_inv, 1)

            @block.tensor
            def _(pe):
                pe.wait_ge(mconst, 6)
                with pe.Fori(0, B) as b:
                    tok = bass.ds(b * T, T)
                    pe.wait_ge(au_ok, at(b))
                    pe.matmul(bank[7][0:R, :], wau_sb[:, :], hT[:, tok], start=True, stop=True).then_inc(au_mm, 1)

                    def add_squares(j):
                        pe.wait_ge(sq_ok, at(b * NQK + j + 1))
                        pe.matmul(bank[4][0:2 * NQK, :], pick[:, j, :], sq_buf[:, j % 2, :],
                                  start=j == 0, stop=j == NQK - 1).then_inc(ss_mm, 1)

                    for j in range(NQK):
                        pe.wait_ge(sq_ok, at(b * NQK + j - 3)) if j >= 4 else pe.wait_ge(sq_ok, at(b * NQK))
                        pe.matmul(bank[j % 4][:, :], (wq_sb if j < HP else wk_sb)[:, j % HP, :], hT[:, tok],
                                  start=True, stop=True).then_inc(qk_mm, 1)
                        if j >= 1:
                            add_squares(j - 1)
                    add_squares(NQK - 1)
                    pe.wait_ge(nrm_inv, at(b + 1))
                    for j in range(NQK):
                        pe.wait_ge(bc_ok, at(b * NQK + j - 1)) if j >= 2 else pe.wait_ge(bc_ok, at(b * NQK))
                        pe.matmul(bank[5 + j % 2][:, :], spread[:, j, :], nrm_e, start=True, stop=True)\
                            .then_inc(bc_mm, 1)

            @block.scalar
            def _(ac):
                with ac.Fori(0, B) as b:
                    tok = bass.ds(b * T, T)
                    ac.wait_ge(au_mm, b + 1)
                    ac.activation(au_sig, bank[7][0:R, :], ACT.Sigmoid, bias=v("b_au", 0, R)).then_inc(au_sg, 1)
                    for j in range(NQK):
                        ac.wait_ge(qk_mm, b * NQK + j + 1)
                        ac.copy(qk_dst(j, tok), bank[j % 4][:, :]).then_inc(raw_ok, 1)
                        ac.wait_ge(ss_mm, at(b * NQK + j - 1)) if j >= 2 else ac.wait_ge(ss_mm, at(b * NQK))
                        ac.activation(sq_buf[:, j % 2, :], bank[j % 4][:, :], ACT.Square).then_inc(sq_ok, 1)
                    ac.wait_ge(ss_mm, at((b + 1) * NQK))
                    ac.wait_ge(nrm_inv, at(b))
                    ac.activation(nrm, bank[4][0:2 * NQK, :], ACT.Sqrt).then_inc(nrm_ok, 1)
                    for j in range(NQK):
                        ac.wait_ge(bc_mm, b * NQK + j + 1)
                        ac.wait_ge(qk_ok, at(b * NQK + j - 1)) if j >= 2 else ac.wait_ge(qk_ok, at(b * NQK))
                        ac.copy(inv_bc[:, j % 2, :], bank[5 + j % 2][:, :]).then_inc(bc_ok, 1)

            @block.gpsimd
            def _(gp):
                gp.memset(pick, 0.0).then_inc(mconst, 1)
                gp.memset(spread, 1.0).then_inc(mconst, 1)
                gp.wait_ge(mconst, 2)
                sp_v = spread.rearrange("r j (x d) -> r (j x) d", x=2)
                gp.affine_select(out=sp_v, in_=sp_v, compare_op=ALU.is_equal, fill=0.0, base=0,
                                 pattern=[[-1, 2 * NQK], [0, DK]], channel_multiplier=1).then_inc(mconst, 1)
                for par in range(2):
                    gp.wait_ge(mconst, 3 + par)
                    for j in range(NQK):
                        last = gp.tensor_copy(pick[:, j, 2 * j + par:2 * j + par + 1], bdones[:, C * par:C * par + 1])
                    last.then_inc(mconst, 1)
                gp.wait_ge(mconst, 5)
                gp.sem_inc(mconst, 1)
                with gp.Fori(0, B) as b:
                    tok = bass.ds(b * T, T)
                    for j in range(NQK):
                        gp.wait_ge(bc_ok, at(b * NQK + j + 1))
                        gp.tensor_tensor(qk_dst(j, tok), qk_dst(j, tok), inv_bc[:, j % 2, :], ALU.mult)\
                            .then_inc(qk_ok, 1)

        used[0] = early_end
        spk = region([2, 512])
        zal = region([2, 512])
        al0 = region([2, 512])
        be0 = region([2, 512])
        NG = HP
        spk_ok = sem("spk_ok")
        cnt_mm = sem("cnt_mm")
        ab_mm = sem("ab_mm")
        zal_ok = sem("zal_ok")
        be0_ok = sem("be0_ok")
        alpha_ok = sem("alpha_ok")

        with nc.Block() as block:
            @block.tensor
            def _(pe):
                with pe.Fori(0, B) as b:
                    tok = bass.ds(b * T, T)
                    for g in range(NG):
                        n, s = b * NG + g, g % 2
                        pe.wait_ge(spk_ok, n + 1)
                        pe.wait_ge(beta_ok, at(n - 1)) if g >= 2 else pe.wait_ge(beta_ok, at(b * NG))
                        pe.matmul(bank[4 * s + 1][:, :], bdones[:, :], spk[:, s, :], start=True, stop=True)\
                            .then_inc(cnt_mm, 1)
                        pe.matmul(bank[4 * s][:, :], wad_sb[:, g, :], auT[:, tok], start=True, stop=True)\
                            .then_inc(ab_mm, 1)
                        pe.matmul(bank[4 * s + 2][:, :], wbeta_rep[:, g].rearrange("p a b -> p (a b)"),
                                  hT[:, tok], start=True, stop=False)
                        pe.matmul(bank[4 * s + 2][:, :], bspike_bd[:, g, :], spk[:, s, :],
                                  start=False, stop=True).then_inc(beta_mm, 1)

            @block.vector
            def _(ve):
                with ve.Fori(0, B) as b:
                    tok = bass.ds(b * T, T)
                    for g in range(NG):
                        n, s = b * NG + g, g % 2
                        ve.wait_ge(beta_mm, at(n - 1)) if g >= 2 else ve.wait_ge(beta_mm, at(b * NG))
                        ve.tensor_scalar(spk[:, s, :], aT[:, g, tok], 1.0, None, ALU.is_gt).then_inc(spk_ok, 1)
                        ve.wait_ge(spk_ok, n + 1)
                        ve.wait_ge(ab_mm, n + 1)
                        ve.wait_ge(al0_ok, at(n - 1)) if g >= 2 else ve.wait_ge(al0_ok, at(b * NG))
                        ve.scalar_tensor_tensor(zal[:, s, :], spk[:, s, :], v("alpha_spike", g), bank[4 * s][:, :],
                                                ALU.mult, ALU.add).then_inc(zal_ok, 1)
                        ve.wait_ge(cnt_mm, n + 1)
                        ve.wait_ge(al0_ok, at(n + 1))
                        ve.scalar_tensor_tensor(aT[:, g, tok], bank[4 * s + 1][:, :], 0.0, al0[:, s, :],
                                                ALU.is_equal, ALU.max).then_inc(alpha_ok, 1)
                        ve.wait_ge(be0_ok, n + 1)
                        ve.scalar_tensor_tensor(bT[:, g, tok], bank[4 * s + 1][:, :], 0.0, be0[:, s, :],
                                                ALU.is_gt, ALU.mult).then_inc(beta_ok, 1)

            @block.scalar
            def _(ac):
                with ac.Fori(0, B) as b:
                    for g in range(NG):
                        n, s = b * NG + g, g % 2
                        ac.wait_ge(zal_ok, n + 1)
                        ac.wait_ge(beta_ok, at(n - 1)) if g >= 2 else ac.wait_ge(beta_ok, at(b * NG))
                        ac.activation(al0[:, s, :], zal[:, s, :], ACT.Sigmoid, bias=v("b_ad", g)).then_inc(al0_ok, 1)
                        ac.wait_ge(beta_mm, at(n + 1))
                        ac.activation(be0[:, s, :], bank[4 * s + 2][:, :], ACT.Sigmoid, bias=v("b_beta", g))\
                            .then_inc(be0_ok, 1)

        used[0] = 0
        state = region([B, HP, DV])
        KS = region([HP, 2, C])
        KQ2 = region([2, 2, HP, C])
        KPn = region([HP, 2, C])
        QPb = region([HP, 2, C])
        AQ2 = region([2, HP, 2, C])
        NE = LEVELS
        E = region([NE, HP, P])
        XY = region([2, 2, 2, P])
        Z = region([2, 2, P])
        KSn = region([2, HP, P])
        res = region([HP, DV])
        U = region([HP, DV])
        On = res
        hc = region([C])
        decay = region([B, HP])
        tot = region([HP * 2 * C])
        ms = mom[:, 0:4, 0:HP]
        tot_at = [2 * HP * (C - (2 * C >> l)) for l in range(LEVELS)]
        tot_of = [None] + [tot[:, tot_at[l]:tot_at[l] + (2 * HP * C >> l)].rearrange("p (a x j) -> p a x j", a=HP, x=2)
                           for l in range(1, LEVELS)]
        G = 2
        GP = HP // G
        psL, psZ, psXY, psR, psO = bank[0:2], bank[2:4], bank[4:6], bank[6], bank[7]

        zeroed = sem("zeroed")
        waited = sem("waited")
        kq_ok = sem("kq_ok")
        ks_ok = sem("ks_ok")
        tot_ok = sem("tot_ok")
        lvl_mm = sem("lvl_mm")
        diag_mm = sem("diag_mm")
        e_ok = sem("e_ok")
        aq_ok = sem("aq_ok")
        x_init = sem("x_init")
        yt_mm = sem("yt_mm")
        xy_ok = sem("xy_ok")
        z_mm = sem("z_mm")
        z_ok = sem("z_ok")
        dxy_mm = sem("dxy_mm")
        hc_ok = sem("hc_ok")
        kpn_ok = sem("kpn_ok")
        qpb_ok = sem("qpb_ok")
        ksn_mm = sem("ksn_mm")
        ksn_ok = sem("ksn_ok")
        res_mm = sem("res_mm")
        res_ok = sem("res_ok")
        u_mm = sem("u_mm")
        u_ok = sem("u_ok")
        o_mm = sem("o_mm")
        o_sq = sem("o_sq")
        ms_ok = sem("ms_ok")
        rr_ok = sem("rr_ok")
        s_mm = sem("s_mm")
        s_ok = sem("s_ok")
        on_ok = sem("on_ok")
        dec_ok = sem("dec_ok")
        yout_mm = sem("yout_mm")
        yout_ok = sem("yout_ok")
        NKQ = LEVELS + 1
        NTOT = LEVELS - 1
        NKS = LEVELS + 2
        NINV = LEVELS - 1

        def halves(t):
            return [t[C * par:C * par + C, :, par, :] for par in range(2)]

        def member(n, l, k):
            if l == 0:
                return aT[:, :, n.tok].rearrange("p a (j s) -> p a j s", s=2)[:, :, :, k].unsqueeze(2)\
                    .broadcast_to([P, HP, 2, C // 2])
            return tot_of[l].rearrange("p a x (j s) -> p a x j s", s=2)[:, :, :, :, k]

        def flat(t, hp):
            return t[:, hp].rearrange("p x t -> p (x t)")

        class Round:
            def __init__(self, c, b):
                self.it, self.b, self.slot = c * B + b, b, b % 2
                self.tok = bass.ds(b * T + c * C, C) if not isinstance(c, int) else \
                    slice(b * T + c * C, b * T + c * C + C)

        def rounds(eng, body, finish=None):
            def chunk(c, first, last):
                for b in range(B):
                    nxt = Round(c, b + 1) if b + 1 < B else None if last else Round(c + 1, 0)
                    if nxt:
                        nxt.after = Round(c, b + 2) if b + 2 < B else None if last else Round(c + 1, b + 2 - B)
                    prev = Round(c, b - 1) if b else None if first else Round(c - 1, B - 1)
                    body(Round(c, b), nxt, prev)

            chunk(0, True, False)
            with eng.Fori(1, NC - 1) as c:
                chunk(c, False, False)
            chunk(NC - 1, False, True)
            if finish:
                finish(Round(NC - 1, B - 1))

        psLv = [t[:, :].rearrange("p (a x t) -> p a x t", a=HP, x=2) for t in psL]

        with nc.Block() as block:
            @block.gpsimd
            def _(gp):
                for t in (state, KS, KPn, QPb):
                    gp.memset(t, 0.0).then_inc(zeroed, 1)
                gp.memset(ms[:, 2, :], -0.5).then_inc(zeroed, 1)
                gp.memset(ms[:, 3, :], 1e-6).then_inc(zeroed, 1)
                gp.wait_ge(zeroed, 6)

                def products(n):
                    gp.sem_inc(waited, 1)
                    for l in range(NTOT):
                        if l:
                            gp.wait_ge(tot_ok, n.it * NTOT + l)
                        gp.tensor_tensor(tot_of[l + 1], member(n, l, 0), member(n, l, 1), ALU.mult).then_inc(tot_ok, 1)

                def total(n):
                    gp.wait_ge(tot_ok, (n.it + 1) * NTOT)
                    gp.tensor_tensor(decay[:, n.b, :], tot_of[NTOT][:, :, 0, 0], tot_of[NTOT][:, :, 0, 1],
                                     ALU.mult).then_inc(dec_ok, 1)

                def keys(n):
                    if not (isinstance(n.it, int) and n.it == 0):
                        gp.wait_ge(ksn_mm, n.it)
                    for par, dst in enumerate(halves(KS)):
                        rows = slice(C * par, C * par + C)
                        gp.tensor_tensor(dst, kT[rows, :, n.tok], bT[rows, :, n.tok], ALU.mult).then_inc(ks_ok, 1)
                        gp.wait_ge(ks_ok, n.it * NKS + par + 1)

                def suffix(n, l):
                    gp.wait_ge(lvl_mm, n.it * LEVELS + l + 1)
                    if l == 0:
                        gp.wait_ge(diag_mm, n.it + 1)
                        gp.sem_inc(waited, 1)
                        first, by = KS[:, :, :, 0:C:2], member(n, 0, 1)
                    else:
                        first = KS.rearrange("p a x (j s t) -> p (a x j) s t", s=2, t=1 << l)[:, :, 0, :]
                        by = tot_of[l].rearrange("p a x (j s) -> p (a x j) s", s=2)[:, :, 1]\
                            .unsqueeze(2).broadcast_to([P, HP * C >> l, 1 << l])
                    gp.tensor_tensor(first, first, by, ALU.mult).then_inc(ks_ok, 1)
                    gp.wait_ge(ks_ok, n.it * NKS + l + 3)

                def start(n):
                    if not (isinstance(n.it, int) and n.it == 0):
                        gp.wait_ge(kq_ok, n.it * NKQ)
                    products(n)
                    total(n)
                    keys(n)
                    suffix(n, 0)

                def body(cur, nxt, prev):
                    if nxt:
                        for l in range(1, LEVELS):
                            suffix(nxt, l)
                        if nxt.after:
                            start(nxt.after)
                    gp.wait_ge(o_sq, cur.it + 1)
                    gp.tensor_tensor(ms[:, 0, :], ms[:, 0, :], ms[:, 3, :], ALU.add).then_inc(ms_ok, 1)
                    gp.wait_ge(ms_ok, cur.it + 1)
                    gp.tensor_tensor(ms[:, 1, :], ms[:, 0, :], ms[:, 2, :], ALU.pow).then_inc(rr_ok, 1)

                start(Round(0, 0))
                for l in range(1, LEVELS):
                    suffix(Round(0, 0), l)
                start(Round(0, 1))
                rounds(gp, body)

            @block.vector
            def _(ve):
                ve.wait_ge(zeroed, 6)

                def prefixes(n):
                    if not (isinstance(n.it, int) and n.it <= 1):
                        ve.wait_ge(kpn_ok, (n.it - 1) * 2)
                    KQ = KQ2[:, n.slot]
                    ve.tensor_tensor(KQ[:, 0], kT[:, :, n.tok], aT[:, :, n.tok], ALU.mult)
                    ve.tensor_tensor(KQ[:, 1], qT[:, :, n.tok], aT[:, :, n.tok], ALU.mult).then_inc(kq_ok, 1)

                def prefix(n, l):
                    L = 1 << l
                    second = KQ2[:, n.slot].rearrange("p x a (j s t) -> p x a j s t", s=2, t=L)[:, :, :, :, 1, :]
                    by = member(n, l, 0)[:, :, 0]
                    ve.wait_ge(lvl_mm, n.it * LEVELS + l + 1)
                    if l:
                        ve.wait_ge(tot_ok, n.it * NTOT + l)
                    ve.wait_ge(kq_ok, n.it * NKQ + l + 1)
                    for x_ in range(2):
                        last = ve.tensor_tensor(second[:, x_], second[:, x_],
                                                by.unsqueeze(3).broadcast_to([P, HP, C // (2 * L), L]), ALU.mult)
                    last.then_inc(kq_ok, 1)

                def diagonal(n):
                    ve.wait_ge(diag_mm, n.it + 1)
                    if not (isinstance(n.it, int) and n.it <= 1):
                        ve.wait_ge(o_mm, n.it - 1)
                    ve.tensor_tensor(AQ2[:, n.slot], psZ[1][:, 0:HP * C].rearrange("p (a t) -> p a t", a=HP)
                                     .unsqueeze(2).broadcast_to([P, HP, 2, C]),
                                     ident[:, :].rearrange("p (x t) -> p x t", x=2).unsqueeze(1)
                                     .broadcast_to([P, HP, 2, C]), ALU.mult).then_inc(aq_ok, 1)

                def keep(n, l):
                    mk = mask[:, l, :].rearrange("p (x t) -> p x t", x=2).unsqueeze(1)
                    ve.wait_ge(aq_ok, n.it * NKQ + l + 1)
                    if l == 0:
                        ve.wait_ge(yt_mm, n.it * G)
                        ve.wait_ge(x_init, n.it)
                    elif not (isinstance(n.it, int) and n.it == 0):
                        ve.wait_ge(z_mm, (n.it - 1) * G * NINV + G * l)
                    ve.tensor_tensor(E[:, l].rearrange("p a (x t) -> p a x t", x=2),
                                     psLv[l % 2][:, :, 0, :].unsqueeze(2).broadcast_to([P, HP, 2, C]),
                                     mk.broadcast_to([P, HP, 2, C]), ALU.mult).then_inc(e_ok, 1)
                    ve.copy_predicated(AQ2[:, n.slot], mk.broadcast_to([P, HP, 2, C]).bitcast(U32),
                                       psLv[l % 2][:, :, 1, :].unsqueeze(2).broadcast_to([P, HP, 2, C])).then_inc(aq_ok, 1)

                def start_x(n):
                    ve.wait_ge(e_ok, n.it * LEVELS + 1)
                    ve.wait_ge(u_mm, n.it)
                    for g in range(G):
                        last = ve.tensor_tensor(XY[:, g, 0], ident[:, :].unsqueeze(1).broadcast_to([P, GP, P]),
                                                E[:, 0, g * GP:(g + 1) * GP, :], ALU.subtract)
                    last.then_inc(x_init, 1)

                def start_y(n):
                    for g in range(G):
                        ve.wait_ge(yt_mm, n.it * G + g + 1)
                        ve.tensor_tensor(XY[:, g, 1], ident[:, :].unsqueeze(1).broadcast_to([P, GP, P]),
                                         psXY[g][:, GP * P:].rearrange("p (h t) -> p h t", h=GP),
                                         ALU.subtract).then_inc(xy_ok, 1)

                def start(n, after):
                    if after:
                        prefixes(after)
                    start_x(n)
                    if after:
                        prefix(after, 0)
                        diagonal(after)
                    start_y(n)
                    if after:
                        keep(after, 0)

                def double(n, l):
                    for g in range(G):
                        ve.wait_ge(dxy_mm, n.it * G * NINV + G * (l - 1) + g + 1)
                        k = 2 if l < NINV else 1
                        ps = psXY[g][:, 0:k * GP * P].rearrange("p (x h t) -> p x h t", x=k, h=GP)
                        ve.tensor_tensor(XY[:, g, 0:k], XY[:, g, 0:k], ps, ALU.subtract).then_inc(xy_ok, 1)

                def normalise(n):
                    ve.wait_ge(rr_ok, n.it + 1)
                    ve.tensor_tensor(On, psO[:, :].rearrange("p (a n) -> p a n", a=HP),
                                     ms[:, 1, :].unsqueeze(2).broadcast_to([P, HP, DV]), ALU.mult).then_inc(on_ok, 1)

                def body(cur, nxt, prev):
                    it = cur.it
                    for l in range(1, LEVELS):
                        if nxt:
                            prefix(nxt, l)
                            keep(nxt, l)
                        double(cur, l)
                    if nxt:
                        start(nxt, nxt.after)
                    ve.wait_ge(dec_ok, it + 1)
                    for hp in range(HP):
                        ve.wait_ge(s_mm, it + 1)
                        ve.scalar_tensor_tensor(state[:, cur.b, hp, :], state[:, cur.b, hp, :],
                                                decay[:, cur.b, hp:hp + 1], psR[:, hp * DV:(hp + 1) * DV],
                                                ALU.mult, ALU.add).then_inc(s_ok, 1)
                    normalise(cur)

                first = Round(0, 0)
                prefixes(first)
                prefix(first, 0)
                diagonal(first)
                keep(first, 0)
                for l in range(1, LEVELS):
                    prefix(first, l)
                    keep(first, l)
                start(first, Round(0, 1))
                rounds(ve, body)

            @block.tensor
            def _(pe):
                pe.wait_ge(zeroed, 6)

                def level(n, l):
                    pe.wait_ge(kq_ok, n.it * NKQ + l + 1)
                    pe.wait_ge(ks_ok, n.it * NKS + l + 2)
                    pe.wait_ge(aq_ok, n.it * NKQ + l) if l >= 2 else pe.wait_ge(aq_ok, n.it * NKQ)
                    if l == 0:
                        pe.wait_ge(ksn_ok, n.it)
                    for hp in range(HP):
                        last = pe.matmul(psL[l % 2][:, hp * P:(hp + 1) * P], flat(KS, hp), KQ2[:, n.slot, :, hp, :],
                                         start=True, stop=True)
                    last.then_inc(lvl_mm, 1)

                def diagonal(n):
                    pe.wait_ge(z_ok, (n.it - 1) * G * NINV) if not (isinstance(n.it, int) and n.it == 0) else None
                    for hp in range(HP):
                        last = pe.matmul(psZ[1][:, hp * C:(hp + 1) * C], flat(KS, hp), qT[:, hp, n.tok],
                                         start=True, stop=True)
                    last.then_inc(diag_mm, 1)

                def double(n, l):
                    it = n.it
                    for g in range(G):
                        pe.wait_ge(e_ok, it * LEVELS + l + 1)
                        pe.wait_ge(x_init, it + 1)
                        pe.wait_ge(xy_ok, it * G * LEVELS + G * (l - 1) + g + 1)
                        if l == 1:
                            pe.wait_ge(aq_ok, n.diag_out)
                        for h in range(GP):
                            last = pe.matmul(psZ[g][:, h * P:(h + 1) * P], E[:, l, g * GP + h, :],
                                             XY[:, g, 1, h, :], start=True, stop=True)
                        last.then_inc(z_mm, 1)
                    for g in range(G):
                        pe.wait_ge(z_ok, it * G * NINV + G * (l - 1) + g + 1)
                        for h in range(GP):
                            last = pe.matmul(psXY[g][:, h * P:(h + 1) * P], Z[:, g, h, :],
                                             XY[:, g, 0, h, :], start=True, stop=True)
                            if l < NINV:
                                last = pe.matmul(psXY[g][:, (GP + h) * P:(GP + h + 1) * P], XY[:, g, 0, h, :],
                                                 Z[:, g, h, :], start=True, stop=True)
                        last.then_inc(dxy_mm, 1)

                def turn_ks(n):
                    pe.wait_ge(ks_ok, (n.it + 1) * NKS)
                    pe.wait_ge(aq_ok, n.it * NKQ + LEVELS)
                    for hp in range(HP):
                        last = pe.transpose(psL[0][:, hp * P:(hp + 1) * P], flat(KS, hp), ident[:, :])
                    last.then_inc(ksn_mm, 1)

                def turn_out(n):
                    pe.wait_ge(on_ok, n.it + 1)
                    for hp in range(HP):
                        last = pe.transpose(psO[:, hp * P:(hp + 1) * P], On[:, hp, :], ident[:, :])
                    last.then_inc(yout_mm, 1)

                def turn_e(n):
                    pe.wait_ge(e_ok, n.it * LEVELS + 1)
                    pe.wait_ge(xy_ok, n.it * G * LEVELS)
                    for g in range(G):
                        for h in range(GP):
                            last = pe.transpose(psXY[g][:, (GP + h) * P:(GP + h + 1) * P], E[:, 0, g * GP + h, :],
                                                ident[:, :])
                        last.then_inc(yt_mm, 1)

                def body(cur, nxt, prev):
                    it = cur.it
                    after = nxt.after if nxt else None
                    cur.diag_out = (it + 1) * NKQ + (1 if nxt else 0)
                    for l in range(1, NINV):
                        if nxt:
                            level(nxt, l)
                        double(cur, l)
                        if l == 1 and prev:
                            turn_out(prev)
                    if nxt:
                        level(nxt, NINV)
                    pe.wait_ge(hc_ok, it + 1)
                    pe.wait_ge(s_ok, it * HP)
                    for par in range(2):
                        pe.matmul(psR[C * par:C * par + C, :], hc, wv_sb[:, :, par, :], start=True, stop=False,
                                  skip_group_check=True)
                    pe.wait_ge(kpn_ok, it * 2 + 2)
                    for hp in range(HP):
                        last = pe.matmul(psR[:, hp * DV:(hp + 1) * DV], flat(KPn, hp), state[:, cur.b, hp, :],
                                         start=False, stop=True, skip_group_check=True)
                    last.then_inc(res_mm, 1)
                    if nxt:
                        turn_ks(nxt)
                    double(cur, NINV)
                    pe.wait_ge(qpb_ok, it * 2 + 2)
                    pe.wait_ge(yout_ok, it * 2)
                    for hp in range(HP):
                        pe.matmul(psO[:, hp * DV:(hp + 1) * DV], flat(QPb, hp), state[:, cur.b, hp, :],
                                  start=hp == 0, stop=False, skip_group_check=True)
                    pe.wait_ge(res_ok, it + 1)
                    pe.wait_ge(xy_ok, (it + 1) * G * LEVELS)
                    for hp in range(HP):
                        last = pe.matmul(psR[:, hp * DV:(hp + 1) * DV], XY[:, hp // GP, 0, hp % GP, :], res[:, hp, :],
                                         start=True, stop=True)
                    last.then_inc(u_mm, 1)
                    if after:
                        level(after, 0)
                    pe.wait_ge(aq_ok, (it + 1) * NKQ)
                    pe.wait_ge(u_ok, it + 1)
                    for hp in range(HP):
                        last = pe.matmul(psO[:, hp * DV:(hp + 1) * DV], flat(AQ2[:, cur.slot], hp), U[:, hp, :],
                                         start=False, stop=True, skip_group_check=True)
                    last.then_inc(o_mm, 1)
                    if after:
                        diagonal(after)
                    if nxt:
                        turn_e(nxt)
                    pe.wait_ge(ksn_ok, it + 1)
                    for hp in range(HP):
                        last = pe.matmul(psR[:, hp * DV:(hp + 1) * DV], KSn[:, cur.slot, hp, :], U[:, hp, :],
                                         start=True, stop=True)
                    last.then_inc(s_mm, 1)

                first = Round(0, 0)
                level(first, 0)
                diagonal(first)
                for l in range(1, LEVELS):
                    level(first, l)
                turn_ks(first)
                level(Round(0, 1), 0)
                diagonal(Round(0, 1))
                turn_e(first)
                rounds(pe, body, turn_out)

            @block.scalar
            def _(ac):
                ac.wait_ge(zeroed, 6)

                def copy_z(n, l):
                    for g in range(G):
                        ac.wait_ge(z_mm, n.it * G * NINV + G * (l - 1) + g + 1)
                        ac.wait_ge(dxy_mm, n.it * G * NINV + G * (l - 2) + g + 1) if l >= 2 else \
                            ac.wait_ge(dxy_mm, n.it * G * NINV)
                        ac.copy(Z[:, g], psZ[g][:, 0:GP * P].rearrange("p (h t) -> p h t", h=GP)).then_inc(z_ok, 1)

                def spread_kq(n):
                    ac.wait_ge(kq_ok, (n.it + 1) * NKQ)
                    ac.wait_ge(o_mm, n.it)
                    for x_, dst, done, by in ((1, QPb, qpb_ok, 1.0), (0, KPn, kpn_ok, -1.0)):
                        for par in range(2):
                            rows = slice(C * par, C * par + C)
                            ac.mul(dst[rows, :, par, :], KQ2[rows, n.slot, x_], by).then_inc(done, 1)

                def keep_ks(n):
                    ac.wait_ge(ksn_mm, n.it + 1)
                    ac.copy(KSn[:, n.slot], psL[0][:, :].rearrange("p (a n) -> p a n", a=HP)).then_inc(ksn_ok, 1)

                def keep_out(n):
                    ac.wait_ge(yout_mm, n.it + 1)
                    for par, dst in enumerate((qT, kT)):
                        ac.copy(dst[:, :, n.tok], psO[:, :].rearrange("p (a x t) -> p a x t", a=HP, x=2)[:, :, par, :])\
                            .then_inc(yout_ok, 1)

                def body(cur, nxt, prev):
                    it = cur.it
                    ac.copy(hc, hT[:, cur.tok]).then_inc(hc_ok, 1)
                    for l in range(1, NINV):
                        copy_z(cur, l)
                        if l == 1 and prev:
                            keep_out(prev)
                    ac.wait_ge(res_mm, it + 1)
                    ac.wait_ge(yout_mm, it)
                    ac.copy(res, psR[:, :].rearrange("p (a n) -> p a n", a=HP)).then_inc(res_ok, 1)
                    copy_z(cur, NINV)
                    if nxt:
                        ac.wait_ge(s_mm, it)
                        keep_ks(nxt)
                    ac.wait_ge(u_mm, it + 1)
                    ac.wait_ge(s_mm, it)
                    ac.copy(U, psR[:, :].rearrange("p (a n) -> p a n", a=HP)).then_inc(u_ok, 1)
                    ac.wait_ge(o_mm, it + 1)
                    ac.wait_ge(rr_ok, it)
                    for hp in range(HP):
                        last = ac.activation(res[:, hp, :], psO[:, hp * DV:(hp + 1) * DV], ACT.Square,
                                             scale=DV ** -0.5, accum_out=ms[:, 0, hp:hp + 1])
                    last.then_inc(o_sq, 1)
                    if nxt:
                        spread_kq(nxt)
                spread_kq(Round(0, 0))
                keep_ks(Round(0, 0))
                rounds(ac, body, keep_out)

        late = gates[:, :, :, :].rearrange("p g a t -> p (g a t)")
        late_at, used[0] = [0], 0

        def late_region(shape):
            return region(shape, late, late_at)

        wff1_sb = late_region([FT * P])
        wff3_sb = late_region([FT * P])
        wff2_sb = late_region([FT, D])
        Wq_sb = late_region([XP, P])
        Wk_sb = late_region([XP, P])
        Wv_sb = late_region([XP * P])
        Wo_sb = late_region([XP, D])
        N0 = k0.shape[1]
        F2 = N0 // P
        w0_sb = late_region([2, N0])
        w1_sb = late_region([F2, k1.shape[1]])
        w2_sb = late_region([F2, D])
        k0_sb = late_region([2 * N0 // 4]).bitcast(U8).rearrange("p (a n) -> p a n", a=2)
        k1_sb = late_region([F2 * k1.shape[1] // 4]).bitcast(U8).rearrange("p (a n) -> p a n", a=F2)
        k2_sb = late_region([F2 * D // 4]).bitcast(U8).rearrange("p (a n) -> p a n", a=F2)
        NTB = T // P
        Q2 = late_region([XP, T])
        XO = Q2
        wout_sb = region([2 * HP, D])
        ctx_sb = region([B, D])[0:S]
        ctxT = region([B, S])
        cb = region([S])
        KB = region([XP, 2, S])
        VB = region([XH * DK])[0:S]
        PR = region([2, XH, S])
        PT = region([XH, P])[0:S]
        FH = hT[:, :].rearrange("p (f t) -> p f t", f=FT)
        smx = region([2, 3, XH])
        m = [region([T]) for _ in range(7)]
        H1 = Q2[:, 0:F2]
        H2 = Q2[:, F2:2 * F2]
        x_nat = region([T // P, D])
        s0x2 = region([1])
        s1x2 = region([1])
        epsr, epsl = 1e-6, 1e-5
        NP3 = [(0, 3), (3, 3), (6, 2)]

        tw = sem("tail_w")
        ctx_ld = sem("ctx_ld")
        wout_ld, wout_ok = sem("wout_ld"), sem("wout_ok")
        signs = sem("signs")
        ctx_mm, ctx_ok = sem("ctx_mm"), sem("ctx_ok")
        kb_zero = sem("kb_zero")
        at_mm, u1_mm, u1_sig, u1_ok = sem("at_mm"), sem("u1_mm"), sem("u1_sig"), sem("u1_ok")
        u2_mm, gate_ok, gated, y1_ok = sem("u2_mm"), sem("gate_ok"), sem("gated"), sem("y1_ok")
        n_sq, n_mm, n_rt, n_inv = sem("n_sq"), sem("n_mm"), sem("n_rt"), sem("n_inv")
        n_cen, n_out, mean_mm = sem("n_cen"), sem("n_out"), sem("mean_mm")
        ff_mm, ff_sig, ff_mul, ff_ok = sem("ff_mm"), sem("ff_sig"), sem("ff_mul"), sem("ff_ok")
        ff2_mm, x1_ok, x_in = sem("ff2_mm"), sem("x1_ok"), sem("x_in")
        q2_mm, q2_ok = sem("q2_mm"), sem("q2_ok")
        cb_ok, kb_mm, kb_ok, vb_mm, vb_ok = sem("cb_ok"), sem("kb_mm"), sem("kb_ok"), sem("vb_mm"), sem("vb_ok")
        sc_mm, mx_ok, exp_ok = sem("sc_mm"), sem("mx_ok"), sem("exp_ok")
        sum_ok, inv_ok, pr_ok = sem("sum_ok"), sem("inv_ok"), sem("pr_ok")
        wo_mm, wo_ok, ln_sc, x2_ok = sem("wo_mm"), sem("wo_ok"), sem("ln_sc"), sem("x2_ok")
        h1_mm, h1_ok, h2_mm, h2_ok = sem("h1_mm"), sem("h1_ok"), sem("h2_mm"), sem("h2_ok")
        h3_mm, y_ok, yt2_mm = sem("h3_mm"), sem("y_ok"), sem("yt2_mm")
        NORMS = 4
        CEN = 3

        TW_FF, TW_Q, TW_K, TW_V, TW_O, TW_SIGN = (16 * n for n in (3, 4, 5, 6, 7, 10))

        with nc.Block() as block:
            @block.sync
            def _(sp):
                sp.dma_start(ctx_sb, ctx_in.rearrange("b s d -> s b d")).then_inc(ctx_ld, 16)
                sp.dma_start(wout_sb, w_out.rearrange("(h v) d -> v h d", v=DV)).then_inc(wout_ld, 16)
                for dst, src in ((wff1_sb, w_ff1), (wff3_sb, w_ff3),
                                 (wff2_sb, w_ff2.rearrange("(a p) d -> p a d", p=P)),
                                 (Wq_sb, Wq.rearrange("d (a n) -> d a n", a=XP)),
                                 (Wk_sb, Wk.rearrange("d (a n) -> d a n", a=XP)), (Wv_sb, Wv),
                                 (Wo_sb, Wo.rearrange("(a p) d -> p a d", p=P)),
                                 (k0_sb, k0.rearrange("(a p) n -> p a n", p=P)),
                                 (k1_sb, k1.rearrange("(a p) n -> p a n", p=P)),
                                 (k2_sb, k2.rearrange("(a p) n -> p a n", p=P))):
                    sp.dma_start(dst, src).then_inc(tw, 16)
                out_v = out.rearrange("b t d -> (b t) d").rearrange("(b n p) d -> b p n d", p=P, n=NTB)
                x_v = x.rearrange("b t d -> (b t) d").rearrange("(b n p) d -> b p n d", p=P, n=NTB)
                sp.dma_start(x_nat, x_v[0]).then_inc(x_in, 16)
                with sp.Fori(0, B) as b:
                    sp.wait_ge(x1_ok, b + 1)
                    nxt_row = (b + 1) % B
                    sp.dma_start(x_nat, x_v[bass.ds(nxt_row, 1)].squeeze(0)).then_inc(x_in, 16)
                    sp.wait_ge(row_done, at(b + 1))
                    sp.dma_start(out_v[bass.ds(b, 1)].squeeze(0), m[6].rearrange("p (n d) -> p n d", n=NTB))\
                        .then_inc(stored, 16)
                sp.wait_ge(stored, at(16 * B))

            @block.gpsimd
            def _(gp):
                gp.memset(KB, 0.0).then_inc(kb_zero, 1)
                gp.wait_ge(tw, TW_SIGN)
                gp.tensor_scalar(w0_sb, k0_sb, 2.0, -1.0, ALU.mult, ALU.add).then_inc(signs, 1)
                gp.tensor_scalar(w1_sb, k1_sb, 2.0, -1.0, ALU.mult, ALU.add).then_inc(signs, 1)
                gp.tensor_scalar(w2_sb, k2_sb, 2.0, -1.0, ALU.mult, ALU.add).then_inc(signs, 1)
                gp.wait_ge(signs, 3)
                gp.tensor_tensor(w0_sb[:, 0], w0_sb[:, 0], w0_sb[:, 1], ALU.subtract).then_inc(signs, 1)
                gp.tensor_scalar(s0x2, v("s0"), 2.0, None, ALU.mult).then_inc(signs, 1)
                gp.tensor_scalar(s1x2, v("s1"), 2.0, None, ALU.mult).then_inc(signs, 1)
                with gp.Fori(0, B) as b:
                    for n in range(NTB):
                        i = b * NTB + n
                        gp.wait_ge(inv_ok, i + 1)
                        gp.tensor_tensor(PR[:, n % 2], PR[:, n % 2], smx[:, n % 2, 2, :].unsqueeze(2).broadcast_to([P, XH, S]), ALU.mult)\
                            .then_inc(pr_ok, 1)

            @block.tensor
            def _(pe):
                pe.wait_ge(ctx_ld, 16)
                for j in range(B):
                    last = pe.transpose(bank[0][:, j * S:(j + 1) * S], ctx_sb[:, j, :], ident[0:S, 0:S])
                last.then_inc(ctx_mm, 1)
                pe.wait_ge(ctx_ok, 1)

                def mean_square(b, k):
                    pe.wait_ge(n_sq, b * NORMS + k + 1)
                    pe.matmul(bank[3][:, :], mean_w[:, :], m[1], start=True, stop=True).then_inc(n_mm, 1)

                def mean(src, centred):
                    pe.matmul(bank[2][:, :], mean_w[:, :], src, start=True, stop=True).then_inc(centred, 1)

                with pe.Fori(0, B) as b:
                    tok = bass.ds(b * T, T)
                    pe.wait_ge(row_done, at(b))
                    pe.matmul(bank[1][0:R, :], wu1_sb[:, :], zT[:, tok], start=True, stop=True).then_inc(u1_mm, 1)
                    pe.wait_ge(wout_ok, 2 * HP)
                    for h in range(2 * HP):
                        last = pe.matmul(bank[0][:, :], wout_sb[:, h, :], (qT, kT)[h % 2][:, h // 2, tok],
                                         start=h == 0, stop=h == 2 * HP - 1)
                    last.then_inc(at_mm, 1)
                    pe.wait_ge(u1_ok, b + 1)
                    pe.matmul(bank[1][:, :], wu2_sb[:, :], m[1][0:R], start=True, stop=True).then_inc(u2_mm, 1)
                    mean_square(b, 0)
                    pe.wait_ge(tw, TW_FF)
                    pe.wait_ge(n_out, b * NORMS + 1)
                    for f in range(FT):
                        if f >= 2:
                            pe.wait_ge(ff_ok, b * FT + f - 1)
                        for j, w in enumerate((wff1_sb, wff3_sb)):
                            last = pe.matmul(bank[4 + 2 * (f % 2) + j][:, :], w[:, f * P:(f + 1) * P], m[4],
                                             start=True, stop=True)
                        last.then_inc(ff_mm, 1)
                    for f in range(FT):
                        pe.wait_ge(ff_ok, b * FT + f + 1)
                        pe.matmul(bank[0][:, :], wff2_sb[:, f, :], FH[:, f, :], start=f == 0, stop=False,
                                  skip_group_check=True)
                    pe.wait_ge(x_in, b * 16 + 16)
                    for n in range(NTB):
                        last = pe.matmul(bank[0][:, n * P:(n + 1) * P], x_nat[:, n, :], ident[:, :],
                                         start=False, stop=True, skip_group_check=True)
                    last.then_inc(ff2_mm, 1)
                    pe.wait_ge(x1_ok, b + 1)
                    mean(m[4], mean_mm)
                    mean_square(b, 1)
                    pe.wait_ge(tw, TW_V)
                    for a in range(XP):
                        last = pe.matmul(bank[a // 4][:, (a % 4) * S:(a % 4 + 1) * S], Wk_sb[:, a, :],
                                         ctxT[:, bass.ds(b, 1), :].squeeze(1), start=True, stop=True)
                    last.then_inc(kb_mm, 1)
                    pe.wait_ge(n_out, b * NORMS + 2)
                    for a in range(XP):
                        if a >= 4:
                            pe.wait_ge(q2_ok, b * XP + a - 3)
                        pe.matmul(bank[4 + a % 4][:, :], Wq_sb[:, a, :], m[3], start=True, stop=True).then_inc(q2_mm, 1)
                    pe.wait_ge(cb_ok, b + 1)
                    for j in range(2):
                        last = pe.matmul(bank[2 + j][0:S, :], cb, Wv_sb[:, j * 512:(j + 1) * 512],
                                         start=True, stop=True)
                    last.then_inc(vb_mm, 1)
                    pe.wait_ge(kb_ok, b * 4 + 4)
                    pe.wait_ge(vb_ok, b * 2 + 2)
                    pe.wait_ge(q2_ok, (b + 1) * XP)

                    def scores(n):
                        pe.wait_ge(sub_ok, at(b * 3 * NTB + 3 * n))
                        for j, (a0, na) in enumerate(NP3):
                            for a in range(na):
                                last = pe.matmul(bank[4 + j][:, a * 2 * S:(a + 1) * 2 * S],
                                                 Q2[:, a0 + a, n * P:(n + 1) * P],
                                                 KB[:, a0 + a].rearrange("p x s -> p (x s)"), start=True, stop=True)
                            last.then_inc(sc_mm, 1)

                    scores(0)
                    scores(1)
                    for n in range(NTB):
                        i = b * NTB + n
                        pe.wait_ge(pr_ok, i + 1)
                        for q in range(4):
                            if q == 0:
                                pe.wait_ge(pt_v, at(i * 2))
                                pe.wait_ge(pt_a, at(i * 2))
                            elif q == 3:
                                pe.wait_ge(pt_a, at(i * 2 + 1))
                            for h in range(4):
                                last = pe.transpose(bank[q % 3][0:S, h * P:(h + 1) * P], PR[:, n % 2, 4 * q + h, :], ident[:, :])
                            last.then_inc(pt_mm, 1)
                        if n + 2 < NTB:
                            scores(n + 2)
                        pe.wait_ge(pt_a, at(i * 2 + 2))
                        pe.wait_ge(pt_v, at(i * 2 + 2))
                        pe.wait_ge(xo_ok, at(i * 2))
                        for h in range(XH):
                            a, par = h // 2, h % 2
                            last = pe.matmul((bank[3], bank[7])[a // 4][DK * par:DK * par + DK, (a % 4) * P:(a % 4 + 1) * P],
                                             VB[:, h * DK:(h + 1) * DK], PT[:, h, :], start=True, stop=True)
                        last.then_inc(pv_mm, 1)
                    pe.wait_ge(xo_ok, at((b + 1) * 2 * NTB))
                    for a in range(XP):
                        last = pe.matmul(bank[0][:, :], Wo_sb[:, a, :], XO[:, a, :], start=a == 0, stop=a == XP - 1)
                    last.then_inc(wo_mm, 1)
                    pe.wait_ge(wo_ok, b + 1)
                    mean(m[5], mean_mm)
                    mean_square(b, 2)
                    pe.wait_ge(x2_ok, b + 1)
                    mean(m[4], mean_mm)
                    mean_square(b, 3)
                    pe.wait_ge(signs, 6)
                    pe.wait_ge(n_out, b * NORMS + 4)
                    for f in range(F2):
                        pe.matmul(bank[4 + f][:, :], w0_sb[:, 0, f * P:(f + 1) * P], m[3], start=True, stop=True)\
                            .then_inc(h1_mm, 1)
                    pe.wait_ge(h1_ok, (b + 1) * F2)
                    for f in range(F2):
                        for a in range(F2):
                            last = pe.matmul(bank[f][:, :], w1_sb[:, a, f * P:(f + 1) * P], H1[:, a, :],
                                             start=a == 0, stop=a == F2 - 1)
                        last.then_inc(h2_mm, 1)
                    for a in range(F2):
                        pe.wait_ge(h2_ok, b * F2 + a + 1)
                        last = pe.matmul(bank[4][:, :], w2_sb[:, a, :], H2[:, a, :], start=a == 0, stop=a == F2 - 1)
                    last.then_inc(h3_mm, 1)
                    pe.wait_ge(y_ok, b + 1)
                    for n in range(NTB):
                        last = pe.transpose(bank[5][:, n * P:(n + 1) * P], m[5][:, n * P:(n + 1) * P], ident[:, :])
                    last.then_inc(yt2_mm, 1)

            @block.scalar
            def _(ac):
                ac.wait_ge(ctx_mm, 1)
                ac.copy(ctxT, bank[0][:, 0:B * S].rearrange("p (b s) -> p b s", b=B)).then_inc(ctx_ok, 1)
                ac.wait_ge(kb_zero, 1)
                ac.wait_ge(ctx_ok, 1)
                ac.wait_ge(signs, 6)

                def root(b, k, eps):
                    ac.wait_ge(n_mm, b * NORMS + k + 1)
                    ac.activation(m[2], bank[3][:, :], ACT.Sqrt, bias=eps).then_inc(n_rt, 1)

                def square(b, k, src):
                    ac.activation(m[1], src, ACT.Square).then_inc(n_sq, 1)

                with ac.Fori(0, B) as b:
                    ac.wait_ge(row_done, at(b))
                    ac.wait_ge(u1_mm, b + 1)
                    ac.activation(m[0][0:R], bank[1][0:R, :], ACT.Sigmoid, bias=v("b_u1", 0, R)).then_inc(u1_sig, 1)
                    ac.wait_ge(u2_mm, b + 1)
                    ac.activation(m[2], bank[1][:, :], ACT.Sigmoid, bias=v("b_u2")).then_inc(gate_ok, 1)
                    ac.wait_ge(y1_ok, b + 1)
                    square(b, 0, m[3])
                    root(b, 0, epsr)
                    for f in range(FT):
                        if f == 1:
                            ac.wait_ge(stored, at(b * 16))
                        ac.wait_ge(ff_mm, b * FT + f + 1)
                        if f >= 2:
                            ac.wait_ge(ff_ok, b * FT + f - 1)
                        ac.activation(m[5 + f % 2], bank[4 + 2 * (f % 2)][:, :], ACT.Sigmoid).then_inc(ff_sig, 1)
                    ac.wait_ge(n_cen, b * CEN + 1)
                    square(b, 1, m[0])
                    root(b, 1, epsl)
                    ac.wait_ge(kb_mm, b + 1)
                    for j in range(2):
                        for par in range(2):
                            rows = slice(DK * par, DK * par + DK)
                            for a in range(4):
                                last = ac.activation(KB[rows, 4 * j + a, par, :],
                                                     bank[j][rows, a * S:(a + 1) * S], ACT.Identity,
                                                     bias=vec[rows, VEC["bk"][0] + 4 * j + a:VEC["bk"][0] + 4 * j + a + 1])
                            last.then_inc(kb_ok, 1)
                    ac.copy(cb, ctxT[:, bass.ds(b, 1), :].squeeze(1)).then_inc(cb_ok, 1)
                    for a in range(XP):
                        ac.wait_ge(q2_mm, b * XP + a + 1)
                        ac.activation(Q2[:, a, :], bank[4 + a % 4][:, :], ACT.Identity, bias=v("bq", a)).then_inc(q2_ok, 1)
                    ac.wait_ge(vb_mm, b + 1)
                    for j in range(2):
                        ac.copy(VB[:, j * 512:(j + 1) * 512], bank[2 + j][0:S, :]).then_inc(vb_ok, 1)
                    def exponent(n):
                        ac.wait_ge(sub_ok, at((b * NTB + n) * 3 + 3))
                        ac.activation(PR[:, n % 2], PR[:, n % 2], ACT.Exp, scale=DK ** -0.5).then_inc(exp_ok, 1)

                    exponent(0)
                    exponent(1)
                    for n in range(NTB):
                        i = b * NTB + n
                        ac.wait_ge(pv_mm, at(i))
                        for q in (0, 2):
                            ac.wait_ge(pt_mm, at(i * 4 + q + 1))
                            ac.copy(PT[:, 4 * q:4 * q + 4, :], bank[q % 3][0:S, :].rearrange("p (h t) -> p h t", h=4))\
                                .then_inc(pt_a, 1)
                        ac.wait_ge(pv_mm, at(i + 1))
                        for j in range(2):
                            for a in range(4):
                                last = ac.activation(XO[:, 4 * j + a, n * P:(n + 1) * P],
                                                     (bank[3], bank[7])[j][:, a * P:(a + 1) * P], ACT.Identity,
                                                     bias=v("bv", 4 * j + a))
                            last.then_inc(xo_ok, 1)
                        if n + 2 < NTB:
                            exponent(n + 2)
                    ac.wait_ge(n_cen, b * CEN + 2)
                    square(b, 2, m[0])
                    root(b, 2, epsl)
                    ac.wait_ge(n_cen, b * CEN + 3)
                    square(b, 3, m[0])
                    root(b, 3, epsl)
                    for f in range(F2):
                        ac.wait_ge(h1_mm, b * F2 + f + 1)
                        ac.activation(H1[:, f, :], bank[4 + f][:, :], ACT.Relu, scale=s0x2).then_inc(h1_ok, 1)
                    for f in range(F2):
                        ac.wait_ge(h2_mm, b * F2 + f + 1)
                        ac.activation(H2[:, f, :], bank[f][:, :], ACT.Relu, scale=s1x2).then_inc(h2_ok, 1)
                    ac.wait_ge(yt2_mm, b + 1)
                    ac.copy(m[6], bank[5][:, :]).then_inc(row_done, 1)

            @block.vector
            def _(ve):
                def invert(b, k):
                    ve.wait_ge(n_rt, b * NORMS + k + 1)
                    ve.reciprocal(m[2], m[2]).then_inc(n_inv, 1)
                    ve.wait_ge(n_inv, b * NORMS + k + 1)

                def centre(b, k, src):
                    ve.wait_ge(mean_mm, b * CEN + k + 1)
                    ve.tensor_tensor(m[0], src, bank[2][:, :], ALU.subtract).then_inc(n_cen, 1)

                ve.wait_ge(wout_ld, 16)
                for h in range(2 * HP):
                    ve.tensor_scalar(wout_sb[:, h, :], wout_sb[:, h, :], v("w_hn", h), None, ALU.mult)\
                        .then_inc(wout_ok, 1)
                with ve.Fori(0, B) as b:
                    tok = bass.ds(b * T, T)
                    ve.wait_ge(u1_sig, b + 1)
                    ve.scalar_tensor_tensor(m[1][0:R], bank[1][0:R, :], v("b_u1", 0, R), m[0][0:R],
                                            ALU.add, ALU.mult).then_inc(u1_ok, 1)
                    ve.wait_ge(gate_ok, b + 1)
                    ve.wait_ge(at_mm, b + 1)
                    ve.tensor_tensor(m[2], m[2], bank[0][:, :], ALU.mult).then_inc(gated, 1)
                    ve.wait_ge(gated, b + 1)
                    ve.tensor_tensor(m[3], m[2], zT[:, tok], ALU.add).then_inc(y1_ok, 1)
                    invert(b, 0)
                    ve.scalar_tensor_tensor(m[4], m[3], v("w_ffn"), m[2], ALU.mult, ALU.mult).then_inc(n_out, 1)
                    for f in range(FT):
                        g = m[5 + f % 2]
                        ve.wait_ge(ff_sig, b * FT + f + 1)
                        ve.tensor_tensor(g, g, bank[4 + 2 * (f % 2)][:, :], ALU.mult).then_inc(ff_mul, 1)
                        ve.wait_ge(ff_mul, b * FT + f + 1)
                        ve.tensor_tensor(FH[:, f, :], g, bank[5 + 2 * (f % 2)][:, :], ALU.mult).then_inc(ff_ok, 1)
                    ve.wait_ge(ff2_mm, b + 1)
                    ve.tensor_tensor(m[4], m[3], bank[0][:, :], ALU.add).then_inc(x1_ok, 1)
                    ve.wait_ge(x1_ok, b + 1)
                    centre(b, 0, m[4])
                    invert(b, 1)
                    ve.tensor_tensor(m[3], m[0], m[2], ALU.mult).then_inc(n_out, 1)
                    def less_max(n):
                        i = b * NTB + n
                        ve.wait_ge(pt_mm, at(i * 4 - 4)) if n >= 2 else ve.wait_ge(pt_mm, at(b * NTB * 4))
                        for j, (a0, na) in enumerate(NP3):
                            heads = slice(2 * a0, 2 * (a0 + na))
                            ps = bank[4 + j][:, 0:2 * na * S].rearrange("p (h s) -> p h s", s=S)
                            ve.wait_ge(sc_mm, i * 3 + j + 1)
                            ve.tensor_reduce(smx[:, n % 2, 0, heads], ps, AX.X, ALU.max).then_inc(mx_ok, 1)
                            ve.wait_ge(mx_ok, i * 3 + j + 1)
                            ve.tensor_tensor(PR[:, n % 2, heads, :], ps,
                                             smx[:, n % 2, 0, heads].unsqueeze(2).broadcast_to([P, 2 * na, S]),
                                             ALU.subtract).then_inc(sub_ok, 1)

                    def inverse_sum(n):
                        i = b * NTB + n
                        ve.wait_ge(exp_ok, i + 1)
                        ve.tensor_reduce(smx[:, n % 2, 1, :], PR[:, n % 2], AX.X, ALU.add).then_inc(sum_ok, 1)
                        ve.wait_ge(sum_ok, i + 1)
                        ve.reciprocal(smx[:, n % 2, 2, :], smx[:, n % 2, 1, :]).then_inc(inv_ok, 1)

                    less_max(0)
                    inverse_sum(0)
                    less_max(1)
                    for n in range(NTB):
                        i = b * NTB + n
                        if n + 1 < NTB:
                            inverse_sum(n + 1)
                        ve.wait_ge(pv_mm, at(i))
                        for q in (1, 3):
                            ve.wait_ge(pt_mm, at(i * 4 + q + 1))
                            ve.tensor_copy(PT[:, 4 * q:4 * q + 4, :],
                                           bank[q % 3][0:S, :].rearrange("p (h t) -> p h t", h=4)).then_inc(pt_v, 1)
                        if n + 2 < NTB:
                            less_max(n + 2)
                    ve.wait_ge(wo_mm, b + 1)
                    ve.scalar_tensor_tensor(m[5], bank[0][:, :], v("bo"), m[3], ALU.add, ALU.add).then_inc(wo_ok, 1)
                    ve.wait_ge(wo_ok, b + 1)
                    centre(b, 1, m[5])
                    invert(b, 2)
                    ve.tensor_tensor(m[3], m[0], m[2], ALU.mult).then_inc(n_out, 1)
                    ve.wait_ge(n_out, b * NORMS + 3)
                    ve.tensor_scalar(m[3], m[3], v("ln_gamma"), v("ln_beta"), ALU.mult, ALU.add).then_inc(ln_sc, 1)
                    ve.wait_ge(ln_sc, b + 1)
                    ve.tensor_tensor(m[4], m[4], m[3], ALU.add).then_inc(x2_ok, 1)
                    ve.wait_ge(x2_ok, b + 1)
                    centre(b, 2, m[4])
                    invert(b, 3)
                    ve.tensor_tensor(m[3], m[0], m[2], ALU.mult).then_inc(n_out, 1)
                    ve.wait_ge(h3_mm, b + 1)
                    ve.scalar_tensor_tensor(m[5], bank[4][:, :], v("s2"), m[4], ALU.mult, ALU.add).then_inc(y_ok, 1)


_OUT = "out_dram"


def pack_vectors(a, np):
    rows = {
        "conv_w": a["L0_attn_conv_w"], "conv_b": a["L0_attn_conv_b"][:, None],
        "w_norm": a["L0_attn_w_norm_in"][:, None], "b_ad": a["L0_attn_b_ad"].reshape(-1, P).T,
        "alpha_spike": a["L0_attn_alpha_spike"].reshape(-1, P).T,
        "beta_spike": a["L0_attn_beta_spike"].reshape(-1, P).T,
        "b_au": a["L0_attn_b_au"][:, None], "b_u1": a["L0_attn_b_u1"][:, None],
        "b_u2": a["L0_attn_b_u2"][:, None], "w_hn": a["L0_attn_w_hn"].T,
        "w_ffn": a["L0_attn_w_ffn"][:, None],
        "b_beta": np.repeat(a["L0_attn_b_beta"], 64).reshape(-1, P).T,
        "bq": a["L0_xattn_bq"].reshape(-1, P).T, "bk": a["L0_xattn_bk"].reshape(-1, P).T,
        "bv": a["L0_xattn_bv"].reshape(-1, P).T, "bo": a["L0_xattn_bo"][:, None],
        "ln_gamma": a["L0_xattn_ln_gamma"][:, None], "ln_beta": a["L0_xattn_ln_beta"][:, None],
        "s0": np.repeat(a["L0_ffn_s0"].reshape(1, 1), P, 0), "s1": np.repeat(a["L0_ffn_s1"].reshape(1, 1), P, 0),
        "s2": np.repeat(a["L0_ffn_s2"].reshape(1, 1), P, 0),
    }
    packed = np.zeros((P, NVEC), np.float32)
    for name, (at, n) in VEC.items():
        r = rows[name]
        packed[:r.shape[0], at:at + n] = r
    return packed


def kernel(**inputs):
    import numpy as np
    import concourse.bacc as bacc
    from concourse.bass_utils import run_bass_kernel_spmd

    a = {n: np.ascontiguousarray(t) for n, t in inputs.items()}
    arrays = {"x": a["x"], "ctx": a["ctx_1024"], "vec": pack_vectors(a, np)}
    for n in ("wq", "wk", "w_spike", "wv", "w_out", "w_au", "w_ad", "w_beta", "w_u1", "w_u2",
              "w_ff1", "w_ff3", "w_ff2"):
        arrays[n] = a["L0_attn_" + n]
    for n in ("Wq", "Wk", "Wv", "Wo"):
        arrays["x_" + n] = a["L0_xattn_" + n]
    for n in ("k0", "k1", "k2"):
        arrays[n] = a["L0_ffn_" + n]
    nc = bacc.Bacc("TRN2", target_bir_lowering=False, num_devices=1)
    arrays = {f"in_{n}_dram": t for n, t in arrays.items()}
    args = [nc.dram_tensor(n, t.shape, mybir.dt.from_np(t.dtype), kind="ExternalInput").ap()
            for n, t in arrays.items()]
    args.append(nc.dram_tensor(_OUT, a["x"].shape, F32, kind="ExternalOutput").ap())
    decoder_kernel(nc, *args)
    return run_bass_kernel_spmd(nc, [arrays], core_ids=[0]).results[0][_OUT]
```

```python
from contextlib import ExitStack

import concourse.bass as bass
from concourse import mybir

P = 128
F32 = mybir.dt.float32
U32 = mybir.dt.uint32
U8 = mybir.dt.uint8
ACT = mybir.ActivationFunctionType
ALU = mybir.AluOpType
AX = mybir.AxisListType

VEC = {}
_at = 0
for _name, _n in (("conv_w", 4), ("conv_b", 1), ("w_norm", 1), ("b_ad", 4), ("alpha_spike", 4),
                  ("beta_spike", 4), ("b_au", 1), ("b_u1", 1), ("b_u2", 1), ("w_hn", 8), ("w_ffn", 1),
                  ("b_beta", 4), ("bq", 8), ("bk", 8), ("bv", 8), ("bo", 1), ("ln_gamma", 1),
                  ("ln_beta", 1), ("s0", 1), ("s1", 1), ("s2", 1)):
    VEC[_name] = (_at, _n)
    _at += _n
NVEC = _at


def decoder_kernel(nc, x, ctx_in, vec_in, wq, wk, w_spike, wv, w_out, w_au, w_ad, w_beta, w_u1, w_u2,
                   w_ff1, w_ff3, w_ff2, Wq, Wk, Wv, Wo, k0, k1, k2, out):
    B, T, D = x.shape
    TOK = B * T
    NT = TOK // P
    DK, DV = 64, 128
    HP = wq.shape[1] // P
    C = 64
    NC = T // C
    LEVELS = 6
    R = w_au.shape[1]
    FT = w_ff1.shape[1] // P
    XP = Wq.shape[1] // P
    XH = 2 * XP
    S = ctx_in.shape[1]
    CTX = B * S
    assert D == P and 2 * DK == P and DV == P and T == 512 and HP == 4 and XP == 8

    ctx = ExitStack()
    with ctx:
        def sb(name, shape, dt=F32):
            return ctx.enter_context(nc.sbuf_tensor(name, shape, dt))

        def sem(name):
            return ctx.enter_context(nc.semaphore(name))

        bank = [ctx.enter_context(nc.psum_tensor(f"bank{i}", [P, 512], F32)) for i in range(8)]

        qT = sb("qT", [P, HP, TOK])
        kT = sb("kT", [P, HP, TOK])
        gates = sb("gates", [P, 2, HP, TOK])
        aT, bT = gates[:, 0], gates[:, 1]
        zT = sb("zT", [P, TOK])
        hT = sb("hT", [P, TOK])
        wv_sb = sb("wv_sb", [P, HP, 2, DV])
        wu1_sb = sb("wu1_sb", [P, R])
        wu2_sb = sb("wu2_sb", [R, D])
        ident = sb("ident", [P, P])
        bdones = sb("bdones", [P, P])
        mean_w = sb("mean_w", [P, P])
        mask = sb("mask", [P, LEVELS, P])
        vec = sb("vec", [P, NVEC])
        WORK = 13200
        work = sb("work", [P, WORK])
        used = [0]

        def region(shape, of=work, cursor=used):
            n = 1
            for s in shape:
                n *= s
            flat = of[:, cursor[0]:cursor[0] + n]
            cursor[0] += n
            assert cursor[0] <= of.shape[1], cursor
            names = "abcd"[:len(shape)]
            if len(shape) == 1:
                return flat
            sizes = {c: s for c, s in zip(names[1:], shape[1:])}
            return flat.rearrange(f"p ({' '.join(names)}) -> p {' '.join(names)}", **sizes)

        def v(name, i=0, rows=P):
            return vec[0:rows, VEC[name][0] + i:VEC[name][0] + i + 1]

        primed = [sem("au_ok"), sem("sq_ok"), sem("ss_mm"), sem("bc_ok"), sem("qk_ok"), sem("nrm_inv"),
                  sem("beta_ok"), sem("beta_mm"), sem("al0_ok"), sem("row_done"), sem("sub_ok"), sem("pt_v"),
                  sem("pt_a"), sem("xo_ok"), sem("stored"), sem("pv_mm"), sem("pt_mm")]
        (au_ok, sq_ok, ss_mm, bc_ok, qk_ok, nrm_inv, beta_ok, beta_mm, al0_ok, row_done, sub_ok,
         pt_v, pt_a, xo_ok, stored, pv_mm, pt_mm) = primed

        def at(n):
            return n + 1

        used[0] = 0
        wq_sb = region([HP, P])
        wk_sb = region([HP, P])
        wsp_sb = region([HP, P])
        wad_sb = region([HP, P])[0:R]
        wau_sb = region([R])
        wbeta_sb = region([2 * HP])
        wbeta_rep = region([HP, 2, DK])
        bspike_bd = region([HP, P])
        auT = region([TOK])[0:R]
        early_end = used[0]
        PAD = 3
        h0T = region([B, T + PAD])
        xn = bT.rearrange("p a t -> p (a t)")[:, 0:TOK].rearrange("p (n d) -> p n d", n=NT)
        zn = bT.rearrange("p a t -> p (a t)")[:, TOK:2 * TOK].rearrange("p (n d) -> p n d", n=NT)
        hn = bT.rearrange("p a t -> p (a t)")[:, 2 * TOK:3 * TOK].rearrange("p (n d) -> p n d", n=NT)
        sqn = bT.rearrange("p a t -> p (a t)")[:, 3 * TOK:4 * TOK].rearrange("p (n d) -> p n d", n=NT)
        conv = xn.rearrange("p n d -> p (n d)").rearrange("p (b t) -> p b t", b=B)
        sig = sqn.rearrange("p n d -> p (n d)").rearrange("p (b t) -> p b t", b=B)
        mom = sb("mom", [P, 6, NT])
        half = sb("half", [P, NT])

        w_loaded = sem("w_loaded")
        x_loaded = sem("x_loaded")
        consts = sem("consts")
        setup = sem("setup")
        vn = sem("vn")
        pn = sem("pn")
        an = sem("an")
        tr_mm = sem("tr_mm")
        tr_out = sem("tr_out")
        conv_ok = sem("conv_ok")
        sig_ok = sem("sig_ok")
        h_ok = sem("h_ok")

        with nc.Block() as block:
            @block.sync
            def _(sp):
                sp.dma_start(xn, x.rearrange("b t d -> (b t) d").rearrange("(n p) d -> p n d", p=P))\
                    .then_inc(x_loaded, 16)
                sp.dma_start(vec[:, :], vec_in).then_inc(w_loaded, 16)
                for dst, src in ((wsp_sb, w_spike.rearrange("d (a n) -> d a n", a=HP)),
                                 (wq_sb, wq.rearrange("d (a n) -> d a n", a=HP)),
                                 (wk_sb, wk.rearrange("d (a n) -> d a n", a=HP)),
                                 (wau_sb, w_au), (wad_sb, w_ad.rearrange("d (a n) -> d a n", a=HP)),
                                 (wbeta_sb, w_beta),
                                 (wv_sb[:, :, :, :], wv.rearrange("d (a b n) -> d a b n", a=HP, b=2)),
                                 (wu1_sb[:, :], w_u1), (wu2_sb[:, :], w_u2)):
                    sp.dma_start(dst, src).then_inc(w_loaded, 16)

            @block.gpsimd
            def _(gp):
                for s in primed:
                    gp.sem_inc(s, 1)
                gp.memset(half[:, :], -0.5).then_inc(consts, 1)
                gp.memset(h0T[:, :, 0:PAD], 0.0).then_inc(consts, 1)
                gp.memset(mean_w[:, :], 1.0 / D).then_inc(consts, 1)
                gp.memset(ident[:, :], 0.0).then_inc(consts, 1)
                gp.memset(bdones[:, :], 1.0).then_inc(consts, 1)
                gp.memset(mask[:, :, :], 0.0).then_inc(consts, 1)
                gp.wait_ge(consts, 6)
                gp.affine_select(out=ident[:, :], in_=ident[:, :], compare_op=ALU.not_equal, fill=1.0,
                                 base=0, pattern=[[-1, P]], channel_multiplier=1).then_inc(consts, 1)

                def keep_block(t, step, n, width, size, done):
                    gp.affine_select(out=t, in_=t, compare_op=ALU.is_ge, fill=0.0, base=0,
                                     pattern=[[-step, n], [0, width]], channel_multiplier=1).then_inc(consts, 1)
                    gp.wait_ge(consts, done + 1)
                    gp.affine_select(out=t, in_=t, compare_op=ALU.is_ge, fill=0.0, base=size - 1,
                                     pattern=[[step, n], [0, width]], channel_multiplier=-1).then_inc(consts, 1)

                keep_block(bdones[:, :].rearrange("p (a t) -> p a t", a=2), C, 2, C, C, 7)
                done = 9
                for l in range(LEVELS):
                    L = 1 << l
                    late = mask[:, l, :].rearrange("p (j s t) -> p j s t", s=2, t=L)[:, :, 1, :]
                    gp.memset(late, 1.0).then_inc(consts, 1)
                    gp.wait_ge(consts, done + 1)
                    keep_block(late, 2 * L, P // (2 * L), L, L, done + 1)
                    done += 3
                for i, (src, dst) in enumerate(((1, 2), (3, 4))):
                    gp.wait_ge(vn, (4, 8)[i])
                    gp.tensor_tensor(mom[:, dst, :], mom[:, src, :], half[:, :], ALU.pow).then_inc(pn, 1)

            N_CONST = 9 + 3 * LEVELS

            @block.vector
            def _(ve):
                ve.wait_ge(x_loaded, 16)
                ve.tensor_reduce(mom[:, 0, :], xn, AX.X, ALU.add).then_inc(vn, 1)
                ve.wait_ge(vn, 1)
                ve.tensor_scalar(mom[:, 5, :], mom[:, 0, :], 1.0 / D, None, ALU.mult).then_inc(vn, 1)
                ve.wait_ge(vn, 2)
                ve.tensor_tensor(zn, xn, mom[:, 5, :].unsqueeze(2).broadcast_to([P, NT, D]),
                                 ALU.subtract).then_inc(vn, 1)
                ve.wait_ge(an, 1)
                ve.tensor_reduce(mom[:, 0, :], sqn, AX.X, ALU.add).then_inc(setup, 1)
                ve.wait_ge(setup, 1)
                ve.tensor_scalar(mom[:, 1, :], mom[:, 0, :], 1.0 / D, 1e-5, ALU.mult, ALU.add).then_inc(vn, 1)
                ve.wait_ge(pn, 1)
                ve.tensor_tensor(zn, zn, mom[:, 2, :].unsqueeze(2).broadcast_to([P, NT, D]),
                                 ALU.mult).then_inc(vn, 1)
                ve.wait_ge(vn, 5)
                ve.tensor_tensor(sqn, zn, zn, ALU.mult).then_inc(vn, 1)
                ve.wait_ge(vn, 6)
                ve.tensor_reduce(mom[:, 0, :], sqn, AX.X, ALU.add).then_inc(vn, 1)
                ve.wait_ge(vn, 7)
                ve.tensor_scalar(mom[:, 3, :], mom[:, 0, :], 1.0 / D, 1e-6, ALU.mult, ALU.add).then_inc(vn, 1)
                ve.wait_ge(pn, 2)
                ve.tensor_tensor(hn, zn, mom[:, 4, :].unsqueeze(2).broadcast_to([P, NT, D]),
                                 ALU.mult).then_inc(vn, 1)
                ve.wait_ge(tr_out, NT // 4)
                ve.wait_ge(w_loaded, 16 * 10)
                for b in range(B):
                    ve.tensor_scalar(conv[:, b], h0T[:, b, 0:T], v("conv_w", 0), v("conv_b"), ALU.mult, ALU.add)\
                        .then_inc(conv_ok, 1)
                for j in range(1, PAD + 1):
                    for b in range(B):
                        ve.wait_ge(conv_ok, B * (j - 1) + b + 1)
                        ve.scalar_tensor_tensor(conv[:, b], h0T[:, b, j:j + T], v("conv_w", j), conv[:, b],
                                                ALU.mult, ALU.add).then_inc(conv_ok, 1)
                for b in range(B):
                    ve.wait_ge(sig_ok, b + 1)
                    ve.tensor_tensor(hT[:, b * T:(b + 1) * T], conv[:, b], sig[:, b], ALU.mult).then_inc(h_ok, 1)
                ve.tensor_copy(wbeta_rep, wbeta_sb.rearrange("p (a b) -> p a b", b=2).unsqueeze(3)
                               .broadcast_to([P, HP, 2, DK])).then_inc(setup, 1)
                for hp in range(HP):
                    ve.tensor_scalar(bspike_bd[:, hp, :], bdones[:, :], v("beta_spike", hp), None, ALU.mult)\
                        .then_inc(setup, 1)

            @block.scalar
            def _(ac):
                ac.wait_ge(vn, 3)
                ac.activation(sqn, zn, ACT.Square).then_inc(an, 1)
                for n in range(NT // 4):
                    ac.wait_ge(tr_mm, n + 1)
                    ac.copy(zT[:, n * 512:(n + 1) * 512], bank[n][:, :])
                ac.wait_ge(w_loaded, 16 * 10)
                ac.wait_ge(consts, 2)
                for b in range(B):
                    ac.wait_ge(tr_mm, NT // 4 + b + 1)
                    ac.activation(h0T[:, b, PAD:], bank[4 + b][:, :], ACT.Copy, scale=v("w_norm")).then_inc(tr_out, 1)
                for b in range(B):
                    ac.wait_ge(conv_ok, B * PAD + b + 1)
                    ac.activation(sig[:, b], conv[:, b], ACT.Sigmoid).then_inc(sig_ok, 1)

            @block.tensor
            def _(pe):
                pe.wait_ge(consts, N_CONST)
                pe.wait_ge(x_loaded, 16)
                for k, (src, ready) in enumerate(((zn, 5), (hn, 9))):
                    pe.wait_ge(vn, ready)
                    for n in range(NT // 4):
                        for j in range(4):
                            last = pe.transpose(bank[4 * k + n][:, j * P:(j + 1) * P],
                                                src[:, 4 * n + j, :], ident[:, :])
                        last.then_inc(tr_mm, 1)

        sd_mm = sem("sd_mm")
        sd_ok = sem("sd_ok")

        with nc.Block() as block:
            @block.tensor
            def _(pe):
                for n in range(B * HP):
                    b, hp = n // HP, n % HP
                    if n >= len(bank):
                        pe.wait_ge(sd_ok, n - len(bank) + 1)
                    pe.matmul(bank[n % len(bank)][:, :], wsp_sb[:, hp, :], hT[:, b * T:(b + 1) * T],
                              start=True, stop=True).then_inc(sd_mm, 1)

            @block.scalar
            def _(ac):
                for n in range(B * HP):
                    b, hp = n // HP, n % HP
                    ac.wait_ge(sd_mm, n + 1)
                    ac.mul(aT[:, hp, b * T:(b + 1) * T], bank[n % len(bank)][:, :], 2.0).then_inc(sd_ok, 1)

        used[0] = early_end
        NQK = 2 * HP
        sq_buf = region([2, T])
        inv_bc = region([2, T])
        nrm = region([T])[0:2 * NQK]
        nrm_e = region([T])[0:2 * NQK]
        au_sig = region([T])[0:R]
        pick = region([NQK, 2 * NQK])
        spread = region([NQK, P])[0:2 * NQK]
        neg_mem = mom[:, 0:2, :].rearrange("p a n -> p (a n)")[:, 0:HP * B]
        mem = aT.rearrange("p a (b t) -> p (a b) t", b=B)
        STEPS = T // B // 2
        win = bT.rearrange("p a t -> p (a t)")[:, 0:2 * HP * B * STEPS].rearrange("p (w n t) -> p w n t", w=2, t=STEPS)

        waited = sem("waited")
        mconst = sem("mconst")
        au_mm, au_sg = sem("au_mm"), sem("au_sg")
        qk_mm, raw_ok = sem("qk_mm"), sem("raw_ok")
        nrm_ok, nrm_add = sem("nrm_ok"), sem("nrm_add")
        bc_mm = sem("bc_mm")
        charged = sem("charged")
        win_in, win_out = sem("win_in"), sem("win_out")
        fired = sem("fired")

        def qk_dst(j, tok):
            return (qT if j < HP else kT)[:, j % HP, tok]

        with nc.Block() as block:
            @block.vector
            def _(ve):
                ve.memset(neg_mem, 0.0).then_inc(fired, 1)
                with ve.Fori(0, B) as b:
                    def window(w):
                        done = (2 * b + w) * STEPS
                        ve.wait_ge(win_in, 2 * b + w + 1)
                        for j in range(STEPS):
                            now = win[:, w, :, j]
                            ve.wait_ge(fired, done + j + 1)
                            ve.scalar_tensor_tensor(now, neg_mem, -0.9, now, ALU.mult, ALU.add).then_inc(charged, 1)
                            ve.wait_ge(charged, done + j + 1)
                            ve.scalar_tensor_tensor(neg_mem, now, 1.0, now, ALU.is_gt, ALU.subtract)\
                                .then_inc(fired, 1)

                    window(0)
                    ve.wait_ge(au_sg, b + 1)
                    ve.scalar_tensor_tensor(auT[:, bass.ds(b * T, T)], bank[7][0:R, :], v("b_au", 0, R), au_sig,
                                            ALU.add, ALU.mult).then_inc(au_ok, 1)
                    ve.wait_ge(nrm_ok, b + 1)
                    ve.tensor_scalar(nrm_e, nrm, 1e-6, None, ALU.add).then_inc(nrm_add, 1)
                    ve.wait_ge(nrm_add, b + 1)
                    ve.reciprocal(nrm_e, nrm_e).then_inc(nrm_inv, 1)
                    window(1)

            @block.tensor
            def _(pe):
                pe.wait_ge(mconst, 6)
                with pe.Fori(0, B) as b:
                    tok = bass.ds(b * T, T)
                    pe.wait_ge(au_ok, at(b))
                    pe.matmul(bank[7][0:R, :], wau_sb[:, :], hT[:, tok], start=True, stop=True).then_inc(au_mm, 1)

                    def add_squares(j):
                        pe.wait_ge(sq_ok, at(b * NQK + j + 1))
                        pe.matmul(bank[4][0:2 * NQK, :], pick[:, j, :], sq_buf[:, j % 2, :],
                                  start=j == 0, stop=j == NQK - 1).then_inc(ss_mm, 1)

                    for j in range(NQK):
                        pe.wait_ge(sq_ok, at(b * NQK + j - 3)) if j >= 4 else pe.wait_ge(sq_ok, at(b * NQK))
                        pe.matmul(bank[j % 4][:, :], (wq_sb if j < HP else wk_sb)[:, j % HP, :], hT[:, tok],
                                  start=True, stop=True).then_inc(qk_mm, 1)
                        if j >= 1:
                            add_squares(j - 1)
                    add_squares(NQK - 1)
                    pe.wait_ge(nrm_inv, at(b + 1))
                    for j in range(NQK):
                        pe.wait_ge(bc_ok, at(b * NQK + j - 1)) if j >= 2 else pe.wait_ge(bc_ok, at(b * NQK))
                        pe.matmul(bank[5 + j % 2][:, :], spread[:, j, :], nrm_e, start=True, stop=True)\
                            .then_inc(bc_mm, 1)

            @block.scalar
            def _(ac):
                with ac.Fori(0, B) as b:
                    tok = bass.ds(b * T, T)
                    ac.wait_ge(au_mm, b + 1)
                    ac.activation(au_sig, bank[7][0:R, :], ACT.Sigmoid, bias=v("b_au", 0, R)).then_inc(au_sg, 1)
                    for j in range(NQK):
                        ac.wait_ge(qk_mm, b * NQK + j + 1)
                        ac.copy(qk_dst(j, tok), bank[j % 4][:, :]).then_inc(raw_ok, 1)
                        ac.wait_ge(ss_mm, at(b * NQK + j - 1)) if j >= 2 else ac.wait_ge(ss_mm, at(b * NQK))
                        ac.activation(sq_buf[:, j % 2, :], bank[j % 4][:, :], ACT.Square).then_inc(sq_ok, 1)
                    ac.wait_ge(ss_mm, at((b + 1) * NQK))
                    ac.wait_ge(nrm_inv, at(b))
                    ac.activation(nrm, bank[4][0:2 * NQK, :], ACT.Sqrt).then_inc(nrm_ok, 1)
                    for j in range(NQK):
                        ac.wait_ge(bc_mm, b * NQK + j + 1)
                        ac.wait_ge(qk_ok, at(b * NQK + j - 1)) if j >= 2 else ac.wait_ge(qk_ok, at(b * NQK))
                        ac.copy(inv_bc[:, j % 2, :], bank[5 + j % 2][:, :]).then_inc(bc_ok, 1)

            @block.gpsimd
            def _(gp):
                gp.tensor_copy(win[:, 0], mem[:, :, 0:STEPS]).then_inc(win_in, 1)
                gp.memset(pick, 0.0).then_inc(mconst, 1)
                gp.memset(spread, 1.0).then_inc(mconst, 1)
                gp.wait_ge(mconst, 2)
                sp_v = spread.rearrange("r j (x d) -> r (j x) d", x=2)
                gp.affine_select(out=sp_v, in_=sp_v, compare_op=ALU.is_equal, fill=0.0, base=0,
                                 pattern=[[-1, 2 * NQK], [0, DK]], channel_multiplier=1).then_inc(mconst, 1)
                for par in range(2):
                    gp.wait_ge(mconst, 3 + par)
                    for j in range(NQK):
                        last = gp.tensor_copy(pick[:, j, 2 * j + par:2 * j + par + 1], bdones[:, C * par:C * par + 1])
                    last.then_inc(mconst, 1)
                gp.wait_ge(mconst, 5)
                gp.sem_inc(mconst, 1)
                gp.tensor_copy(win[:, 1], mem[:, :, STEPS:2 * STEPS]).then_inc(win_in, 1)
                with gp.Fori(0, B) as b:
                    tok = bass.ds(b * T, T)

                    def change(w):
                        gp.wait_ge(fired, (2 * b + w + 1) * STEPS + 1)
                        gp.sem_inc(waited, 1)
                        gp.tensor_copy(mem[:, :, bass.ds((2 * b + w) * STEPS, STEPS)], win[:, w]).then_inc(win_out, 1)
                        gp.wait_ge(win_out, 2 * b + w + 1)
                        gp.sem_inc(waited, 1)
                        gp.tensor_copy(win[:, w], mem[:, :, bass.ds((b + 1) % B * 2 * STEPS + w * STEPS, STEPS)])\
                            .then_inc(win_in, 1)

                    change(0)
                    for j in range(NQK):
                        gp.wait_ge(bc_ok, at(b * NQK + j + 1))
                        gp.tensor_tensor(qk_dst(j, tok), qk_dst(j, tok), inv_bc[:, j % 2, :], ALU.mult)\
                            .then_inc(qk_ok, 1)
                    change(1)

        used[0] = early_end
        spk = region([2, 512])
        zal = region([2, 512])
        al0 = region([2, 512])
        be0 = region([2, 512])
        NG = HP
        spk_ok = sem("spk_ok")
        cnt_mm = sem("cnt_mm")
        ab_mm = sem("ab_mm")
        zal_ok = sem("zal_ok")
        be0_ok = sem("be0_ok")
        alpha_ok = sem("alpha_ok")

        with nc.Block() as block:
            @block.tensor
            def _(pe):
                with pe.Fori(0, B) as b:
                    tok = bass.ds(b * T, T)
                    for g in range(NG):
                        n, s = b * NG + g, g % 2
                        pe.wait_ge(beta_ok, at(n - 1)) if g else pe.wait_ge(beta_ok, at(n))
                        pe.matmul(bank[4 * s + 2][:, :], wbeta_rep[:, g].rearrange("p a b -> p (a b)"),
                                  hT[:, tok], start=True, stop=False)
                        pe.matmul(bank[4 * s][:, :], wad_sb[:, g, :], auT[:, tok], start=True, stop=True)\
                            .then_inc(ab_mm, 1)
                        pe.wait_ge(spk_ok, n + 1)
                        pe.matmul(bank[4 * s + 1][:, :], bdones[:, :], spk[:, s, :], start=True, stop=True)\
                            .then_inc(cnt_mm, 1)
                        pe.matmul(bank[4 * s + 2][:, :], bspike_bd[:, g, :], spk[:, s, :],
                                  start=False, stop=True).then_inc(beta_mm, 1)

            @block.vector
            def _(ve):
                ve.tensor_scalar(spk[:, 0, :], aT[:, 0, 0:T], 1.0, None, ALU.is_gt).then_inc(spk_ok, 1)
                with ve.Fori(0, B) as b:
                    tok = bass.ds(b * T, T)
                    for g in range(NG):
                        n, s = b * NG + g, g % 2
                        g1, tok1 = (g + 1, tok) if g + 1 < NG else (0, bass.ds((b + 1) % B * T, T))
                        ve.wait_ge(beta_mm, at(n))
                        ve.tensor_scalar(spk[:, 1 - s, :], aT[:, g1, tok1], 1.0, None, ALU.is_gt).then_inc(spk_ok, 1)
                        ve.wait_ge(spk_ok, n + 1)
                        ve.wait_ge(ab_mm, n + 1)
                        ve.wait_ge(al0_ok, at(n - 1)) if g >= 2 else ve.wait_ge(al0_ok, at(b * NG))
                        ve.scalar_tensor_tensor(zal[:, s, :], spk[:, s, :], v("alpha_spike", g), bank[4 * s][:, :],
                                                ALU.mult, ALU.add).then_inc(zal_ok, 1)
                        ve.wait_ge(cnt_mm, n + 1)
                        ve.wait_ge(al0_ok, at(n + 1))
                        ve.scalar_tensor_tensor(aT[:, g, tok], bank[4 * s + 1][:, :], 0.0, al0[:, s, :],
                                                ALU.is_equal, ALU.max).then_inc(alpha_ok, 1)
                        ve.wait_ge(be0_ok, n + 1)
                        ve.scalar_tensor_tensor(bT[:, g, tok], bank[4 * s + 1][:, :], 0.0, be0[:, s, :],
                                                ALU.is_gt, ALU.mult).then_inc(beta_ok, 1)

            @block.scalar
            def _(ac):
                with ac.Fori(0, B) as b:
                    for g in range(NG):
                        n, s = b * NG + g, g % 2
                        ac.wait_ge(zal_ok, n + 1)
                        ac.wait_ge(beta_ok, at(n - 1)) if g >= 2 else ac.wait_ge(beta_ok, at(b * NG))
                        ac.activation(al0[:, s, :], zal[:, s, :], ACT.Sigmoid, bias=v("b_ad", g)).then_inc(al0_ok, 1)
                        ac.wait_ge(beta_mm, at(n + 1))
                        ac.activation(be0[:, s, :], bank[4 * s + 2][:, :], ACT.Sigmoid, bias=v("b_beta", g))\
                            .then_inc(be0_ok, 1)

        used[0] = 0
        state = region([B, HP, DV])
        KS = region([HP, 2, C])
        KQ2 = region([2, 2, HP, C])
        KPn = region([HP, 2, C])
        QPb = region([HP, 2, C])
        AQ2 = region([2, HP, 2, C])
        NE = LEVELS
        E = region([NE, HP, P])
        XY = region([2, 2, 2, P])
        Z = region([2, 2, P])
        KSn = region([2, HP, P])
        res = region([HP, DV])
        U = region([HP, DV])
        On = res
        hc = region([C])
        decay = region([B, HP])
        tot = region([HP * 2 * C])
        ms = mom[:, 0:4, 0:HP]
        tot_at = [2 * HP * (C - (2 * C >> l)) for l in range(LEVELS)]
        tot_of = [None] + [tot[:, tot_at[l]:tot_at[l] + (2 * HP * C >> l)].rearrange("p (a x j) -> p a x j", a=HP, x=2)
                           for l in range(1, LEVELS)]
        G = 2
        GP = HP // G
        psL, psZ, psXY, psR, psO = bank[0:2], bank[2:4], bank[4:6], bank[6], bank[7]

        zeroed = sem("zeroed")
        kq_ok = sem("kq_ok")
        ks_ok = sem("ks_ok")
        tot_ok = sem("tot_ok")
        lvl_mm = sem("lvl_mm")
        diag_mm = sem("diag_mm")
        e_ok = sem("e_ok")
        aq_ok = sem("aq_ok")
        x_init = sem("x_init")
        xt0_mm = sem("xt0_mm")
        xy_ok = sem("xy_ok")
        z_mm = sem("z_mm")
        z_ok = sem("z_ok")
        dxy_mm = sem("dxy_mm")
        xt_mm, y_new = sem("xt_mm"), sem("y_new")
        hc_ok = sem("hc_ok")
        kpn_ok = sem("kpn_ok")
        qpb_ok = sem("qpb_ok")
        ksn_mm = sem("ksn_mm")
        ksn_ok = sem("ksn_ok")
        res_mm = sem("res_mm")
        res_ok = sem("res_ok")
        u_mm = sem("u_mm")
        u_ok = sem("u_ok")
        o_mm = sem("o_mm")
        o_sq = sem("o_sq")
        ms_ok = sem("ms_ok")
        rr_ok = sem("rr_ok")
        s_mm = sem("s_mm")
        s_ok = sem("s_ok")
        on_ok = sem("on_ok")
        dec_ok = sem("dec_ok")
        yout_mm = sem("yout_mm")
        yout_ok = sem("yout_ok")
        NKQ = LEVELS + 1
        NTOT = LEVELS - 1
        NKS = LEVELS + 2
        NINV = LEVELS - 1

        def halves(t):
            return [t[C * par:C * par + C, :, par, :] for par in range(2)]

        def member(n, l, k):
            if l == 0:
                return aT[:, :, n.tok].rearrange("p a (j s) -> p a j s", s=2)[:, :, :, k].unsqueeze(2)\
                    .broadcast_to([P, HP, 2, C // 2])
            return tot_of[l].rearrange("p a x (j s) -> p a x j s", s=2)[:, :, :, :, k]

        def flat(t, hp):
            return t[:, hp].rearrange("p x t -> p (x t)")

        class Round:
            def __init__(self, c, b):
                self.it, self.b, self.slot = c * B + b, b, b % 2
                self.tok = bass.ds(b * T + c * C, C) if not isinstance(c, int) else \
                    slice(b * T + c * C, b * T + c * C + C)

        def early(n, k):
            return isinstance(n.it, int) and n.it < k

        def rounds(eng, body, finish):
            def chunk(c, first, last):
                for b in range(B):
                    nxt = Round(c, b + 1) if b + 1 < B else None if last else Round(c + 1, 0)
                    if nxt:
                        nxt.after = Round(c, b + 2) if b + 2 < B else None if last else Round(c + 1, b + 2 - B)
                    prev = Round(c, b - 1) if b else None if first else Round(c - 1, B - 1)
                    body(Round(c, b), nxt, prev)

            chunk(0, True, False)
            with eng.Fori(1, NC - 1) as c:
                chunk(c, False, False)
            chunk(NC - 1, False, True)
            finish(Round(NC - 1, B - 1))

        psLv = [t[:, :].rearrange("p (a x t) -> p a x t", a=HP, x=2) for t in psL]

        with nc.Block() as block:
            @block.gpsimd
            def _(gp):
                for t in (state, KS, KPn, QPb):
                    gp.memset(t, 0.0).then_inc(zeroed, 1)
                gp.memset(ms[:, 2, :], -0.5).then_inc(zeroed, 1)
                gp.memset(ms[:, 3, :], 1e-6).then_inc(zeroed, 1)
                gp.wait_ge(zeroed, 6)

                def products(n):
                    gp.sem_inc(waited, 1)
                    for l in range(NTOT):
                        if l:
                            gp.wait_ge(tot_ok, n.it * NTOT + l)
                        gp.tensor_tensor(tot_of[l + 1], member(n, l, 0), member(n, l, 1), ALU.mult).then_inc(tot_ok, 1)

                def total(n):
                    gp.wait_ge(tot_ok, (n.it + 1) * NTOT)
                    gp.tensor_tensor(decay[:, n.b, :], tot_of[NTOT][:, :, 0, 0], tot_of[NTOT][:, :, 0, 1],
                                     ALU.mult).then_inc(dec_ok, 1)

                def keys(n):
                    if not early(n, 1):
                        gp.wait_ge(ksn_mm, n.it)
                    for par, dst in enumerate(halves(KS)):
                        rows = slice(C * par, C * par + C)
                        gp.tensor_tensor(dst, kT[rows, :, n.tok], bT[rows, :, n.tok], ALU.mult).then_inc(ks_ok, 1)
                        gp.wait_ge(ks_ok, n.it * NKS + par + 1)

                def suffix(n, l):
                    gp.wait_ge(lvl_mm, n.it * LEVELS + l + 1)
                    if l == 0:
                        gp.wait_ge(diag_mm, n.it + 1)
                        gp.sem_inc(waited, 1)
                        first, by = KS[:, :, :, 0:C:2], member(n, 0, 1)
                    else:
                        first = KS.rearrange("p a x (j s t) -> p (a x j) s t", s=2, t=1 << l)[:, :, 0, :]
                        by = tot_of[l].rearrange("p a x (j s) -> p (a x j) s", s=2)[:, :, 1]\
                            .unsqueeze(2).broadcast_to([P, HP * C >> l, 1 << l])
                    gp.tensor_tensor(first, first, by, ALU.mult).then_inc(ks_ok, 1)
                    gp.wait_ge(ks_ok, n.it * NKS + l + 3)

                def start(n):
                    if not early(n, 1):
                        gp.wait_ge(kq_ok, n.it * NKQ)
                    products(n)
                    total(n)
                    keys(n)
                    suffix(n, 0)

                def root(n):
                    gp.wait_ge(o_sq, n.it + 1)
                    gp.tensor_tensor(ms[:, 0, :], ms[:, 0, :], ms[:, 3, :], ALU.add).then_inc(ms_ok, 1)
                    gp.wait_ge(ms_ok, n.it + 1)
                    gp.tensor_tensor(ms[:, 1, :], ms[:, 0, :], ms[:, 2, :], ALU.pow).then_inc(rr_ok, 1)

                def body(cur, nxt, prev):
                    if nxt:
                        suffix(nxt, 1)
                    if prev:
                        root(prev)
                    if nxt:
                        for l in range(2, LEVELS):
                            suffix(nxt, l)
                        if nxt.after:
                            start(nxt.after)

                start(Round(0, 0))
                for l in range(1, LEVELS):
                    suffix(Round(0, 0), l)
                start(Round(0, 1))
                rounds(gp, body, root)

            @block.vector
            def _(ve):
                ve.wait_ge(zeroed, 6)

                def prefixes(n):
                    if not early(n, 2):
                        ve.wait_ge(kpn_ok, (n.it - 1) * 2)
                    KQ = KQ2[:, n.slot]
                    ve.tensor_tensor(KQ[:, 0], kT[:, :, n.tok], aT[:, :, n.tok], ALU.mult)
                    ve.tensor_tensor(KQ[:, 1], qT[:, :, n.tok], aT[:, :, n.tok], ALU.mult).then_inc(kq_ok, 1)

                def prefix(n, l):
                    L = 1 << l
                    second = KQ2[:, n.slot].rearrange("p x a (j s t) -> p x a j s t", s=2, t=L)[:, :, :, :, 1, :]
                    by = member(n, l, 0)[:, :, 0]
                    ve.wait_ge(lvl_mm, n.it * LEVELS + l + 1)
                    if l:
                        ve.wait_ge(tot_ok, n.it * NTOT + l)
                    ve.wait_ge(kq_ok, n.it * NKQ + l + 1)
                    if l:
                        ve.wait_ge(aq_ok, n.it * NKQ + l + 1)
                    for x_ in range(2):
                        last = ve.tensor_tensor(second[:, x_], second[:, x_],
                                                by.unsqueeze(3).broadcast_to([P, HP, C // (2 * L), L]), ALU.mult)
                    last.then_inc(kq_ok, 1)

                def diagonal(n):
                    ve.wait_ge(diag_mm, n.it + 1)
                    if not early(n, 2):
                        ve.wait_ge(o_mm, n.it - 1)
                    ve.tensor_tensor(AQ2[:, n.slot], psZ[1][:, 0:HP * C].rearrange("p (a t) -> p a t", a=HP)
                                     .unsqueeze(2).broadcast_to([P, HP, 2, C]),
                                     ident[:, :].rearrange("p (x t) -> p x t", x=2).unsqueeze(1)
                                     .broadcast_to([P, HP, 2, C]), ALU.mult).then_inc(aq_ok, 1)

                def keep(n, l):
                    mk = mask[:, l, :].rearrange("p (x t) -> p x t", x=2).unsqueeze(1)
                    def add_to_aq():
                        ve.copy_predicated(AQ2[:, n.slot], mk.broadcast_to([P, HP, 2, C]).bitcast(U32),
                                           psLv[l % 2][:, :, 1, :].unsqueeze(2).broadcast_to([P, HP, 2, C])).then_inc(aq_ok, 1)

                    if l == 0:
                        ve.wait_ge(x_init, n.it)
                        ve.wait_ge(aq_ok, n.it * NKQ + 1)
                    else:
                        add_to_aq()
                        if not early(n, 1):
                            ve.wait_ge(z_mm, (n.it - 1) * G * NINV + G * l)
                    ve.tensor_tensor(E[:, l].rearrange("p a (x t) -> p a x t", x=2),
                                     psLv[l % 2][:, :, 0, :].unsqueeze(2).broadcast_to([P, HP, 2, C]),
                                     mk.broadcast_to([P, HP, 2, C]), ALU.mult).then_inc(e_ok, 1)
                    if l == 0:
                        add_to_aq()

                def start_x(n):
                    ve.wait_ge(e_ok, n.it * LEVELS + 1)
                    ve.wait_ge(u_mm, n.it)
                    for g in range(G):
                        last = ve.tensor_tensor(XY[:, g, 0], ident[:, :].unsqueeze(1).broadcast_to([P, GP, P]),
                                                E[:, 0, g * GP:(g + 1) * GP, :], ALU.subtract)
                    last.then_inc(x_init, 1)

                def start(n, after):
                    if after:
                        prefixes(after)
                    start_x(n)
                    if after:
                        prefix(after, 0)
                        diagonal(after)
                        keep(after, 0)

                def double(n, l):
                    for g in range(G):
                        ve.wait_ge(dxy_mm, n.it * G * NINV + G * (l - 1) + g + 1)
                        ps = psXY[g][:, 0:GP * P].rearrange("p (h t) -> p h t", h=GP)
                        ve.tensor_tensor(XY[:, g, 0], XY[:, g, 0], ps, ALU.subtract).then_inc(xy_ok, 1)

                def normalise(n):
                    ve.wait_ge(rr_ok, n.it + 1)
                    ve.tensor_tensor(On, psO[:, :].rearrange("p (a n) -> p a n", a=HP),
                                     ms[:, 1, :].unsqueeze(2).broadcast_to([P, HP, DV]), ALU.mult).then_inc(on_ok, 1)

                def update(n, pairs):
                    ve.wait_ge(dec_ok, n.it + 1)
                    for hp in pairs:
                        ve.wait_ge(s_mm, n.it + 1)
                        ve.scalar_tensor_tensor(state[:, n.b, hp, :], state[:, n.b, hp, :],
                                                decay[:, n.b, hp:hp + 1], psR[:, hp * DV:(hp + 1) * DV],
                                                ALU.mult, ALU.add).then_inc(s_ok, 1)

                def finish(n):
                    update(n, range(HP))
                    normalise(n)

                def body(cur, nxt, prev):
                    for l in range(1, LEVELS):
                        if nxt:
                            prefix(nxt, l)
                            keep(nxt, l)
                        double(cur, l)
                        if prev and l == 2:
                            normalise(prev)
                        if prev and l in (1, 3):
                            update(prev, (0, 1) if l == 1 else (2, 3))
                    if nxt:
                        start(nxt, nxt.after)

                first = Round(0, 0)
                prefixes(first)
                prefix(first, 0)
                diagonal(first)
                keep(first, 0)
                for l in range(1, LEVELS):
                    prefix(first, l)
                    keep(first, l)
                start(first, Round(0, 1))
                rounds(ve, body, finish)

            @block.tensor
            def _(pe):
                pe.wait_ge(zeroed, 6)

                def level(n, l, pairs=range(HP)):
                    if pairs[0] == 0:
                        pe.wait_ge(kq_ok, n.it * NKQ + l + 1)
                        pe.wait_ge(ks_ok, n.it * NKS + l + 2)
                        pe.wait_ge(e_ok, n.it * LEVELS + l - 1) if l >= 2 else pe.wait_ge(e_ok, n.it * LEVELS)
                        if l == 2:
                            pe.wait_ge(aq_ok, n.it * NKQ + 2)
                        if l == 0:
                            pe.wait_ge(ksn_ok, n.it)
                    for hp in pairs:
                        last = pe.matmul(psL[l % 2][:, hp * P:(hp + 1) * P], flat(KS, hp), KQ2[:, n.slot, :, hp, :],
                                         start=True, stop=True)
                    if pairs[-1] == HP - 1:
                        last.then_inc(lvl_mm, 1)

                def diagonal(n):
                    if not early(n, 2):
                        pe.wait_ge(z_ok, (n.it - 1) * G * NINV)
                    for hp in range(HP):
                        last = pe.matmul(psZ[1][:, hp * C:(hp + 1) * C], flat(KS, hp), qT[:, hp, n.tok],
                                         start=True, stop=True)
                    last.then_inc(diag_mm, 1)

                def double_z(n, l):
                    it = n.it
                    for g in range(G):
                        pe.wait_ge(e_ok, it * LEVELS + l + 1)
                        pe.wait_ge(x_init, it + 1)
                        pe.wait_ge(y_new, it * G * NINV + G * (l - 1) + g + 1)
                        if l == 1:
                            pe.wait_ge(aq_ok, n.diag_out)
                        for h in range(GP):
                            last = pe.matmul(psZ[g][:, h * P:(h + 1) * P], E[:, l, g * GP + h, :],
                                             XY[:, g, 1, h, :], start=True, stop=True)
                        last.then_inc(z_mm, 1)

                def double_x(n, l):
                    for g in range(G):
                        pe.wait_ge(z_ok, n.it * G * NINV + G * (l - 1) + g + 1)
                        for h in range(GP):
                            last = pe.matmul(psXY[g][:, h * P:(h + 1) * P], Z[:, g, h, :],
                                             XY[:, g, 0, h, :], start=True, stop=True)
                        last.then_inc(dxy_mm, 1)

                def turn_x(n, l, g):
                    pe.wait_ge(xy_ok, n.it * G * NINV + G * (l - 1) + g + 1)
                    for h in range(GP):
                        last = pe.transpose(psXY[g][:, (GP + h) * P:(GP + h + 1) * P], XY[:, g, 0, h, :], ident[:, :])
                    last.then_inc(xt_mm, 1)

                def turn_ks(n):
                    pe.wait_ge(ks_ok, (n.it + 1) * NKS)
                    pe.wait_ge(e_ok, n.it * LEVELS + LEVELS - 1)
                    for hp in range(HP):
                        last = pe.transpose(psL[0][:, hp * P:(hp + 1) * P], flat(KS, hp), ident[:, :])
                    last.then_inc(ksn_mm, 1)

                def turn_out(n):
                    pe.wait_ge(on_ok, n.it + 1)
                    for hp in range(HP):
                        last = pe.transpose(psO[:, hp * P:(hp + 1) * P], On[:, hp, :], ident[:, :])
                    last.then_inc(yout_mm, 1)

                def turn_start(n):
                    pe.wait_ge(x_init, n.it + 1)
                    pe.wait_ge(xy_ok, n.it * G * NINV)
                    for g in range(G):
                        for h in range(GP):
                            last = pe.transpose(psXY[g][:, (GP + h) * P:(GP + h + 1) * P], XY[:, g, 0, h, :],
                                                ident[:, :])
                        last.then_inc(xt0_mm, 1)

                def body(cur, nxt, prev):
                    it = cur.it
                    after = nxt.after if nxt else None
                    cur.diag_out = (it + 1) * NKQ + (1 if nxt else 0)
                    if nxt:
                        level(nxt, 1)
                    for l in range(1, NINV):
                        double_z(cur, l)
                        if nxt:
                            level(nxt, l + 1, (0, 1))
                        double_x(cur, l)
                        if nxt:
                            level(nxt, l + 1, (2,))
                        if l == 3 and prev:
                            turn_out(prev)
                        turn_x(cur, l, 0)
                        if nxt:
                            level(nxt, l + 1, (3,))
                        turn_x(cur, l, 1)
                    pe.wait_ge(hc_ok, it + 1)
                    pe.wait_ge(s_ok, it * HP)
                    for par in range(2):
                        pe.matmul(psR[C * par:C * par + C, :], hc, wv_sb[:, :, par, :], start=True, stop=False,
                                  skip_group_check=True)
                    pe.wait_ge(kpn_ok, it * 2 + 2)
                    for hp in range(HP):
                        last = pe.matmul(psR[:, hp * DV:(hp + 1) * DV], flat(KPn, hp), state[:, cur.b, hp, :],
                                         start=False, stop=True, skip_group_check=True)
                    last.then_inc(res_mm, 1)
                    double_z(cur, NINV)
                    if nxt:
                        turn_ks(nxt)
                    double_x(cur, NINV)
                    pe.wait_ge(qpb_ok, it * 2 + 2)
                    pe.wait_ge(yout_ok, it * 2)
                    for hp in range(HP):
                        pe.matmul(psO[:, hp * DV:(hp + 1) * DV], flat(QPb, hp), state[:, cur.b, hp, :],
                                  start=hp == 0, stop=False, skip_group_check=True)
                    pe.wait_ge(res_ok, it + 1)
                    pe.wait_ge(xy_ok, (it + 1) * G * NINV)
                    for hp in range(HP):
                        last = pe.matmul(psR[:, hp * DV:(hp + 1) * DV], XY[:, hp // GP, 0, hp % GP, :], res[:, hp, :],
                                         start=True, stop=True)
                    last.then_inc(u_mm, 1)
                    if after:
                        level(after, 0)
                    pe.wait_ge(aq_ok, (it + 1) * NKQ)
                    pe.wait_ge(u_ok, it + 1)
                    for hp in range(HP):
                        last = pe.matmul(psO[:, hp * DV:(hp + 1) * DV], flat(AQ2[:, cur.slot], hp), U[:, hp, :],
                                         start=False, stop=True, skip_group_check=True)
                    last.then_inc(o_mm, 1)
                    if after:
                        diagonal(after)
                    if nxt:
                        turn_start(nxt)
                    pe.wait_ge(ksn_ok, it + 1)
                    for hp in range(HP):
                        last = pe.matmul(psR[:, hp * DV:(hp + 1) * DV], KSn[:, cur.slot, hp, :], U[:, hp, :],
                                         start=True, stop=True)
                    last.then_inc(s_mm, 1)

                first = Round(0, 0)
                level(first, 0)
                diagonal(first)
                for l in range(1, LEVELS):
                    level(first, l)
                turn_ks(first)
                level(Round(0, 1), 0)
                diagonal(Round(0, 1))
                turn_start(first)
                rounds(pe, body, turn_out)

            @block.scalar
            def _(ac):
                ac.wait_ge(zeroed, 6)

                def copy_z(n, l):
                    for g in range(G):
                        ac.wait_ge(z_mm, n.it * G * NINV + G * (l - 1) + g + 1)
                        ac.wait_ge(dxy_mm, n.it * G * NINV + G * (l - 2) + g + 1) if l >= 2 else \
                            ac.wait_ge(dxy_mm, n.it * G * NINV)
                        ac.copy(Z[:, g], psZ[g][:, 0:GP * P].rearrange("p (h t) -> p h t", h=GP)).then_inc(z_ok, 1)

                def copy_start(n):
                    for g in range(G):
                        ac.wait_ge(xt0_mm, n.it * G + g + 1)
                        ac.copy(XY[:, g, 1], psXY[g][:, GP * P:].rearrange("p (h t) -> p h t", h=GP)).then_inc(y_new, 1)

                def copy_y(n, l):
                    for g in range(G):
                        ac.wait_ge(xt_mm, n.it * G * (NINV - 1) + G * (l - 1) + g + 1)
                        ac.copy(XY[:, g, 1], psXY[g][:, GP * P:].rearrange("p (h t) -> p h t", h=GP)).then_inc(y_new, 1)

                def spread_kq(n):
                    ac.wait_ge(kq_ok, (n.it + 1) * NKQ)
                    ac.wait_ge(o_mm, n.it)
                    for x_, dst, done, by in ((1, QPb, qpb_ok, 1.0), (0, KPn, kpn_ok, -1.0)):
                        for par in range(2):
                            rows = slice(C * par, C * par + C)
                            ac.mul(dst[rows, :, par, :], KQ2[rows, n.slot, x_], by).then_inc(done, 1)

                def keep_ks(n):
                    ac.wait_ge(ksn_mm, n.it + 1)
                    ac.copy(KSn[:, n.slot], psL[0][:, :].rearrange("p (a n) -> p a n", a=HP)).then_inc(ksn_ok, 1)

                def keep_out(n):
                    ac.wait_ge(yout_mm, n.it + 1)
                    for par, dst in enumerate((qT, kT)):
                        ac.copy(dst[:, :, n.tok], psO[:, :].rearrange("p (a x t) -> p a x t", a=HP, x=2)[:, :, par, :])\
                            .then_inc(yout_ok, 1)

                def body(cur, nxt, prev):
                    it = cur.it
                    ac.copy(hc, hT[:, cur.tok]).then_inc(hc_ok, 1)
                    for l in range(1, NINV):
                        copy_z(cur, l)
                        copy_y(cur, l)
                        if l == 3 and prev:
                            keep_out(prev)
                    ac.wait_ge(res_mm, it + 1)
                    ac.wait_ge(yout_mm, it)
                    ac.copy(res, psR[:, :].rearrange("p (a n) -> p a n", a=HP)).then_inc(res_ok, 1)
                    copy_z(cur, NINV)
                    if nxt:
                        ac.wait_ge(s_mm, it)
                        keep_ks(nxt)
                    ac.wait_ge(u_mm, it + 1)
                    ac.wait_ge(s_mm, it)
                    ac.copy(U, psR[:, :].rearrange("p (a n) -> p a n", a=HP)).then_inc(u_ok, 1)
                    if nxt:
                        copy_start(nxt)
                    ac.wait_ge(o_mm, it + 1)
                    ac.wait_ge(rr_ok, it)
                    for hp in range(HP):
                        last = ac.activation(res[:, hp, :], psO[:, hp * DV:(hp + 1) * DV], ACT.Square,
                                             scale=DV ** -0.5, accum_out=ms[:, 0, hp:hp + 1])
                    last.then_inc(o_sq, 1)
                    if nxt:
                        spread_kq(nxt)
                spread_kq(Round(0, 0))
                keep_ks(Round(0, 0))
                copy_start(Round(0, 0))
                rounds(ac, body, keep_out)

        late = gates[:, :, :, :].rearrange("p g a t -> p (g a t)")
        late_at, used[0] = [0], 0

        def late_region(shape):
            return region(shape, late, late_at)

        wff1_sb = late_region([FT * P])
        wff3_sb = late_region([FT * P])
        wff2_sb = late_region([FT, D])
        Wq_sb = late_region([XP, P])
        Wk_sb = late_region([XP, P])
        Wv_sb = late_region([XP * P])
        Wo_sb = late_region([XP, D])
        N0 = k0.shape[1]
        F2 = N0 // P
        w0_sb = late_region([2, N0])
        w1_sb = late_region([F2, k1.shape[1]])
        w2_sb = late_region([F2, D])
        k0_sb = late_region([2 * N0 // 4]).bitcast(U8).rearrange("p (a n) -> p a n", a=2)
        k1_sb = late_region([F2 * k1.shape[1] // 4]).bitcast(U8).rearrange("p (a n) -> p a n", a=F2)
        k2_sb = late_region([F2 * D // 4]).bitcast(U8).rearrange("p (a n) -> p a n", a=F2)
        NTB = T // P
        Q2 = late_region([XP, T])
        XO = Q2
        wout_sb = region([2 * HP, D])
        ctx_sb = region([B, D])[0:S]
        ctxT = region([B, S])
        cb = region([S])
        KB = region([XP, 2, S])
        VB = region([XH * DK])[0:S]
        PR = region([2, XH, S])
        PT = region([XH, P])[0:S]
        FH = hT[:, :].rearrange("p (f t) -> p f t", f=FT)
        smx = region([2, 3, XH])
        m = [region([T]) for _ in range(7)]
        H1 = Q2[:, 0:F2]
        H2 = Q2[:, F2:2 * F2]
        u1_gate, u1_act = FH[0:R, 0], FH[0:R, 1]
        x_nat = region([T // P, D])
        s0x2 = region([1])
        s1x2 = region([1])
        EPS = (1e-6, 1e-5, 1e-5, 1e-5)
        centre_w = region([P])
        stat = region([2, NTB])
        NP3 = [(0, 3), (3, 3), (6, 2)]

        tw = sem("tail_w")
        ctx_ld = sem("ctx_ld")
        wout_ld, wout_ok = sem("wout_ld"), sem("wout_ok")
        signs = sem("signs")
        ctx_mm, ctx_ok = sem("ctx_mm"), sem("ctx_ok")
        kb_zero = sem("kb_zero")
        at_mm, u1_mm, u1_sig, u1_ok = sem("at_mm"), sem("u1_mm"), sem("u1_sig"), sem("u1_ok")
        u2_mm, gate_ok, gated, y1_ok = sem("u2_mm"), sem("gate_ok"), sem("gated"), sem("y1_ok")
        n_cen, n_sq, n_mm, n_eps = sem("n_cen"), sem("n_sq"), sem("n_mm"), sem("n_eps")
        n_rs, n_bc, n_out, cen_out = sem("n_rs"), sem("n_bc"), sem("n_out"), sem("cen_out")
        ff_mm, ff_sig, ff_mul, ff_ok = sem("ff_mm"), sem("ff_sig"), sem("ff_mul"), sem("ff_ok")
        ff2_mm, x1_ok, x_in = sem("ff2_mm"), sem("x1_ok"), sem("x_in")
        q2_mm, q2_ok = sem("q2_mm"), sem("q2_ok")
        cb_ok, kb_mm, kb_ok, vb_mm, vb_ok = sem("cb_ok"), sem("kb_mm"), sem("kb_ok"), sem("vb_mm"), sem("vb_ok")
        sc_mm, mx_ok, exp_ok = sem("sc_mm"), sem("mx_ok"), sem("exp_ok")
        sum_ok, inv_ok, pr_ok = sem("sum_ok"), sem("inv_ok"), sem("pr_ok")
        wo_mm, wo_ok, x2_ok = sem("wo_mm"), sem("wo_ok"), sem("x2_ok")
        h1_mm, h1_ok, h2_mm, h2_ok = sem("h1_mm"), sem("h1_ok"), sem("h2_mm"), sem("h2_ok")
        h3_mm, y_ok, yt2_mm = sem("h3_mm"), sem("y_ok"), sem("yt2_mm")
        NORMS = 4
        CEN = 3

        TW_FF, TW_Q, TW_K, TW_V, TW_O, TW_SIGN = (16 * n for n in (3, 4, 5, 6, 7, 10))

        with nc.Block() as block:
            @block.sync
            def _(sp):
                sp.dma_start(ctx_sb, ctx_in.rearrange("b s d -> s b d")).then_inc(ctx_ld, 16)
                sp.dma_start(wout_sb, w_out.rearrange("(h v) d -> v h d", v=DV)).then_inc(wout_ld, 16)
                for dst, src in ((wff1_sb, w_ff1), (wff3_sb, w_ff3),
                                 (wff2_sb, w_ff2.rearrange("(a p) d -> p a d", p=P)),
                                 (Wq_sb, Wq.rearrange("d (a n) -> d a n", a=XP)),
                                 (Wk_sb, Wk.rearrange("d (a n) -> d a n", a=XP)), (Wv_sb, Wv),
                                 (Wo_sb, Wo.rearrange("(a p) d -> p a d", p=P)),
                                 (k0_sb, k0.rearrange("(a p) n -> p a n", p=P)),
                                 (k1_sb, k1.rearrange("(a p) n -> p a n", p=P)),
                                 (k2_sb, k2.rearrange("(a p) n -> p a n", p=P))):
                    sp.dma_start(dst, src).then_inc(tw, 16)
                out_v = out.rearrange("b t d -> (b t) d").rearrange("(b n p) d -> b p n d", p=P, n=NTB)
                x_v = x.rearrange("b t d -> (b t) d").rearrange("(b n p) d -> b p n d", p=P, n=NTB)
                sp.dma_start(x_nat, x_v[0]).then_inc(x_in, 16)
                with sp.Fori(0, B) as b:
                    sp.wait_ge(x1_ok, b + 1)
                    nxt_row = (b + 1) % B
                    sp.dma_start(x_nat, x_v[bass.ds(nxt_row, 1)].squeeze(0)).then_inc(x_in, 16)
                    sp.wait_ge(row_done, at(b + 1))
                    sp.dma_start(out_v[bass.ds(b, 1)].squeeze(0), m[6].rearrange("p (n d) -> p n d", n=NTB))\
                        .then_inc(stored, 16)
                sp.wait_ge(stored, at(16 * B))

            @block.gpsimd
            def _(gp):
                gp.memset(KB, 0.0).then_inc(kb_zero, 1)
                gp.wait_ge(tw, TW_SIGN)
                gp.tensor_scalar(w0_sb, k0_sb, 2.0, -1.0, ALU.mult, ALU.add).then_inc(signs, 1)
                gp.tensor_scalar(w1_sb, k1_sb, 2.0, -1.0, ALU.mult, ALU.add).then_inc(signs, 1)
                gp.tensor_scalar(w2_sb, k2_sb, 2.0, -1.0, ALU.mult, ALU.add).then_inc(signs, 1)
                gp.wait_ge(signs, 3)
                gp.tensor_tensor(w0_sb[:, 0], w0_sb[:, 0], w0_sb[:, 1], ALU.subtract).then_inc(signs, 1)
                gp.tensor_scalar(s0x2, v("s0"), 2.0, None, ALU.mult).then_inc(signs, 1)
                gp.tensor_scalar(s1x2, v("s1"), 2.0, None, ALU.mult).then_inc(signs, 1)
                gp.tensor_tensor(centre_w, ident[:, :], mean_w[:, :], ALU.subtract).then_inc(signs, 1)

                def root(b, k):
                    gp.wait_ge(n_eps, b * NORMS + k + 1)
                    gp.tensor_tensor(stat[:, 1], stat[:, 0], half[:, 0:NTB], ALU.pow).then_inc(n_rs, 1)

                with gp.Fori(0, B) as b:
                    root(b, 0)
                    root(b, 1)
                    for n in range(NTB):
                        i = b * NTB + n
                        gp.wait_ge(inv_ok, i + 1)
                        gp.tensor_tensor(PR[:, n % 2], PR[:, n % 2],
                                         smx[:, n % 2, 2, :].unsqueeze(2).broadcast_to([P, XH, S]), ALU.mult)\
                            .then_inc(pr_ok, 1)
                    root(b, 2)
                    root(b, 3)

            @block.tensor
            def _(pe):
                pe.wait_ge(ctx_ld, 16)
                for j in range(B):
                    last = pe.transpose(bank[0][:, j * S:(j + 1) * S], ctx_sb[:, j, :], ident[0:S, 0:S])
                last.then_inc(ctx_mm, 1)
                pe.wait_ge(ctx_ok, 1)

                def centre(src):
                    pe.wait_ge(signs, 7)
                    pe.matmul(bank[2][:, :], centre_w, src, start=True, stop=True).then_inc(n_cen, 1)

                def mean_square(b, k):
                    pe.wait_ge(n_sq, b * NORMS + k + 1)
                    for n in range(NTB):
                        last = pe.matmul(bank[3][:, n:n + 1], m[1][:, n * P:(n + 1) * P], mean_w[:, 0:1],
                                         start=True, stop=True)
                    last.then_inc(n_mm, 1)

                def spread_root(b, k):
                    pe.wait_ge(n_rs, b * NORMS + k + 1)
                    for n in range(NTB):
                        last = pe.matmul(bank[3][:, n * P:(n + 1) * P], stat[:, 1, n:n + 1].broadcast_to([P, P]),
                                         ident[:, :], start=True, stop=True)
                    last.then_inc(n_bc, 1)

                def front_u1(tok):
                    pe.matmul(bank[1][0:R, :], wu1_sb[:, :], zT[:, tok], start=True, stop=True).then_inc(u1_mm, 1)

                def front_out(tok, heads):
                    for h in heads:
                        last = pe.matmul(bank[0][:, :], wout_sb[:, h, :], (qT, kT)[h % 2][:, h // 2, tok],
                                         start=h == 0, stop=h == 2 * HP - 1)
                    if heads[-1] == 2 * HP - 1:
                        last.then_inc(at_mm, 1)

                def front_u2(row):
                    pe.wait_ge(u1_ok, row + 1)
                    pe.matmul(bank[1][:, :], wu2_sb[:, :], u1_act, start=True, stop=True).then_inc(u2_mm, 1)

                pe.wait_ge(wout_ok, 2 * HP)
                front_u1(slice(0, T))
                front_out(slice(0, T), range(2 * HP))
                front_u2(0)
                mean_square(0, 0)
                with pe.Fori(0, B) as b:
                    tok_next = bass.ds((b + 1) % B * T, T)
                    spread_root(b, 0)
                    pe.wait_ge(row_done, at(b))
                    pe.wait_ge(tw, TW_FF)
                    pe.wait_ge(n_out, b * NORMS + 1)
                    for f in range(FT):
                        if f >= 2:
                            pe.wait_ge(ff_ok, b * FT + f - 1)
                        for j, w in enumerate((wff1_sb, wff3_sb)):
                            last = pe.matmul(bank[4 + 2 * (f % 2) + j][:, :], w[:, f * P:(f + 1) * P], m[4],
                                             start=True, stop=True)
                        last.then_inc(ff_mm, 1)
                    for f in range(FT):
                        pe.wait_ge(ff_ok, b * FT + f + 1)
                        pe.matmul(bank[0][:, :], wff2_sb[:, f, :], FH[:, f, :], start=f == 0, stop=False,
                                  skip_group_check=True)
                    pe.wait_ge(x_in, b * 16 + 16)
                    for n in range(NTB):
                        last = pe.matmul(bank[0][:, n * P:(n + 1) * P], x_nat[:, n, :], ident[:, :],
                                         start=False, stop=True, skip_group_check=True)
                    last.then_inc(ff2_mm, 1)
                    pe.wait_ge(x1_ok, b + 1)
                    centre(m[4])
                    mean_square(b, 1)
                    pe.wait_ge(tw, TW_V)
                    for a in range(XP):
                        last = pe.matmul(bank[a // 4][:, (a % 4) * S:(a % 4 + 1) * S], Wk_sb[:, a, :],
                                         ctxT[:, bass.ds(b, 1), :].squeeze(1), start=True, stop=True)
                    last.then_inc(kb_mm, 1)
                    spread_root(b, 1)
                    pe.wait_ge(n_out, b * NORMS + 2)
                    for a in range(XP):
                        if a >= 4:
                            pe.wait_ge(q2_ok, b * XP + a - 3)
                        pe.matmul(bank[4 + a % 4][:, :], Wq_sb[:, a, :], m[3], start=True, stop=True).then_inc(q2_mm, 1)
                    pe.wait_ge(cb_ok, b + 1)
                    for j in range(2):
                        last = pe.matmul(bank[2 + j][0:S, :], cb, Wv_sb[:, j * 512:(j + 1) * 512],
                                         start=True, stop=True)
                    last.then_inc(vb_mm, 1)
                    pe.wait_ge(kb_ok, b * 4 + 4)
                    pe.wait_ge(vb_ok, b * 2 + 2)
                    pe.wait_ge(q2_ok, (b + 1) * XP)

                    def scores(n):
                        pe.wait_ge(sub_ok, at(b * 3 * NTB + 3 * n))
                        for j, (a0, na) in enumerate(NP3):
                            for a in range(na):
                                last = pe.matmul(bank[4 + j][:, a * 2 * S:(a + 1) * 2 * S],
                                                 Q2[:, a0 + a, n * P:(n + 1) * P],
                                                 KB[:, a0 + a].rearrange("p x s -> p (x s)"), start=True, stop=True)
                            last.then_inc(sc_mm, 1)

                    scores(0)
                    scores(1)
                    for n in range(NTB):
                        i = b * NTB + n
                        pe.wait_ge(pr_ok, i + 1)
                        for q in range(4):
                            if q == 0:
                                pe.wait_ge(pt_v, at(i * 2))
                                pe.wait_ge(pt_a, at(i * 2))
                            elif q == 3:
                                pe.wait_ge(pt_a, at(i * 2 + 1))
                            for h in range(4):
                                last = pe.transpose(bank[q % 3][0:S, h * P:(h + 1) * P], PR[:, n % 2, 4 * q + h, :], ident[:, :])
                            last.then_inc(pt_mm, 1)
                        if n + 2 < NTB:
                            scores(n + 2)
                        pe.wait_ge(pt_a, at(i * 2 + 2))
                        pe.wait_ge(pt_v, at(i * 2 + 2))
                        pe.wait_ge(xo_ok, at(i * 2))
                        for h in range(XH):
                            a, par = h // 2, h % 2
                            last = pe.matmul((bank[3], bank[7])[a // 4][DK * par:DK * par + DK, (a % 4) * P:(a % 4 + 1) * P],
                                             VB[:, h * DK:(h + 1) * DK], PT[:, h, :], start=True, stop=True)
                        last.then_inc(pv_mm, 1)
                    pe.wait_ge(xo_ok, at((b + 1) * 2 * NTB))
                    for a in range(XP):
                        last = pe.matmul(bank[0][:, :], Wo_sb[:, a, :], XO[:, a, :], start=a == 0, stop=a == XP - 1)
                    last.then_inc(wo_mm, 1)
                    pe.wait_ge(wo_ok, b + 1)
                    centre(m[5])
                    front_u1(tok_next)
                    mean_square(b, 2)
                    front_out(tok_next, (0, 1))
                    spread_root(b, 2)
                    front_out(tok_next, (2, 3))
                    pe.wait_ge(x2_ok, b + 1)
                    centre(m[4])
                    front_out(tok_next, (4,))
                    mean_square(b, 3)
                    front_out(tok_next, (5, 6))
                    spread_root(b, 3)
                    front_out(tok_next, (7,))
                    front_u2(b + 1)
                    pe.wait_ge(signs, 7)
                    pe.wait_ge(n_out, b * NORMS + 4)
                    for f in range(F2):
                        pe.matmul(bank[4 + f][:, :], w0_sb[:, 0, f * P:(f + 1) * P], m[3], start=True, stop=True)\
                            .then_inc(h1_mm, 1)
                    pe.wait_ge(h1_ok, (b + 1) * F2)
                    pe.wait_ge(gated, b + 2)
                    for f in range(F2):
                        for a in range(F2):
                            last = pe.matmul(bank[f][:, :], w1_sb[:, a, f * P:(f + 1) * P], H1[:, a, :],
                                             start=a == 0, stop=a == F2 - 1)
                        last.then_inc(h2_mm, 1)
                    for a in range(F2):
                        pe.wait_ge(h2_ok, b * F2 + a + 1)
                        last = pe.matmul(bank[4][:, :], w2_sb[:, a, :], H2[:, a, :], start=a == 0, stop=a == F2 - 1)
                    last.then_inc(h3_mm, 1)
                    mean_square(b + 1, 0)
                    pe.wait_ge(y_ok, b + 1)
                    for n in range(NTB):
                        last = pe.transpose(bank[5][:, n * P:(n + 1) * P], m[5][:, n * P:(n + 1) * P], ident[:, :])
                    last.then_inc(yt2_mm, 1)

            @block.scalar
            def _(ac):
                ac.wait_ge(ctx_mm, 1)
                ac.copy(ctxT, bank[0][:, 0:B * S].rearrange("p (b s) -> p b s", b=B)).then_inc(ctx_ok, 1)
                def square(src):
                    ac.activation(m[1], src, ACT.Square).then_inc(n_sq, 1)

                def front_sig(row):
                    ac.wait_ge(u1_mm, row + 1)
                    ac.activation(u1_gate, bank[1][0:R, :], ACT.Sigmoid, bias=v("b_u1", 0, R)).then_inc(u1_sig, 1)

                def front_gate(row):
                    ac.wait_ge(u2_mm, row + 1)
                    ac.activation(m[2], bank[1][:, :], ACT.Sigmoid, bias=v("b_u2")).then_inc(gate_ok, 1)

                front_sig(0)
                front_gate(0)
                ac.wait_ge(y1_ok, 1)
                square(m[3])
                ac.wait_ge(kb_zero, 1)
                ac.wait_ge(ctx_ok, 1)
                ac.wait_ge(signs, 7)
                with ac.Fori(0, B) as b:
                    for f in range(FT):
                        if f == 1:
                            ac.wait_ge(stored, at(b * 16))
                        ac.wait_ge(ff_mm, b * FT + f + 1)
                        if f >= 2:
                            ac.wait_ge(ff_ok, b * FT + f - 1)
                        ac.activation(m[5 + f % 2], bank[4 + 2 * (f % 2)][:, :], ACT.Sigmoid).then_inc(ff_sig, 1)
                    ac.wait_ge(n_cen, b * CEN + 1)
                    square(bank[2][:, :])
                    ac.copy(m[0], bank[2][:, :]).then_inc(cen_out, 1)
                    ac.wait_ge(kb_mm, b + 1)
                    for j in range(2):
                        for par in range(2):
                            rows = slice(DK * par, DK * par + DK)
                            for a in range(4):
                                last = ac.activation(KB[rows, 4 * j + a, par, :],
                                                     bank[j][rows, a * S:(a + 1) * S], ACT.Identity,
                                                     bias=vec[rows, VEC["bk"][0] + 4 * j + a:VEC["bk"][0] + 4 * j + a + 1])
                            last.then_inc(kb_ok, 1)
                    ac.copy(cb, ctxT[:, bass.ds(b, 1), :].squeeze(1)).then_inc(cb_ok, 1)
                    for a in range(XP):
                        ac.wait_ge(q2_mm, b * XP + a + 1)
                        ac.activation(Q2[:, a, :], bank[4 + a % 4][:, :], ACT.Identity, bias=v("bq", a)).then_inc(q2_ok, 1)
                    ac.wait_ge(vb_mm, b + 1)
                    for j in range(2):
                        ac.copy(VB[:, j * 512:(j + 1) * 512], bank[2 + j][0:S, :]).then_inc(vb_ok, 1)
                    def exponent(n):
                        ac.wait_ge(sub_ok, at((b * NTB + n) * 3 + 3))
                        ac.activation(PR[:, n % 2], PR[:, n % 2], ACT.Exp, scale=DK ** -0.5).then_inc(exp_ok, 1)

                    def keep_turned(n, q):
                        i = b * NTB + n
                        ac.wait_ge(pv_mm, at(i))
                        ac.wait_ge(pt_mm, at(i * 4 + q + 1))
                        ac.copy(PT[:, 4 * q:4 * q + 4, :], bank[q % 3][0:S, :].rearrange("p (h t) -> p h t", h=4))\
                            .then_inc(pt_a, 1)

                    exponent(0)
                    exponent(1)
                    keep_turned(0, 0)
                    keep_turned(0, 2)
                    for n in range(NTB):
                        ac.wait_ge(pv_mm, at(b * NTB + n + 1))
                        for j in range(2):
                            for a in range(4):
                                last = ac.activation(XO[:, 4 * j + a, n * P:(n + 1) * P],
                                                     (bank[3], bank[7])[j][:, a * P:(a + 1) * P], ACT.Identity,
                                                     bias=v("bv", 4 * j + a))
                            last.then_inc(xo_ok, 1)
                        if n + 1 < NTB:
                            keep_turned(n + 1, 0)
                        if n + 2 < NTB:
                            exponent(n + 2)
                        if n + 1 < NTB:
                            keep_turned(n + 1, 2)
                    ac.wait_ge(n_cen, b * CEN + 2)
                    square(bank[2][:, :])
                    ac.copy(m[0], bank[2][:, :]).then_inc(cen_out, 1)
                    front_sig(b + 1)
                    ac.wait_ge(n_cen, b * CEN + 3)
                    square(bank[2][:, :])
                    ac.copy(m[0], bank[2][:, :]).then_inc(cen_out, 1)
                    front_gate(b + 1)
                    for f in range(F2):
                        ac.wait_ge(h1_mm, b * F2 + f + 1)
                        ac.activation(H1[:, f, :], bank[4 + f][:, :], ACT.Relu, scale=s0x2).then_inc(h1_ok, 1)
                    for f in range(F2):
                        ac.wait_ge(h2_mm, b * F2 + f + 1)
                        ac.activation(H2[:, f, :], bank[f][:, :], ACT.Relu, scale=s1x2).then_inc(h2_ok, 1)
                    ac.wait_ge(y1_ok, b + 2)
                    square(m[3])
                    ac.wait_ge(yt2_mm, b + 1)
                    ac.copy(m[6], bank[5][:, :]).then_inc(row_done, 1)

            @block.vector
            def _(ve):
                def factors(b, k):
                    ve.wait_ge(n_mm, b * NORMS + k + 1)
                    ve.tensor_scalar(stat[:, 0], bank[3][:, 0:NTB], EPS[k], None, ALU.add).then_inc(n_eps, 1)
                    if k:
                        ve.wait_ge(cen_out, b * CEN + k)
                    ve.wait_ge(n_bc, b * NORMS + k + 1)

                ve.wait_ge(wout_ld, 16)
                for h in range(2 * HP):
                    ve.tensor_scalar(wout_sb[:, h, :], wout_sb[:, h, :], v("w_hn", h), None, ALU.mult)\
                        .then_inc(wout_ok, 1)
                def front_act(row):
                    ve.wait_ge(u1_sig, row + 1)
                    ve.scalar_tensor_tensor(u1_act, bank[1][0:R, :], v("b_u1", 0, R), u1_gate,
                                            ALU.add, ALU.mult).then_inc(u1_ok, 1)

                def front_gated(row):
                    ve.wait_ge(gate_ok, row + 1)
                    ve.wait_ge(at_mm, row + 1)
                    ve.tensor_tensor(m[2], m[2], bank[0][:, :], ALU.mult).then_inc(gated, 1)

                def front_y1(row, tok):
                    ve.wait_ge(gated, row + 1)
                    ve.tensor_tensor(m[3], m[2], zT[:, tok], ALU.add).then_inc(y1_ok, 1)

                front_act(0)
                front_gated(0)
                front_y1(0, slice(0, T))
                with ve.Fori(0, B) as b:
                    factors(b, 0)
                    ve.scalar_tensor_tensor(m[4], m[3], v("w_ffn"), bank[3][:, :], ALU.mult, ALU.mult).then_inc(n_out, 1)
                    for f in range(FT):
                        g = m[5 + f % 2]
                        ve.wait_ge(ff_sig, b * FT + f + 1)
                        ve.tensor_tensor(g, g, bank[4 + 2 * (f % 2)][:, :], ALU.mult).then_inc(ff_mul, 1)
                        ve.wait_ge(ff_mul, b * FT + f + 1)
                        ve.tensor_tensor(FH[:, f, :], g, bank[5 + 2 * (f % 2)][:, :], ALU.mult).then_inc(ff_ok, 1)
                    ve.wait_ge(ff2_mm, b + 1)
                    ve.tensor_tensor(m[4], m[3], bank[0][:, :], ALU.add).then_inc(x1_ok, 1)
                    factors(b, 1)
                    ve.tensor_tensor(m[3], m[0], bank[3][:, :], ALU.mult).then_inc(n_out, 1)

                    def less_max(n):
                        i = b * NTB + n
                        ve.wait_ge(pt_mm, at(i * 4 - 4)) if n >= 2 else ve.wait_ge(pt_mm, at(b * NTB * 4))
                        for j, (a0, na) in enumerate(NP3):
                            heads = slice(2 * a0, 2 * (a0 + na))
                            ps = bank[4 + j][:, 0:2 * na * S].rearrange("p (h s) -> p h s", s=S)
                            ve.wait_ge(sc_mm, i * 3 + j + 1)
                            ve.tensor_reduce(smx[:, n % 2, 0, heads], ps, AX.X, ALU.max).then_inc(mx_ok, 1)
                            ve.wait_ge(mx_ok, i * 3 + j + 1)
                            ve.tensor_tensor(PR[:, n % 2, heads, :], ps,
                                             smx[:, n % 2, 0, heads].unsqueeze(2).broadcast_to([P, 2 * na, S]),
                                             ALU.subtract).then_inc(sub_ok, 1)

                    def inverse_sum(n):
                        i = b * NTB + n
                        ve.wait_ge(exp_ok, i + 1)
                        ve.tensor_reduce(smx[:, n % 2, 1, :], PR[:, n % 2], AX.X, ALU.add).then_inc(sum_ok, 1)
                        ve.wait_ge(sum_ok, i + 1)
                        ve.reciprocal(smx[:, n % 2, 2, :], smx[:, n % 2, 1, :]).then_inc(inv_ok, 1)

                    less_max(0)
                    inverse_sum(0)
                    less_max(1)
                    inverse_sum(1)
                    for n in range(NTB):
                        i = b * NTB + n
                        ve.wait_ge(pv_mm, at(i))
                        for q in (1, 3):
                            ve.wait_ge(pt_mm, at(i * 4 + q + 1))
                            ve.tensor_copy(PT[:, 4 * q:4 * q + 4, :],
                                           bank[q % 3][0:S, :].rearrange("p (h t) -> p h t", h=4)).then_inc(pt_v, 1)
                        if 1 <= n < NTB - 1:
                            inverse_sum(n + 1)
                        if n + 2 < NTB:
                            less_max(n + 2)
                    ve.wait_ge(wo_mm, b + 1)
                    ve.scalar_tensor_tensor(m[5], bank[0][:, :], v("bo"), m[3], ALU.add, ALU.add).then_inc(wo_ok, 1)
                    factors(b, 2)
                    ve.scalar_tensor_tensor(m[3], m[0], v("ln_gamma"), bank[3][:, :], ALU.mult, ALU.mult)\
                        .then_inc(n_out, 1)
                    ve.wait_ge(n_out, b * NORMS + 3)
                    ve.scalar_tensor_tensor(m[4], m[3], v("ln_beta"), m[4], ALU.add, ALU.add).then_inc(x2_ok, 1)
                    front_act(b + 1)
                    factors(b, 3)
                    ve.tensor_tensor(m[3], m[0], bank[3][:, :], ALU.mult).then_inc(n_out, 1)
                    front_gated(b + 1)
                    ve.wait_ge(h1_mm, (b + 1) * F2)
                    front_y1(b + 1, bass.ds((b + 1) % B * T, T))
                    ve.wait_ge(h3_mm, b + 1)
                    ve.scalar_tensor_tensor(m[5], bank[4][:, :], v("s2"), m[4], ALU.mult, ALU.add).then_inc(y_ok, 1)


_OUT = "out_dram"


def pack_vectors(a, np):
    rows = {
        "conv_w": a["L0_attn_conv_w"], "conv_b": a["L0_attn_conv_b"][:, None],
        "w_norm": a["L0_attn_w_norm_in"][:, None], "b_ad": a["L0_attn_b_ad"].reshape(-1, P).T,
        "alpha_spike": a["L0_attn_alpha_spike"].reshape(-1, P).T,
        "beta_spike": a["L0_attn_beta_spike"].reshape(-1, P).T,
        "b_au": a["L0_attn_b_au"][:, None], "b_u1": a["L0_attn_b_u1"][:, None],
        "b_u2": a["L0_attn_b_u2"][:, None], "w_hn": a["L0_attn_w_hn"].T,
        "w_ffn": a["L0_attn_w_ffn"][:, None],
        "b_beta": np.repeat(a["L0_attn_b_beta"], 64).reshape(-1, P).T,
        "bq": a["L0_xattn_bq"].reshape(-1, P).T, "bk": a["L0_xattn_bk"].reshape(-1, P).T,
        "bv": a["L0_xattn_bv"].reshape(-1, P).T, "bo": a["L0_xattn_bo"][:, None],
        "ln_gamma": a["L0_xattn_ln_gamma"][:, None], "ln_beta": a["L0_xattn_ln_beta"][:, None],
        "s0": np.repeat(a["L0_ffn_s0"].reshape(1, 1), P, 0), "s1": np.repeat(a["L0_ffn_s1"].reshape(1, 1), P, 0),
        "s2": np.repeat(a["L0_ffn_s2"].reshape(1, 1), P, 0),
    }
    packed = np.zeros((P, NVEC), np.float32)
    for name, (at, n) in VEC.items():
        r = rows[name]
        packed[:r.shape[0], at:at + n] = r
    return packed


def kernel(**inputs):
    import numpy as np
    import concourse.bacc as bacc
    from concourse.bass_utils import run_bass_kernel_spmd

    a = {n: np.ascontiguousarray(t) for n, t in inputs.items()}
    arrays = {"x": a["x"], "ctx": a["ctx_1024"], "vec": pack_vectors(a, np)}
    for n in ("wq", "wk", "w_spike", "wv", "w_out", "w_au", "w_ad", "w_beta", "w_u1", "w_u2",
              "w_ff1", "w_ff3", "w_ff2"):
        arrays[n] = a["L0_attn_" + n]
    for n in ("Wq", "Wk", "Wv", "Wo"):
        arrays["x_" + n] = a["L0_xattn_" + n]
    for n in ("k0", "k1", "k2"):
        arrays[n] = a["L0_ffn_" + n]
    nc = bacc.Bacc("TRN2", target_bir_lowering=False, num_devices=1)
    arrays = {f"in_{n}_dram": t for n, t in arrays.items()}
    args = [nc.dram_tensor(n, t.shape, mybir.dt.from_np(t.dtype), kind="ExternalInput").ap()
            for n, t in arrays.items()]
    args.append(nc.dram_tensor(_OUT, a["x"].shape, F32, kind="ExternalOutput").ap())
    decoder_kernel(nc, *args)
    return run_bass_kernel_spmd(nc, [arrays], core_ids=[0]).results[0][_OUT]
```
